# Optimizing a Trainium2 kernel written in Bass

```python
import numpy as np
import jax
import jax.numpy as jnp

def _softmax(x, axis=-1):
    return jax.nn.softmax(x, axis=axis)

def _gelu(x):
    return jax.nn.gelu(x, approximate=True)

def _silu(x):
    return jax.nn.silu(x)

def _sigmoid(x):
    return jax.nn.sigmoid(x)

def _layernorm(x, axis=-1, eps=1e-05):
    m = jnp.mean(x, axis=axis, keepdims=True)
    v = jnp.var(x, axis=axis, keepdims=True)
    return (x - m) / jnp.sqrt(v + eps)

def _scatter_add(tgt, idx, src, axis=0):
    return tgt.at[idx].add(src)

def _segment_sum(src, seg, n):
    return jax.ops.segment_sum(src, seg, n)
kernel_name = 'mk_prb_d2_jaxref_r8_e28b7a'

def setup_inputs(seed: int=0):
    np.random.seed(seed)
    _w = jnp.asarray

    def _L0_attn_setup():
        import jax, jax.numpy as jnp
        import numpy as np
        MAX_LR = 0.01
        NS_A, NS_B, NS_C = (3.4445, -4.775, 2.0315)

        def newtonschulz5(G, steps=5, eps=1e-07):
            transpose = G.shape[-2] > G.shape[-1]
            X = jnp.swapaxes(G, -2, -1) if transpose else G
            X = X / (jnp.linalg.norm(X, axis=(-2, -1), keepdims=True) + eps)
            for _ in range(steps):
                A = X @ jnp.swapaxes(X, -2, -1)
                Bm = NS_B * A + NS_C * (A @ A)
                X = NS_A * X + Bm @ X
            return jnp.swapaxes(X, -2, -1) if transpose else X

        def _reference_tuple_inner(tokens, wq, wk, wv, wo, w_lr, w_target, w_gates, rms_w):
            N = tokens.shape[1]
            scale = wq.shape[-1] ** (-0.5)
            eps = jnp.finfo(tokens.dtype).eps
            t = tokens * jax.lax.rsqrt(jnp.mean(tokens * tokens, -1, keepdims=True) + eps) * rms_w
            gates = jnp.swapaxes(jax.nn.sigmoid(t @ w_gates), -2, -1)[..., None]
            q = jnp.einsum('bnd,hde->bhne', t, wq)
            k = jnp.einsum('bnd,hde->bhne', t, wk)
            v = jnp.einsum('bnd,hde->bhne', t, wv)
            score = jnp.einsum('bhie,bhje->bhij', q, k) * scale
            causal_mask = jnp.triu(jnp.ones((N, N), bool), 1)
            score = jnp.where(causal_mask, -jnp.finfo(score.dtype).max, score)
            attn = jax.nn.softmax(score, axis=-1)
            out = jnp.einsum('bhij,bhje->bhie', attn, v) * gates
            pred_values = jnp.einsum('bhne,hed->bnd', out, wo)
            tv = t[:, 1:] @ w_target
            tv = (tv - tv.mean(-1, keepdims=True)) * jax.lax.rsqrt(tv.var(-1, keepdims=True) + 1e-05)
            ts = t[:, :-1]
            pv = pred_values[:, :-1]
            o = out[:, :, :-1]
            g = gates[:, :, :-1]
            a = attn[:, :, :-1, :-1]
            qs, ks_, vs = (q[:, :, :-1], k[:, :, :-1], v[:, :, :-1])
            lrs = jax.nn.sigmoid(ts @ w_lr) * MAX_LR
            lr, mlr = (lrs[..., 0], lrs[..., 1])
            error = tv - pv
            dout = jnp.einsum('bnd,hed->bhne', error, wo)
            du = dout * g
            delta = jnp.sum(dout * o, -1, keepdims=True)
            dv = jnp.einsum('bhij,bhie->bhje', a, du)
            dattn = jnp.einsum('bhje,bhie->bhij', vs, du)
            dscore = scale * a * (dattn - delta)
            dq = jnp.einsum('bhje,bhij->bhie', ks_, dscore)
            dk = jnp.einsum('bhie,bhij->bhje', qs, dscore)
            t_qk = ts * lr[..., None]
            t_v = ts * mlr[..., None]
            o_wo = o * mlr[:, None, :, None]
            dwq = jnp.einsum('bhie,bid->bhde', dq, t_qk)
            dwk = jnp.einsum('bhje,bjd->bhde', dk, t_qk)
            dwv = jnp.einsum('bhje,bjd->bhde', dv, t_v)
            dwo = jnp.einsum('bnd,bhne->bhed', error, o_wo)
            dwv = newtonschulz5(dwv)
            dwo = newtonschulz5(dwo)
            return (pred_values, dwq, dwk, dwv, dwo)
        key = jax.random.key(seed)
        ks = jax.random.split(key, 9)
        B, N, D, H, DH = (4, 128, 128, 8, 64)
        s = D ** (-0.5)
        return {'tokens': jax.random.normal(ks[0], (B, N, D), jnp.float32), 'wq': jax.random.normal(ks[1], (H, D, DH), jnp.float32) * s, 'wk': jax.random.normal(ks[2], (H, D, DH), jnp.float32) * s, 'wv': jax.random.normal(ks[3], (H, D, DH), jnp.float32) * s, 'wo': jax.random.normal(ks[4], (H, DH, D), jnp.float32) * s, 'w_lr': jax.random.normal(ks[5], (D, 2), jnp.float32) * 0.02, 'w_target': jax.random.normal(ks[6], (D, D), jnp.float32) * 0.02, 'w_gates': jax.random.normal(ks[7], (D, H), jnp.float32) * 0.02, 'rms_w': jnp.ones((D,), jnp.float32)}
    _L0_attn_in = _L0_attn_setup()

    def _L0_ffn_setup():
        import jax, jax.numpy as jnp
        import numpy as np
        DIM = 128

        def _reference_tuple_inner(x, W_r, W_k, W_v, mu_r, mu_k):
            B, T, C = x.shape
            x_prev = jnp.concatenate([jnp.zeros((B, 1, C), x.dtype), x[:, :-1, :]], axis=1)
            xr = mu_r * x + (1.0 - mu_r) * x_prev
            xk = mu_k * x + (1.0 - mu_k) * x_prev
            r = jax.nn.sigmoid(jnp.einsum('btc,dc->btd', xr, W_r))
            k = jnp.einsum('btc,dc->btd', xk, W_k)
            k_act = jnp.square(jax.nn.relu(k))
            out = r * jnp.einsum('btc,dc->btd', k_act, W_v)
            new_state = x[:, -1, :]
            return (out, new_state)
        key = jax.random.key(seed)
        ks = jax.random.split(key, 6)
        B, T, C = (8, 256, DIM)
        x = jax.random.normal(ks[0], (B, T, C), dtype=jnp.float32)
        s = 1.0 / np.sqrt(C)
        W_r = jax.random.uniform(ks[1], (C, C), jnp.float32, -s, s)
        W_k = jax.random.uniform(ks[2], (C, C), jnp.float32, -s, s)
        W_v = jax.random.uniform(ks[3], (C, C), jnp.float32, -s, s)
        mu_r = jax.random.uniform(ks[4], (C,), jnp.float32)
        mu_k = jax.random.uniform(ks[5], (C,), jnp.float32)
        return {'x': x, 'W_r': W_r, 'W_k': W_k, 'W_v': W_v, 'mu_r': mu_r, 'mu_k': mu_k}
    _L0_ffn_in = _L0_ffn_setup()

    def _L1_attn_setup():
        import jax, jax.numpy as jnp
        import numpy as np
        D = 128
        H = 4
        HD = D // H
        K = 4
        EPS = 1e-06

        def _dwconv_silu(x, w):
            xc = jnp.transpose(x, (0, 2, 1))
            xp = jnp.pad(xc, ((0, 0), (0, 0), (K - 1, 0)))
            y = jax.lax.conv_general_dilated(xp, w, window_strides=(1,), padding='VALID', dimension_numbers=('NCH', 'OIH', 'NCH'), feature_group_count=D)
            return jax.nn.silu(jnp.transpose(y, (0, 2, 1)))

        def _l2norm(x):
            n = jnp.sqrt(jnp.sum(x * x, axis=-1, keepdims=True))
            return x / jnp.maximum(n, EPS)

        def _rmsnorm(x):
            ms = jnp.mean(x * x, axis=-1, keepdims=True)
            return x * jax.lax.rsqrt(ms + EPS)

        def _forward(x, W_in, W_ctrl, b_ctrl, w_q, w_k, w_v, W_out, b_out, ramp_logit):
            B, S, _ = x.shape
            qkv = jnp.einsum('bsd,de->bse', x, W_in)
            q_in, k_in, v_in = jnp.split(qkv, [D, 2 * D], axis=-1)
            ctrl = jnp.einsum('bsd,de->bse', x, W_ctrl) + b_ctrl
            alpha_in = ctrl[..., :H]
            beta_in = ctrl[..., H:2 * H]
            og_in = ctrl[..., 2 * H:]
            q = _l2norm(_dwconv_silu(q_in, w_q).reshape(B, S, H, HD))
            k = _l2norm(_dwconv_silu(k_in, w_k).reshape(B, S, H, HD))
            v = _dwconv_silu(v_in, w_v).reshape(B, S, H, HD)
            alpha = jax.nn.sigmoid(alpha_in) * 0.98 + 0.01
            beta = jax.nn.sigmoid(beta_in)
            og = jax.nn.sigmoid(og_in)
            ramp = jax.nn.sigmoid(ramp_logit)

            def step(state, inp):
                qt, kt, vt, at, bt, ot = inp
                old = jnp.einsum('bhvk,bhk->bhv', state, kt)
                erase = jnp.einsum('bhv,bhk->bhvk', old, kt)
                write = jnp.einsum('bhv,bhk->bhvk', vt, kt)
                a4 = at[:, :, None, None]
                b4 = bt[:, :, None, None]
                state = a4 * (state - b4 * erase) + b4 * write
                read = jnp.einsum('bhvk,bhk->bhv', state, qt)
                read = _rmsnorm(read).reshape(B, D)
                out = ot * (read @ W_out + b_out) * ramp
                return (state, out)
            state0 = jnp.zeros((B, H, HD, HD), x.dtype)
            xs = (jnp.swapaxes(q, 0, 1), jnp.swapaxes(k, 0, 1), jnp.swapaxes(v, 0, 1), jnp.swapaxes(alpha, 0, 1), jnp.swapaxes(beta, 0, 1), jnp.swapaxes(og, 0, 1))
            final_state, outs = jax.lax.scan(step, state0, xs)
            return (jnp.swapaxes(outs, 0, 1), final_state)

        def _reference_tuple_inner(x, W_in, W_ctrl, b_ctrl, w_q, w_k, w_v, W_out, b_out, ramp_logit):
            return _forward(x, W_in, W_ctrl, b_ctrl, w_q, w_k, w_v, W_out, b_out, ramp_logit)
        key = jax.random.key(seed)
        ks = jax.random.split(key, 6)
        x = jax.random.normal(ks[0], (4, 256, D), dtype=jnp.float32)
        W_in = jax.random.normal(ks[1], (D, 3 * D), dtype=jnp.float32) * 0.02
        W_ctrl = jax.random.normal(ks[2], (D, 2 * H + D), dtype=jnp.float32) * 0.02
        b_ctrl = jnp.concatenate([jnp.full((H,), 1.5, jnp.float32), jnp.full((H,), -2.0, jnp.float32), jnp.full((D,), -1.5, jnp.float32)])
        wconv = np.zeros((D, 1, K), dtype=np.float32)
        wconv[:, 0, -1] = 1.0
        w_q = jnp.asarray(wconv)
        w_k = jnp.asarray(wconv)
        w_v = jnp.asarray(wconv)
        lim = 0.1 * np.sqrt(6.0 / (D + D))
        W_out = jax.random.uniform(ks[3], (D, D), jnp.float32, -lim, lim)
        b_out = jnp.zeros((D,), jnp.float32)
        ramp_logit = jnp.full((D,), -2.1972246, jnp.float32)
        return {'x': x, 'W_in': W_in, 'W_ctrl': W_ctrl, 'b_ctrl': b_ctrl, 'w_q': w_q, 'w_k': w_k, 'w_v': w_v, 'W_out': W_out, 'b_out': b_out, 'ramp_logit': ramp_logit}
    _L1_attn_in = _L1_attn_setup()

    def _L1_ffn_setup():
        import jax, jax.numpy as jnp
        import numpy as np

        def _binarize(w):
            alpha = jax.lax.stop_gradient(jnp.mean(jnp.abs(w), axis=1, keepdims=True))
            bw = alpha * jnp.sign(w)
            return w + jax.lax.stop_gradient(bw - w)
        key = jax.random.key(seed)
        k1, k2, k3, k4, k5 = jax.random.split(key, 5)
        D, H = (128, 512)
        x = jax.random.normal(k1, (64, 196, D), dtype=jnp.float32)
        w1 = jax.random.normal(k2, (H, D), dtype=jnp.float32) * 0.02
        b1 = jax.random.normal(k3, (H,), dtype=jnp.float32) * 0.02
        w2 = jax.random.normal(k4, (D, H), dtype=jnp.float32) * 0.02
        b2 = jax.random.normal(k5, (D,), dtype=jnp.float32) * 0.02
        return {'x': x, 'w1': w1, 'b1': b1, 'w2': w2, 'b2': b2}
    _L1_ffn_in = _L1_ffn_setup()
    _d = {'L0_attn_tokens': _L0_attn_in['tokens'], 'L0_attn_wq': _L0_attn_in['wq'], 'L0_attn_wk': _L0_attn_in['wk'], 'L0_attn_wv': _L0_attn_in['wv'], 'L0_attn_wo': _L0_attn_in['wo'], 'L0_attn_w_lr': _L0_attn_in['w_lr'], 'L0_attn_w_target': _L0_attn_in['w_target'], 'L0_attn_w_gates': _L0_attn_in['w_gates'], 'L0_attn_rms_w': _L0_attn_in['rms_w'], 'L0_ffn_W_r': _L0_ffn_in['W_r'], 'L0_ffn_W_k': _L0_ffn_in['W_k'], 'L0_ffn_W_v': _L0_ffn_in['W_v'], 'L0_ffn_mu_r': _L0_ffn_in['mu_r'], 'L0_ffn_mu_k': _L0_ffn_in['mu_k'], 'L1_attn_W_in': _L1_attn_in['W_in'], 'L1_attn_W_ctrl': _L1_attn_in['W_ctrl'], 'L1_attn_b_ctrl': _L1_attn_in['b_ctrl'], 'L1_attn_w_q': _L1_attn_in['w_q'], 'L1_attn_w_k': _L1_attn_in['w_k'], 'L1_attn_w_v': _L1_attn_in['w_v'], 'L1_attn_W_out': _L1_attn_in['W_out'], 'L1_attn_b_out': _L1_attn_in['b_out'], 'L1_attn_ramp_logit': _L1_attn_in['ramp_logit'], 'L1_ffn_w1': _L1_ffn_in['w1'], 'L1_ffn_b1': _L1_ffn_in['b1'], 'L1_ffn_w2': _L1_ffn_in['w2'], 'L1_ffn_b2': _L1_ffn_in['b2']}
    _x0 = _d['L0_attn_tokens']
    _d['L0_attn_tokens'] = jax.random.normal(jax.random.fold_in(jax.random.key(seed), 1), (4, 1024, 128), dtype=_x0.dtype)
    del _x0
    return _d

def reference(L0_attn_tokens, L0_attn_wq, L0_attn_wk, L0_attn_wv, L0_attn_wo, L0_attn_w_lr, L0_attn_w_target, L0_attn_w_gates, L0_attn_rms_w, L0_ffn_W_r, L0_ffn_W_k, L0_ffn_W_v, L0_ffn_mu_r, L0_ffn_mu_k, L1_attn_W_in, L1_attn_W_ctrl, L1_attn_b_ctrl, L1_attn_w_q, L1_attn_w_k, L1_attn_w_v, L1_attn_W_out, L1_attn_b_out, L1_attn_ramp_logit, L1_ffn_w1, L1_ffn_b1, L1_ffn_w2, L1_ffn_b2):

    def _L0_attn_ref(tokens, wq, wk, wv, wo, w_lr, w_target, w_gates, rms_w):
        import jax, jax.numpy as jnp
        import numpy as np
        MAX_LR = 0.01
        NS_A, NS_B, NS_C = (3.4445, -4.775, 2.0315)

        def newtonschulz5(G, steps=5, eps=1e-07):
            transpose = G.shape[-2] > G.shape[-1]
            X = jnp.swapaxes(G, -2, -1) if transpose else G
            X = X / (jnp.linalg.norm(X, axis=(-2, -1), keepdims=True) + eps)
            for _ in range(steps):
                A = X @ jnp.swapaxes(X, -2, -1)
                Bm = NS_B * A + NS_C * (A @ A)
                X = NS_A * X + Bm @ X
            return jnp.swapaxes(X, -2, -1) if transpose else X

        def _reference_tuple_inner(tokens, wq, wk, wv, wo, w_lr, w_target, w_gates, rms_w):
            N = tokens.shape[1]
            scale = wq.shape[-1] ** (-0.5)
            eps = jnp.finfo(tokens.dtype).eps
            t = tokens * jax.lax.rsqrt(jnp.mean(tokens * tokens, -1, keepdims=True) + eps) * rms_w
            gates = jnp.swapaxes(jax.nn.sigmoid(t @ w_gates), -2, -1)[..., None]
            q = jnp.einsum('bnd,hde->bhne', t, wq)
            k = jnp.einsum('bnd,hde->bhne', t, wk)
            v = jnp.einsum('bnd,hde->bhne', t, wv)
            score = jnp.einsum('bhie,bhje->bhij', q, k) * scale
            causal_mask = jnp.triu(jnp.ones((N, N), bool), 1)
            score = jnp.where(causal_mask, -jnp.finfo(score.dtype).max, score)
            attn = jax.nn.softmax(score, axis=-1)
            out = jnp.einsum('bhij,bhje->bhie', attn, v) * gates
            pred_values = jnp.einsum('bhne,hed->bnd', out, wo)
            tv = t[:, 1:] @ w_target
            tv = (tv - tv.mean(-1, keepdims=True)) * jax.lax.rsqrt(tv.var(-1, keepdims=True) + 1e-05)
            ts = t[:, :-1]
            pv = pred_values[:, :-1]
            o = out[:, :, :-1]
            g = gates[:, :, :-1]
            a = attn[:, :, :-1, :-1]
            qs, ks_, vs = (q[:, :, :-1], k[:, :, :-1], v[:, :, :-1])
            lrs = jax.nn.sigmoid(ts @ w_lr) * MAX_LR
            lr, mlr = (lrs[..., 0], lrs[..., 1])
            error = tv - pv
            dout = jnp.einsum('bnd,hed->bhne', error, wo)
            du = dout * g
            delta = jnp.sum(dout * o, -1, keepdims=True)
            dv = jnp.einsum('bhij,bhie->bhje', a, du)
            dattn = jnp.einsum('bhje,bhie->bhij', vs, du)
            dscore = scale * a * (dattn - delta)
            dq = jnp.einsum('bhje,bhij->bhie', ks_, dscore)
            dk = jnp.einsum('bhie,bhij->bhje', qs, dscore)
            t_qk = ts * lr[..., None]
            t_v = ts * mlr[..., None]
            o_wo = o * mlr[:, None, :, None]
            dwq = jnp.einsum('bhie,bid->bhde', dq, t_qk)
            dwk = jnp.einsum('bhje,bjd->bhde', dk, t_qk)
            dwv = jnp.einsum('bhje,bjd->bhde', dv, t_v)
            dwo = jnp.einsum('bnd,bhne->bhed', error, o_wo)
            dwv = newtonschulz5(dwv)
            dwo = newtonschulz5(dwo)
            return (pred_values, dwq, dwk, dwv, dwo)
        return _reference_tuple_inner(tokens, wq, wk, wv, wo, w_lr, w_target, w_gates, rms_w)[0]

    def _L0_ffn_ref(x, W_r, W_k, W_v, mu_r, mu_k):
        import jax, jax.numpy as jnp
        import numpy as np
        DIM = 128

        def _reference_tuple_inner(x, W_r, W_k, W_v, mu_r, mu_k):
            B, T, C = x.shape
            x_prev = jnp.concatenate([jnp.zeros((B, 1, C), x.dtype), x[:, :-1, :]], axis=1)
            xr = mu_r * x + (1.0 - mu_r) * x_prev
            xk = mu_k * x + (1.0 - mu_k) * x_prev
            r = jax.nn.sigmoid(jnp.einsum('btc,dc->btd', xr, W_r))
            k = jnp.einsum('btc,dc->btd', xk, W_k)
            k_act = jnp.square(jax.nn.relu(k))
            out = r * jnp.einsum('btc,dc->btd', k_act, W_v)
            new_state = x[:, -1, :]
            return (out, new_state)
        return _reference_tuple_inner(x, W_r, W_k, W_v, mu_r, mu_k)[0]

    def _L1_attn_ref(x, W_in, W_ctrl, b_ctrl, w_q, w_k, w_v, W_out, b_out, ramp_logit):
        import jax, jax.numpy as jnp
        import numpy as np
        D = 128
        H = 4
        HD = D // H
        K = 4
        EPS = 1e-06

        def _dwconv_silu(x, w):
            xc = jnp.transpose(x, (0, 2, 1))
            xp = jnp.pad(xc, ((0, 0), (0, 0), (K - 1, 0)))
            y = jax.lax.conv_general_dilated(xp, w, window_strides=(1,), padding='VALID', dimension_numbers=('NCH', 'OIH', 'NCH'), feature_group_count=D)
            return jax.nn.silu(jnp.transpose(y, (0, 2, 1)))

        def _l2norm(x):
            n = jnp.sqrt(jnp.sum(x * x, axis=-1, keepdims=True))
            return x / jnp.maximum(n, EPS)

        def _rmsnorm(x):
            ms = jnp.mean(x * x, axis=-1, keepdims=True)
            return x * jax.lax.rsqrt(ms + EPS)

        def _forward(x, W_in, W_ctrl, b_ctrl, w_q, w_k, w_v, W_out, b_out, ramp_logit):
            B, S, _ = x.shape
            qkv = jnp.einsum('bsd,de->bse', x, W_in)
            q_in, k_in, v_in = jnp.split(qkv, [D, 2 * D], axis=-1)
            ctrl = jnp.einsum('bsd,de->bse', x, W_ctrl) + b_ctrl
            alpha_in = ctrl[..., :H]
            beta_in = ctrl[..., H:2 * H]
            og_in = ctrl[..., 2 * H:]
            q = _l2norm(_dwconv_silu(q_in, w_q).reshape(B, S, H, HD))
            k = _l2norm(_dwconv_silu(k_in, w_k).reshape(B, S, H, HD))
            v = _dwconv_silu(v_in, w_v).reshape(B, S, H, HD)
            alpha = jax.nn.sigmoid(alpha_in) * 0.98 + 0.01
            beta = jax.nn.sigmoid(beta_in)
            og = jax.nn.sigmoid(og_in)
            ramp = jax.nn.sigmoid(ramp_logit)

            def step(state, inp):
                qt, kt, vt, at, bt, ot = inp
                old = jnp.einsum('bhvk,bhk->bhv', state, kt)
                erase = jnp.einsum('bhv,bhk->bhvk', old, kt)
                write = jnp.einsum('bhv,bhk->bhvk', vt, kt)
                a4 = at[:, :, None, None]
                b4 = bt[:, :, None, None]
                state = a4 * (state - b4 * erase) + b4 * write
                read = jnp.einsum('bhvk,bhk->bhv', state, qt)
                read = _rmsnorm(read).reshape(B, D)
                out = ot * (read @ W_out + b_out) * ramp
                return (state, out)
            state0 = jnp.zeros((B, H, HD, HD), x.dtype)
            xs = (jnp.swapaxes(q, 0, 1), jnp.swapaxes(k, 0, 1), jnp.swapaxes(v, 0, 1), jnp.swapaxes(alpha, 0, 1), jnp.swapaxes(beta, 0, 1), jnp.swapaxes(og, 0, 1))
            final_state, outs = jax.lax.scan(step, state0, xs)
            return (jnp.swapaxes(outs, 0, 1), final_state)

        def _reference_tuple_inner(x, W_in, W_ctrl, b_ctrl, w_q, w_k, w_v, W_out, b_out, ramp_logit):
            return _forward(x, W_in, W_ctrl, b_ctrl, w_q, w_k, w_v, W_out, b_out, ramp_logit)
        return _reference_tuple_inner(x, W_in, W_ctrl, b_ctrl, w_q, w_k, w_v, W_out, b_out, ramp_logit)[0]

    def _L1_ffn_ref(x, w1, b1, w2, b2):
        import jax, jax.numpy as jnp
        import numpy as np

        def _binarize(w):
            alpha = jax.lax.stop_gradient(jnp.mean(jnp.abs(w), axis=1, keepdims=True))
            bw = alpha * jnp.sign(w)
            return w + jax.lax.stop_gradient(bw - w)
        bw1 = _binarize(w1)
        h = jnp.einsum('bsd,hd->bsh', x, bw1) + b1
        h = jax.nn.gelu(h, approximate=False)
        bw2 = _binarize(w2)
        out = jnp.einsum('bsh,dh->bsd', h, bw2) + b2
        return out
    x = L0_attn_tokens
    xn = _layernorm(x, axis=-1)
    x = x + _L0_attn_ref(xn, L0_attn_wq, L0_attn_wk, L0_attn_wv, L0_attn_wo, L0_attn_w_lr, L0_attn_w_target, L0_attn_w_gates, L0_attn_rms_w) + _L0_ffn_ref(xn, L0_ffn_W_r, L0_ffn_W_k, L0_ffn_W_v, L0_ffn_mu_r, L0_ffn_mu_k)
    xn = _layernorm(x, axis=-1)
    x = x + _L1_attn_ref(xn, L1_attn_W_in, L1_attn_W_ctrl, L1_attn_b_ctrl, L1_attn_w_q, L1_attn_w_k, L1_attn_w_v, L1_attn_W_out, L1_attn_b_out, L1_attn_ramp_logit) + _L1_ffn_ref(xn, L1_ffn_w1, L1_ffn_b1, L1_ffn_w2, L1_ffn_b2)
    return x

_drawn_inputs = setup_inputs


def setup_inputs(seed=0):
    import zlib

    import numpy as np

    out = dict(_drawn_inputs(seed))
    spreads = {'L0_attn_rms_w': (1.0, 0.2),
     'L1_attn_b_out': (0.0, 2.0),
     'L1_attn_ramp_logit': (-2.1972246170043945, 0.6)}
    factors = {'L0_attn_w_gates': 3.072,
     'L0_ffn_W_r': 3.198,
     'L0_ffn_mu_r': 6.291,
     'L1_attn_W_in': 64.0,
     'L1_attn_W_ctrl': 64.0,
     'L1_attn_b_ctrl': 64.0,
     'L1_attn_w_q': 64.0,
     'L1_attn_w_k': 64.0,
     'L1_attn_w_v': 64.0,
     'L1_attn_W_out': 64.0,
     'L1_ffn_b1': 8.0,
     'L1_ffn_b2': 2.828}
    for name, (base, spread) in spreads.items():
        noise = np.random.default_rng([zlib.crc32(name.encode()), seed]).standard_normal(out[name].shape)
        drawn = base * np.exp(spread * noise) if base else spread * noise
        out[name] = jnp.asarray(drawn.astype(out[name].dtype))
    for name, factor in factors.items():
        out[name] = (out[name] * factor).astype(out[name].dtype)
    return out
```

```python
from contextlib import ExitStack

import concourse.bass as bass
from concourse import mybir

ALU = mybir.AluOpType
ACT = mybir.ActivationFunctionType
AX = mybir.AxisListType
F32 = mybir.dt.float32
BF16 = mybir.dt.bfloat16
ds = bass.ds

P = 128
EPS_LN = 1e-5
EPS_RMS = 1.1920928955078125e-07
MASKED = -1e30
Z_MIN = -87.0


def build(nc, A, out):
    B, N, D = A["L0_attn_tokens"].shape
    H, _, E = A["L0_attn_wq"].shape
    NT = N // P
    TILES = B * NT
    QUADS = TILES // 4
    PAIRS = H // 2
    STEPS = B * PAIRS
    UNITS = 2 * NT
    SCALE = float(E) ** -0.5
    H1 = 4
    E1 = D // H1
    SUB = 32
    NB = P // SUB
    GH = B * H1
    CT = A["L1_attn_W_ctrl"].shape[1]
    FT = A["L1_ffn_w1"].shape[0] // P
    assert E1 == SUB == 32 and B == 4 and NB == 4

    x_dram = A["L0_attn_tokens"].rearrange("b (t p) d -> p (b t) d", p=P)
    out_dram = out.rearrange("b (t p) d -> p (b t) d", p=P)

    with ExitStack() as ctx:
        def sb(name, shape, dt=F32):
            return ctx.enter_context(nc.sbuf_tensor(name, shape, dt))

        sems = {}
        shared = {}
        for family, steps in {
            "conv": [f"conv{i}_{k}" for k in (2, 1, 0) for i in range(3)] + [f"conv{i}_done" for i in range(3)],
            "silu": [f"silu{i}_{k}" for k in ("a", "b", "ready") for i in range(3)],
            "join": ["T2_raw", "T0_ready", "Z0_ready", "Tx0_ready"]
            + [f"{x}{k}_ready" for k in (1, 2, 3) for x in ("Z", "T", "Tx")] + ["Z4_ready", "Tx4_ready"],
            "state": ["St0_ready", "St1_ready", "St2_ready", "St3_ready"],
            "norm": ["ss_raw", "ss_ready"],
            "control": ["ctl_raw", "ctl_ready", "sg1", "sg_ready", "al_ready"],
            "read": ["rd_ready", "rss_raw", "rss_ready", "rdn_ready"],
            "gated": ["ao1", "ao2"],
            "qkv_done": [f"qkv{i}_done" for i in range(3)],
            "ffn_done": [f"ffn{t}_done" for t in range(FT)],
            "tok_turned": [f"tok{i}_turned" for i in range(3)],
            "join_products": [f"{x}{k}_done" for k in range(4) for x in ("Y", "ZY")],
            "AS_done": [f"AS{q}_done" for q in range(NB)],
            "qkv_ready": [f"qkv{i}_ready" for i in range(3)],
            "ce_ready": [f"ce{i}_ready" for i in range(3)],
            "h_ready": [f"h{t}_ready" for t in range(FT)],
            "Bx_ready": [f"Bx{k}_ready" for k in range(4)],
            "Y_ready": [f"Y{k}_ready" for k in range(4)],
            "Bm_ready": [f"Bm{k}_ready" for k in range(4)],
        }.items():
            for i, step in enumerate(steps):
                shared[step] = (family, len(steps), i)

        def count(name, s):
            _, per, i = shared.get(name, (name, 1, 0))
            return s * per + (i + 1)

        def S(name):
            name = shared.get(name, (name,))[0]
            if name not in sems:
                sems[name] = ctx.enter_context(nc.semaphore(name))
            return sems[name]

        banks = [ctx.enter_context(nc.psum_tensor(f"bank{i}", [P, 512], F32)) for i in range(0)]
        ps_all = ctx.enter_context(nc.psum_tensor("ps_all", [P, 8, 512], F32))

        def bank(i, n=1):
            return ps_all[:, i, :] if n == 1 else ps_all[:, i:i + n, :].rearrange("p b n -> p (b n)")

        X = sb("X", [P, TILES, D])
        stats = sb("stats", [P, TILES, 6])
        mean = sb("mean", [P, TILES])
        var = sb("var", [P, TILES])
        ve = sb("ve", [P, TILES])
        rstd = sb("rstd", [P, TILES])
        rms2 = sb("rms2", [P, TILES])
        rrms = sb("rrms", [P, TILES])
        neg_half = sb("neg_half", [P, TILES])
        ident = sb("ident", [P, P])
        identb = sb("identb", [P, P], BF16)
        causal = sb("causal", [P, P], BF16)
        half_one = sb("half_one", [P, 1])
        w_in = sb("w_in", [P, 3 * D])
        w_ctrl = sb("w_ctrl", [P, CT])
        w_out = sb("w_out", [P, D])
        b_ctrl = sb("b_ctrl", [P, CT])
        b_out = sb("b_out", [P, D])
        ramp = sb("ramp", [P, D])
        b2row = sb("b2row", [P, D])
        b1col = sb("b1col", [P, FT])
        conv_w = sb("conv_w", [P, 3, 4])
        w1T = sb("w1T", [P, FT * P])
        w2T = sb("w2T", [P, FT, D])
        masks = sb("masks", [P, 2 * P + NB + 8 * SUB])
        upto = masks[:, 0:P]
        beyond = masks[:, P:2 * P]
        in_block = masks[:, 2 * P:2 * P + NB]
        compact = masks[:, 2 * P + NB:].rearrange("p (k j) -> p k j", j=SUB)
        eye, below, upto_c = compact[:, 0, :], compact[:, 1, :], compact[:, 2, :]
        merge = compact[:, 3:8, :]
        persistent = sb
        l0 = ExitStack()

        def sb(name, shape, dt=F32):
            return l0.enter_context(nc.sbuf_tensor(name, shape, dt))

        wv_sb = sb("wv_sb", [P, H, E])
        wg_sb = sb("wg_sb", [P, H])
        rms_w = sb("rms_w", [P, 1])
        wqk = sb("wqk", [P, 2, 2 * E])
        wo_sb = sb("wo_sb", [P, PAIRS, D])
        w3 = sb("w3", [P, 3, D])
        w3T = sb("w3T", [P, 3, D])
        mu = sb("mu", [P, 4])
        TT = sb("TT", [P, B * N])
        V = sb("V", [P, TILES, H * E])
        G = sb("G", [P, TILES, H])

        Pbuf = sb("Pbuf", [P, 4, N])
        PT = sb("PT", [P, 2, N])
        Qp = sb("Qp", [P, 2, N])
        K = sb("K", [P, N])
        Vp = sb("Vp", [P, NT, 2 * E])
        OT = sb("OT", [P, N])
        R = sb("R", [P, 2, 512])
        Sx = sb("Sx", [P, 4, 2, E])
        nb = sb("nb", [P, UNITS])
        rs = sb("rs", [P, UNITS])
        rinv = sb("rinv", [P, UNITS])
        gs = sb("gs", [P, 4, 2])

        xn = Pbuf[:, 0, 0:512].rearrange("p (t d) -> p t d", t=4)
        tn = Pbuf[:, 0, 512:1024].rearrange("p (t d) -> p t d", t=4)
        xT = sb("xT", [P, 2, 1 + 512])
        tS = Pbuf[:, 1, 0:512]
        xr = Pbuf[:, 1, 512:1024]
        xk = Pbuf[:, 2, 0:512]
        tmr = Pbuf[:, 2, 512:1024]
        tmk = Pbuf[:, 3, 0:512]
        kr = Pbuf[:, 3, 512:1024]
        ka = PT[:, 0, 0:512]
        er = PT[:, 0, 512:1024]
        rr = PT[:, 1, 0:512]
        fo = PT[:, 1, 512:1024]
        eg = sb("eg", [P, 32])
        rg = sb("rg", [P, 32])

        w12 = sb("w12", [P, 2, 512])
        w12s = sb("w12s", [P, 2, 512])
        alpha = sb("alpha", [P, FT + 1])
        l0.close()
        sb = persistent

        xn1 = sb("xn1", [P, B, D])
        x1T = sb("x1T", [P, 512])
        qkv_in = sb("qkv_in", [P, 3, B, 3 + P])
        cy = sb("cy", [P, 3, B, P])
        ce = sb("ce", [P, 3, B, P])
        tok = sb("tok", [P, 3, B, D])
        sq = sb("sq", [P, 2, B, D])
        ss = sb("ss", [P, 2, GH])
        rn = sb("rn", [P, 2, GH])
        half16 = sb("half16", [P, 2, GH])
        qk_n = sb("qk_n", [P, 2, B, D])
        kqT = sb("kqT", [P, B, 2, P])
        ctl = sb("ctl", [P, B, CT])
        sg = sb("sg", [P, B, CT])
        al = sb("al", [P, B, H1])
        la = sb("la", [P, B, H1])
        ogr = sb("ogr", [P, B, D])
        laG = sb("laG", [P, GH, SUB])
        laX = sb("laX", [P, B, D])
        ones = sb("ones", [P, SUB])
        gam = sb("gam", [P, GH, SUB])
        gam_b = sb("gam_b", [P, GH, SUB])
        gam_t = sb("gam_t", [P, GH, SUB])
        gam_m = sb("gam_m", [P, GH, SUB])
        dec = sb("dec", [P, 48])
        bD = sb("bD", [P, GH])
        Lc = sb("Lc", [P, GH, SUB])
        Pc = sb("Pc", [P, GH, SUB])
        Bm = sb("Bm", [P, 4, GH, SUB])
        Bx = sb("Bx", [P, 2, GH, P])
        Tx = sb("Tx", [P, GH, P])
        Tc = sb("Tc", [P, GH, SUB])
        Zc = sb("Zc", [P, 2, GH, SUB])
        Yc = sb("Yc", [P, GH, SUB])
        Rv = sb("Rv", [P, GH, 2 * SUB])
        Wv = sb("Wv", [P, GH, 2 * SUB])
        Px = sb("Px", [P, GH, P])
        Qd = sb("Qd", [P, GH, SUB])
        Kd = sb("Kd", [P, GH, SUB])
        Mo = sb("Mo", [P, GH, SUB])
        MoT = sb("MoT", [P, B, P])
        Ov = sb("Ov", [P, GH, SUB])
        Ac = sb("Ac", [P, NB, B, SUB])
        At = sb("At", [P, NB, B, SUB])
        Ax = sb("Ax", [P, NB, B, P])
        Bc = sb("Bc", [P, NB, B, SUB])
        St = sb("St", [P, NB + 1, B, SUB])
        rd = sb("rd", [P, GH, SUB])
        rsq = sb("rsq", [P, GH, SUB])
        rss = sb("rss", [P, GH])
        rrs = sb("rrs", [P, GH])
        rdn = sb("rdn", [P, B, D])
        rdT = sb("rdT", [P, B, P])
        hT = sb("hT", [P, FT, 512])
        acc = sb("acc", [P, B, D])
        ao = sb("ao", [P, B, D])
        res = sb("res", [P, B, D])

        block = ctx.enter_context(nc.Block())

        @block.sync
        def _(sp):
            for b in range(B):
                sp.dma_start(X[:, b * NT:(b + 1) * NT, :], x_dram[:, b * NT:(b + 1) * NT, :]).then_inc(S("x_loaded"), 16)
            for i, name in enumerate(("W_r", "W_k", "W_v")):
                sp.dma_start(w3[:, i, :], A["L0_ffn_" + name]).then_inc(S("w3_loaded"), 16)
            sp.dma_start(mu[:, 0:1], A["L0_ffn_mu_r"].rearrange("(d a) -> d a", a=1)).then_inc(S("mu_loaded"), 16)
            sp.dma_start(mu[:, 2:3], A["L0_ffn_mu_k"].rearrange("(d a) -> d a", a=1)).then_inc(S("mu_loaded"), 16)
            sp.dma_start(rms_w[:, :], A["L0_attn_rms_w"].rearrange("(d a) -> d a", a=1)).then_inc(S("rms_loaded"), 16)
            sp.dma_start(wv_sb[:, :, :], A["L0_attn_wv"].rearrange("h d e -> d h e")).then_inc(S("wv_loaded"), 16)
            sp.dma_start(wg_sb[:, :], A["L0_attn_w_gates"]).then_inc(S("wv_loaded"), 16)
            sp.dma_start(wo_sb[:, :, :], A["L0_attn_wo"].rearrange("(a h) e d -> (h e) a d", h=2)).then_inc(S("wo_loaded"), 16)

            for name, dst in (("W_in", w_in), ("W_ctrl", w_ctrl), ("W_out", w_out)):
                sp.dma_start(dst[:, :], A["L1_attn_" + name]).then_inc(S("l1_loaded"), 16)
            for name, dst in (("L1_attn_b_ctrl", b_ctrl), ("L1_attn_b_out", b_out), ("L1_attn_ramp_logit", ramp),
                              ("L1_ffn_b2", b2row)):
                sp.dma_start(dst[:, :], A[name].partition_broadcast(P)).then_inc(S("l1_loaded"), 16)
            sp.dma_start(masks[:, :], A["masks"]).then_inc(S("l1_loaded"), 16)
            for t in range(FT):
                sp.dma_start(b1col[:, t:t + 1], A["L1_ffn_b1"][t * P:(t + 1) * P].rearrange("(p a) -> p a", a=1)).then_inc(S("l1_loaded"), 16)
            for i, name in enumerate(("w_q", "w_k", "w_v")):
                sp.dma_start(conv_w[:, i, :], A["L1_attn_" + name].rearrange("d a k -> d (a k)")).then_inc(S("l1_loaded"), 16)
            sp.dma_start(w12[:, 0, :].rearrange("p (t d) -> p t d", t=FT),
                         A["L1_ffn_w1"].rearrange("(t p) d -> p t d", p=P)).then_inc(S("w12_loaded"), 16)
            sp.dma_start(w12[:, 1, :], A["L1_ffn_w2"]).then_inc(S("w12_loaded"), 16)

            def load_qk(p):
                sp.dma_start(wqk[:, 0, :].rearrange("d (h e) -> d h e", h=2),
                             A["L0_attn_wq"][ds(p * 2, 2)].rearrange("h d e -> d h e")).then_inc(S("wqk_loaded"), 16)
                sp.dma_start(wqk[:, 1, :].rearrange("d (h e) -> d h e", h=2),
                             A["L0_attn_wk"][ds(p * 2, 2)].rearrange("h d e -> d h e")).then_inc(S("wqk_loaded"), 16)

            load_qk(0)
            with sp.Fori(0, STEPS) as n:
                nxt = sp.snap(((n + 1) % PAIRS))
                sp.wait_ge(S("proj_done"), n + 1)
                load_qk(nxt)
            sp.wait_ge(S("wqk_loaded"), 32 * (STEPS + 1))
            with sp.Fori(0, NT) as s:
                sp.wait_ge(S("res_ready"), s + 1)
                sp.dma_start(out_dram.rearrange("p (g t) d -> p g t d", g=B)[:, :, ds(s, 1), :].rearrange("p g a d -> p g (a d)"),
                             res[:, :, :]).then_inc(S("stored"), 16)
            sp.wait_ge(S("stored"), 16 * (NT + 1))

        @block.gpsimd
        def _(g):
            g.memset(neg_half[:, :], -0.5).then_inc(S("half_set"), 1)
            g.memset(ident[:, :], 0.0).then_inc(S("ident_zero"), 1)
            g.memset(causal[:, :], 0.0).then_inc(S("ident_zero"), 1)
            g.memset(Qp[:, :, :], 0.0).then_inc(S("q_zero"), 1)
            g.memset(xT[:, 0, 0:1], 0.0).then_inc(S("halo_zero"), 1)
            g.wait_ge(S("ident_zero"), 2)
            g.affine_select(out=ident[:, :], in_=ident[:, :], compare_op=ALU.not_equal, fill=1.0,
                            base=0, pattern=[[-1, P]], channel_multiplier=1).then_inc(S("ident_set"), 1)
            g.affine_select(out=causal[:, :], in_=causal[:, :], compare_op=ALU.is_ge, fill=MASKED,
                            base=0, pattern=[[-1, P]], channel_multiplier=1).then_inc(S("causal_set"), 1)
            g.wait_ge(S("ident_set"), 1)
            g.tensor_copy(identb[:, :], ident[:, :]).then_inc(S("causal_set"), 1)
            g.wait_ge(S("mu_loaded"), 32)
            for c in (0, 2):
                g.tensor_scalar(mu[:, c + 1:c + 2], mu[:, c:c + 1], -1.0, 1.0, ALU.mult, ALU.add).then_inc(S("mu_set"), 1)
            g.wait_ge(S("mu_set"), 2)
            g.wait_ge(S("half_set"), 1)
            g.wait_ge(S("stats_done"), 1)
            g.tensor_scalar(ve[:, :], var[:, :], EPS_LN, None, ALU.add).then_inc(S("rstd_step"), 1)
            g.wait_ge(S("rstd_step"), 1)
            g.tensor_tensor(rstd[:, :], ve[:, :], neg_half[:, :], ALU.pow).then_inc(S("rstd_step"), 1)
            g.wait_ge(S("rstd_step"), 2)
            g.tensor_tensor(rms2[:, :], rstd[:, :], rstd[:, :], ALU.mult).then_inc(S("rstd_step"), 1)
            g.wait_ge(S("rstd_step"), 3)
            g.tensor_tensor(ve[:, :], rms2[:, :], var[:, :], ALU.mult).then_inc(S("rstd_step"), 1)
            g.wait_ge(S("rstd_step"), 4)
            g.tensor_scalar(rms2[:, :], ve[:, :], EPS_RMS, None, ALU.add).then_inc(S("rstd_step"), 1)
            g.wait_ge(S("rstd_step"), 5)
            g.tensor_tensor(rrms[:, :], rms2[:, :], neg_half[:, :], ALU.pow).then_inc(S("rstd_step"), 1)
            with g.Fori(0, B) as b:
                for qd in range(2):
                    w = b * 2 + (qd + 1)
                    g.wait_ge(S("xT_ready"), w)
                    g.tensor_tensor(tmr, xT[:, qd, 0:512], mu[:, 1:2].to_broadcast([P, 512]), ALU.mult)
                    g.tensor_tensor(tmk, xT[:, qd, 0:512], mu[:, 3:4].to_broadcast([P, 512]), ALU.mult).then_inc(S("shift_ready"), 1)
                    g.wait_ge(S("tS_ready"), w)
                    g.tensor_copy(TT[:, ds(b * N + qd * 512, 512)], tS).then_inc(S("TT_ready"), 1)
                    g.wait_ge(S("kr_ready"), w)
                    g.tensor_tensor(ka, kr, kr, ALU.mult).then_inc(S("ka_ready"), 1)

            g.wait_ge(S("sign_ready"), 3)
            g.wait_ge(S("alpha_ready"), 2)
            for t in range(FT):
                g.tensor_tensor(w12s[:, 0, t * D:(t + 1) * D], w12s[:, 0, t * D:(t + 1) * D],
                                alpha[:, t:t + 1].to_broadcast([P, D]), ALU.mult)
            g.tensor_tensor(w12s[:, 1, :], w12s[:, 1, :], alpha[:, FT:FT + 1].to_broadcast([P, FT * P]),
                            ALU.mult).then_inc(S("bin_step"), 1)
            g.wait_ge(S("bin_step"), 1)
            g.tensor_tensor(w12s[:, :, :], w12s[:, :, :], w12[:, :, :], ALU.subtract).then_inc(S("bin_step"), 1)
            g.wait_ge(S("bin_step"), 2)
            g.tensor_tensor(w12[:, :, :], w12[:, :, :], w12s[:, :, :], ALU.add).then_inc(S("bin_ready"), 1)

            g.wait_ge(S("x1_done"), 1 + STEPS)
            g.wait_ge(S("bin_turned"), 2)
            g.wait_ge(S("ramp_ready"), 1)
            g.memset(half16[:, :, :], -0.5)
            g.memset(ones[:, :], 1.0)
            g.memset(qkv_in[:, :, :, :], 0.0)
            g.memset(Bx[:, :, :, :], 0.0)
            g.memset(Tx[:, :, :], 0.0)
            g.memset(Px[:, :, :], 0.0)
            g.memset(Ax[:, :, :, :], 0.0)
            g.memset(St[:, :, :, :], 0.0)
            g.memset(res[:, :, :], 0.0).then_inc(S("stored"), 16)
            g.memset(Pc[:, :, :], 0.0).then_inc(S("l1_zero"), 1)
            g.wait_ge(S("l1_zero"), 1)
            g.wait_ge(S("stats_done"), 2)
            g.tensor_scalar(ve[:, :], var[:, :], EPS_LN, None, ALU.add).then_inc(S("rstd_step"), 1)
            g.wait_ge(S("rstd_step"), 7)
            g.tensor_tensor(rstd[:, :], ve[:, :], neg_half[:, :], ALU.pow).then_inc(S("rstd_step"), 1)
            with g.Fori(0, NT) as s:

                def tt(out, a, b, op, done=None):
                    ins = g.tensor_tensor(out, a, b, op)
                    if done:
                        ins.then_inc(S(done), 1)

                def over(ap, shape, at):
                    return ap.unsqueeze(at).to_broadcast(shape)

                G3 = [P, GH, SUB]
                G4 = [P, B, H1, SUB]
                g.wait_ge(S("la_ready"), count("la_ready", s))
                tt(laG[:, :, :], over(la[:, :, :].rearrange("p g h -> p (g h)"), G3, 2), over(below, G3, 1), ALU.mult, "laG_ready")
                tt(laX[:, :, :].rearrange("p g (h e) -> p g h e", h=H1), over(la[:, :, :], G4, 3),
                   ones[:, :].unsqueeze(1).unsqueeze(1).to_broadcast(G4), ALU.mult, "laX_ready")
                g.wait_ge(S("tok_ready"), count("tok_ready", s))
                tt(sq[:, 0, :, :], tok[:, 0, :, :], tok[:, 0, :, :], ALU.mult)
                tt(sq[:, 1, :, :], tok[:, 1, :, :], tok[:, 1, :, :], ALU.mult, "sq_ready")
                tt(ogr[:, :, :], sg[:, :, 2 * H1:], over(ramp[:, :], [P, B, D], 1), ALU.mult, "ogr_ready")
                g.wait_ge(S("ss_ready"), count("ss_ready", s))
                g.tensor_tensor(rn[:, :, :], ss[:, :, :], half16[:, :, :], ALU.pow).then_inc(S("rn_ready"), 1)
                bt = sg[:, :, H1:2 * H1]
                tt(gam_b[:, :, :].rearrange("p (g h) j -> p g h j", g=B), over(bt, G4, 3),
                   below.unsqueeze(1).unsqueeze(1).to_broadcast(G4), ALU.mult, "bm_ready")
                g.wait_ge(S("gam_ready"), count("gam_ready", s))
                g.wait_ge(S("bm_ready"), count("bm_ready", s))
                tt(gam_b[:, :, :], gam_b[:, :, :], gam[:, :, :], ALU.mult, "gam_b_ready")
                tt(gam_m[:, :, :], gam[:, :, :], over(upto_c, G3, 1), ALU.mult, "gam_m_ready")
                g.wait_ge(S("dec_ready"), count("dec_ready", s))
                tt(bD[:, :].rearrange("p (g h) -> p g h", g=B), bt, dec[:, 0:16].rearrange("p (g h) -> p g h", g=B), ALU.mult, "bD_ready")
                R4 = Rv[:, :, :].rearrange("p (g h) j -> p g h j", g=B)
                tt(R4[:, :, :, 0:SUB], tok[:, 2, :, :].rearrange("p g (h e) -> p g h e", h=H1), over(bt, G4, 3), ALU.mult)
                g.wait_ge(S("kn_ready"), count("kn_ready", s))
                g.wait_ge(S("bD_ready"), count("bD_ready", s))
                kn = qk_n[:, 1, :, :].rearrange("p g (h e) -> p (g h) e", h=H1)
                qn = qk_n[:, 0, :, :].rearrange("p g (h e) -> p (g h) e", h=H1)
                tt(Rv[:, :, SUB:], kn, over(bD[:, :], G3, 2), ALU.mult, "Rv_ready")
                tt(Qd[:, :, :], qn, over(dec[:, 0:16], G3, 2), ALU.mult, "Qd_ready")
                tt(Kd[:, :, :], kn, over(dec[:, 16:32], G3, 2), ALU.mult, "Kd_ready")
                g.wait_ge(S("Lc_ready"), count("Lc_ready", s))
                for k in range(4):
                    tt(Bm[:, k, :, :], Lc[:, :, :], over(merge[:, k + 1, :], G3, 1), ALU.mult, f"Bm{k}_ready")
                g.wait_ge(S("rd_ready"), count("rd_ready", s))
                tt(rsq[:, :, :], rd[:, :, :], rd[:, :, :], ALU.mult, "rsq_ready")
                g.wait_ge(S("rss_ready"), count("rss_ready", s))
                g.tensor_tensor(rrs[:, :], rss[:, :], half16[:, 0, :], ALU.pow).then_inc(S("rrs_ready"), 1)

        @block.scalar
        def _(act):
            act.wait_ge(S("w3_turned"), 1)
            act.activation(w3T[:, :, :], bank(0)[:, 0:384].rearrange("p (i d) -> p i d", i=3), ACT.Copy).then_inc(S("w3T_ready"), 1)
            act.wait_ge(S("w12_loaded"), 32)
            act.wait_ge(S("l1_loaded"), 16 * 15)
            act.activation(w12s[:, 0, :], w12[:, 0, :], ACT.Sign).then_inc(S("sign_ready"), 1)
            act.activation(w12s[:, 1, :], w12[:, 1, :], ACT.Sign).then_inc(S("sign_ready"), 1)
            act.activation(ramp[:, :], ramp[:, :], ACT.Exp, scale=-1.0).then_inc(S("sign_ready"), 1)
            act.wait_ge(S("halo_zero"), 1)
            with act.Fori(0, B) as b:
                for qd in range(2):
                    w = b * 2 + (qd + 1)
                    act.wait_ge(S("xn_turned"), w)
                    if qd == 1:
                        act.wait_ge(S("xT_ready"), w - 1)
                        act.activation(xT[:, 1, 0:1], xT[:, 0, 512:513], ACT.Copy)
                    act.activation(xT[:, qd, 1:513], bank(0), ACT.Copy).then_inc(S("xT_ready"), 1)
                    act.wait_ge(S("z_ready"), (b * 2 + qd) * 2 + 1)
                    act.activation(eg[:, :], eg[:, :], ACT.Exp, scale=-1.0).then_inc(S("eg_ready"), 1)
                    act.wait_ge(S("k_done"), w)
                    act.activation(kr, bank(2), ACT.Relu).then_inc(S("kr_ready"), 1)
                    act.wait_ge(S("z_ready"), (b * 2 + qd) * 2 + 2)
                    act.activation(er, er, ACT.Exp, scale=-1.0).then_inc(S("er_ready"), 1)
                    for t in range(4):
                        act.wait_ge(S("v_done"), (b * 2 + qd) * 4 + (t + 1))
                        act.activation(V[:, ds((b * 2 + qd) * 4 + t, 1), :].rearrange("p a n -> p (a n)"),
                                       bank(6 + t % 2), ACT.Copy).then_inc(S("V_ready"), 1)

            def qk_evac(nth):
                act.wait_ge(S("proj_done"), nth)
                act.activation(Qp[0:64, 0, :], bank(0, 2)[0:64, :], ACT.Copy, scale=SCALE)
                act.activation(Qp[64:128, 1, :], bank(0, 2)[64:128, :], ACT.Copy, scale=SCALE).then_inc(S("qk_act"), 1)

            act.wait_ge(S("q_zero"), 1)
            qk_evac(1)
            with act.Fori(0, STEPS) as n:
                for k in range(UNITS + 2):
                    if k < UNITS:
                        W = (k // 2 + 1) * P
                        if k >= 4:
                            act.wait_ge(S("PT_turned"), n * UNITS + (k - 3))
                        act.wait_ge(S("max_ready"), n * UNITS + (k + 1))
                        act.activation(Pbuf[:, k % 4, 0:W], bank(2 * (k % 2), 2)[:, 0:W], ACT.Exp,
                                       bias=nb[:, k:k + 1], accum_out=rs[:, k:k + 1]).then_inc(S("exp_done"), 1)
                    if k >= 2 and (k - 2) // 2 >= 4:
                        u = k - 2
                        W = (u // 2 + 1) * P
                        act.wait_ge(S("PT_turned"), n * UNITS + (u + 1))
                        act.wait_ge(S("pv_done"), n * UNITS + (u - 1))
                        act.activation(PT[:, u % 2, 512:W], bank(5)[:, 0:W - 512], ACT.Copy).then_inc(S("PT_hi"), 1)
                    if k in (10, UNITS + 1):
                        half = int(k != 10)
                        act.wait_ge(S("R_turned"), n * 2 + (half + 1))
                        act.activation(R[:, half, :], bank(7 - half), ACT.Copy).then_inc(S("R_ready"), 1)
                qk_evac(n + 2)

            act.wait_ge(S("x1_done"), 1 + STEPS)
            act.wait_ge(S("l1_zero"), 1)
            with act.Fori(0, NT) as s:

                def cp(out, src, done, after=None, func=ACT.Copy, **kw):
                    if after:
                        act.wait_ge(S(after), count(after, s))
                    ins = act.activation(out, src, func, **kw)
                    if done:
                        ins.then_inc(S(done), 1)

                def spread(dst, src, done, after):
                    if after:
                        act.wait_ge(S(after), count(after, s))
                    for q in range(NB):
                        r = slice(q * SUB, (q + 1) * SUB)
                        ins = act.activation(dst[r, :, q * SUB:(q + 1) * SUB], src[r, :, :], ACT.Copy)
                    ins.then_inc(S(done), 1)

                cp(x1T[:, :], bank(0), "x1T_ready", "xn1_turned")
                act.activation(qkv_in[:, :, :, 0:3].rearrange("p i g k -> p (i g) k"),
                               qkv_in[:, :, :, P:P + 3].rearrange("p i g k -> p (i g) k"), ACT.Copy).then_inc(S("halo_ready"), 1)
                act.wait_ge(S("halo_ready"), count("halo_ready", s))
                for i in range(3):
                    act.wait_ge(S(f"qkv{i}_done"), count(f"qkv{i}_done", s))
                    act.activation(cy[:, i, :, :], bank(1 + i).rearrange("p (g t) -> p g t", g=B), ACT.Copy,
                                   scale=conv_w[:, i, 3:4])
                    act.activation(qkv_in[:, i, :, 3:], bank(1 + i).rearrange("p (g t) -> p g t", g=B),
                                   ACT.Copy).then_inc(S(f"qkv{i}_ready"), 1)
                cp(sg[:, :, :], ctl[:, :, :], "esg_ready", "ctl_ready", ACT.Exp, scale=-1.0)
                for i in range(3):
                    cp(ce[:, i, :, :], ce[:, i, :, :], f"ce{i}_ready", f"conv{i}_done", ACT.Exp, scale=-1.0)
                cp(la[:, :, :], al[:, :, :], "la_ready", "al_ready", ACT.Ln)
                cp(gam[:, :, :].rearrange("p g j -> p (g j)"), bank(4), "gam_ready", "gam_summed", ACT.Exp)
                cp(dec[:, :], bank(5)[:, 0:48], "dec_ready", "dec_summed", ACT.Exp)
                for t in range(FT):
                    cp(hT[:, t, :], bank(6 + t % 2), f"h{t}_ready", f"ffn{t}_done", ACT.Gelu, bias=b1col[:, t:t + 1])
                cp(kqT[:, :, 0, :], bank(6).rearrange("p (g t) -> p g t", g=B), "kT_ready", "kn_turned")
                cp(kqT[:, :, 1, :], bank(7).rearrange("p (g t) -> p g t", g=B), "qT_ready", "qn_turned")
                for k in range(4):
                    spread(Bx[:, k % 2, :, :], Bm[:, k, :, :], f"Bx{k}_ready", f"Bm{k}_ready")
                    cp(Yc[:, :, :].rearrange("p g j -> p (g j)"), bank(4), f"Y{k}_ready", f"Y{k}_done")
                    if k == 0:
                        spread(Px[:, :, :], Pc[:, :, :], "Px_ready", "Pc_ready")
                cp(Wv[:, :, :].rearrange("p g j -> p (g j)"), bank(6, 2), "Wv_ready", "W_done")
                cp(MoT[:, :, :].rearrange("p g t -> p (g t)"), bank(2), "MoT_ready", "Mo_turned")
                act.wait_ge(S("Ac_ready"), count("Ac_ready", s))
                for h in range(H1):
                    r = slice(h * E1, (h + 1) * E1)
                    ins = act.activation(Ax[r, :, :, h * E1:(h + 1) * E1].rearrange("p q g e -> p (q g) e"),
                                         Ac[r, :, :, :].rearrange("p q g e -> p (q g) e"), ACT.Copy)
                ins.then_inc(S("Ax_ready"), 1)
                cp(rdT[:, :, :].rearrange("p g t -> p (g t)"), bank(4), "rdT_ready", "rd_turned")

        @block.tensor
        def _(pe):
            pe.wait_ge(S("ident_set"), 1)
            pe.wait_ge(S("w3_loaded"), 48)
            for i in range(3):
                ins = pe.transpose(bank(0)[:, i * P:(i + 1) * P], w3[:, i, :], ident[:, :])
            ins.then_inc(S("w3_turned"), 1)
            pe.wait_ge(S("wv_loaded"), 32)
            pe.wait_ge(S("w3T_ready"), 1)
            with pe.Fori(0, B) as b:
                for qd in range(2):
                    w = b * 2 + (qd + 1)
                    pe.wait_ge(S("xn_ready"), w)
                    for t in range(4):
                        ins = pe.transpose(bank(0)[:, t * P:(t + 1) * P], xn[:, t, :], ident[:, :])
                    ins.then_inc(S("xn_turned"), 1)
                    pe.wait_ge(S("tn_ready"), w)
                    for t in range(4):
                        ins = pe.transpose(bank(1)[:, t * P:(t + 1) * P], tn[:, t, :], ident[:, :])
                    ins.then_inc(S("tn_turned"), 1)
                    pe.wait_ge(S("tS_ready"), w)
                    for t in range(4):
                        ins = pe.matmul(bank(5)[:, t * H:(t + 1) * H], tS[:, t * P:(t + 1) * P], wg_sb[:, :],
                                        start=True, stop=True)
                    ins.then_inc(S("gates_done"), 1)
                    pe.wait_ge(S("xrk_ready"), w)
                    pe.matmul(bank(2), w3T[:, 1, :], xk, start=True, stop=True).then_inc(S("k_done"), 1)
                    for t in range(4):
                        ins = pe.matmul(bank(3)[:, t * P:(t + 1) * P], xr[:, t * P:(t + 1) * P], w3T[:, 0, :],
                                        start=True, stop=True)
                    ins.then_inc(S("r_done"), 1)
                    for t in range(4):
                        pe.wait_ge(S("V_credit"), 1)
                        if t >= 2:
                            pe.wait_ge(S("V_ready"), (b * 2 + qd) * 4 + (t - 1))
                        pe.matmul(bank(6 + t % 2), tS[:, t * P:(t + 1) * P],
                                  wv_sb[:, :, :].rearrange("p h e -> p (h e)"), start=True, stop=True).then_inc(S("v_done"), 1)
                    pe.wait_ge(S("ka_ready"), w)
                    for t in range(4):
                        ins = pe.matmul(bank(4)[:, t * P:(t + 1) * P], ka[:, t * P:(t + 1) * P], w3T[:, 2, :],
                                        start=True, stop=True)
                    ins.then_inc(S("v2_done"), 1)

            def project(i, c_first):
                b_next = i // PAIRS
                for c in range(2):
                    ins = pe.matmul(bank(2 * c_first + c), wqk[:, c_first, :],
                                    TT[:, ds(b_next * N + c * 512, 512)], start=True, stop=True)
                return ins

            pe.wait_ge(S("V_ready"), TILES)
            pe.wait_ge(S("TT_ready"), QUADS)
            pe.wait_ge(S("x_ffn"), QUADS)
            pe.wait_ge(S("causal_set"), 2)
            pe.wait_ge(S("wo_loaded"), 16)
            pe.wait_ge(S("wqk_loaded"), 32)
            for c in (0, 1):
                for j in range(2):
                    ins = pe.matmul(bank(2 * c + j), wqk[:, c, :], TT[:, j * 512:(j + 1) * 512], start=True, stop=True)
            ins.then_inc(S("proj_done"), 1)
            with pe.Fori(0, STEPS) as n:
                nxt = pe.snap((n + 1) % STEPS)
                pr = pe.snap(n % PAIRS)
                for k in range(UNITS + 3):
                    if k < UNITS:
                        ib, hh = divmod(k, 2)
                        if k == 0:
                            pe.wait_ge(S("qk_act"), n + 1)
                            pe.wait_ge(S("qk_dve"), n + 1)
                        if k >= 2:
                            pe.wait_ge(S("exp_done"), n * UNITS + (k - 1))
                        for c in range(ib // 4 + 1):
                            w = min(512, (ib + 1) * P - c * 512)
                            last = c == ib // 4
                            ins = pe.matmul(bank(2 * (k % 2) + c)[:, 0:w], Qp[:, hh, ib * P:(ib + 1) * P],
                                            K[:, c * 512:c * 512 + w], start=True, stop=not last)
                        d0 = (ib % 4) * P
                        ins = pe.matmul(bank(2 * (k % 2) + ib // 4)[:, d0:d0 + P], identb[:, :], causal[:, :],
                                        start=False, stop=True)
                        ins.then_inc(S("scores_done"), 1)
                    if k == UNITS:
                        pe.wait_ge(S("wqk_loaded"), n * 32 + 64)
                        pe.wait_ge(S("exp_done"), n * UNITS + (UNITS - 1))
                        project(nxt, 0)
                    if 2 <= k < UNITS + 2:
                        u = k - 2
                        if u == 0:
                            pe.wait_ge(S("x1_done"), n + 1)
                        else:
                            pe.wait_ge(S("PT_lo"), n * UNITS + u)
                            if u - 1 >= 8:
                                pe.wait_ge(S("PT_hi"), n * 8 + (u - 8))
                        pe.wait_ge(S("exp_done"), n * UNITS + (u + 1))
                        for j in range(u // 2 + 1):
                            ins = pe.transpose(bank(4 + j // 4)[:, (j % 4) * P:(j % 4 + 1) * P],
                                               Pbuf[:, u % 4, j * P:(j + 1) * P], ident[:, :])
                        ins.then_inc(S("PT_turned"), 1)
                    if k == UNITS + 1:
                        project(nxt, 1).then_inc(S("proj_done"), 1)
                    if k in (10, UNITS + 1):
                        half = int(k != 10)
                        pe.wait_ge(S("Sx_ready"), n * 2 + (half + 1))
                        if half:
                            pe.wait_ge(S("OT_ready"), n * 2 + 1)
                        for t in range(4):
                            ins = pe.transpose(bank(7 - half)[:, t * P:(t + 1) * P],
                                               Sx[:, t, :, :].rearrange("p h e -> p (h e)"), ident[:, :])
                        ins.then_inc(S("R_turned"), 1)
                    if 3 <= k:
                        u = k - 3
                        ib, hh = divmod(u, 2)
                        pe.wait_ge(S("causal_set"), 2)
                        if u == 0:
                            pe.wait_ge(S("Vp_ready"), n + 1)
                        if u == 8:
                            pe.wait_ge(S("R_ready"), n * 2 + 1)
                        pe.wait_ge(S("PT_lo"), n * UNITS + (u + 1))
                        if u >= 8:
                            pe.wait_ge(S("PT_hi"), n * 8 + (u - 7))
                        for j in range(ib + 1):
                            ins = pe.matmul(bank(6 + ib // 4)[64 * hh:64 * hh + 64, (ib % 4) * P:(ib % 4 + 1) * P],
                                            Vp[:, j, 64 * hh:64 * hh + 64], PT[:, u % 2, j * P:(j + 1) * P],
                                            start=(j == 0), stop=(j == ib))
                        ins.then_inc(S("pv_done"), 1)
                for ib in range(NT):
                    if ib % 4 == 0:
                        pe.wait_ge(S("OT_ready"), n * 2 + (ib // 4 + 1))
                    ins = pe.matmul(bank(4 + ib // 4)[:, (ib % 4) * P:(ib % 4 + 1) * P], OT[:, ib * P:(ib + 1) * P],
                                    wo_sb[:, ds(pr, 1), :].rearrange("p a d -> p (a d)"), start=True, stop=True)
                ins.then_inc(S("wo_done"), 1)

            pe.wait_ge(S("x1_done"), 1 + STEPS)
            pe.wait_ge(S("bin_ready"), 1)
            pe.wait_ge(S("qk_act"), STEPS + 1)
            pe.wait_ge(S("qk_dve"), STEPS + 1)
            for i in range(2):
                for t in range(FT):
                    ins = pe.transpose(bank(i)[:, t * P:(t + 1) * P], w12[:, i, t * P:(t + 1) * P], ident[:, :])
            ins.then_inc(S("bin_done"), 1)
            pe.wait_ge(S("l1_loaded"), 16 * 15)
            pe.wait_ge(S("bin_turned"), 2)
            pe.wait_ge(S("l1_zero"), 1)
            with pe.Fori(0, NT) as s:

                def wait(*names):
                    for name in names:
                        pe.wait_ge(S(name), count(name, s))

                def wait_small(*names):
                    pe.wait_ge(S("l1_zero"), 1)
                    wait(*names)

                wait("xn1_ready")
                for g in range(B):
                    ins = pe.transpose(bank(0)[:, g * P:(g + 1) * P], xn1[:, g, :], ident[:, :])
                ins.then_inc(S("xn1_turned"), 1)
                wait("x1T_ready")
                for i in range(3):
                    pe.matmul(bank(1 + i), w_in[:, i * D:(i + 1) * D], x1T[:, :], start=True, stop=True).then_inc(S(f"qkv{i}_done"), 1)
                for g in range(B):
                    ins = pe.matmul(bank(4 + g // 2)[:, (g % 2) * CT:(g % 2 + 1) * CT], x1T[:, g * P:(g + 1) * P],
                                    w_ctrl[:, :], start=True, stop=True)
                ins.then_inc(S("ctrl_done"), 1)
                for t in range(FT):
                    if t >= 2:
                        wait(f"h{t - 2}_ready")
                    pe.matmul(bank(6 + t % 2), w1T[:, t * P:(t + 1) * P], x1T[:, :], start=True, stop=True).then_inc(S(f"ffn{t}_done"), 1)
                    if t == 1:
                        wait("ctl_ready", "laG_ready")
                        pe.matmul(bank(4), upto, laG[:, :, :].rearrange("p g j -> p (g j)"), start=True, stop=True).then_inc(S("gam_summed"), 1)
                        flat = la[:, :, :].rearrange("p g h -> p (g h)")
                        pe.matmul(bank(5)[:, 0:16], upto, flat, start=True, stop=True)
                        pe.matmul(bank(5)[:, 16:32], beyond, flat, start=True, stop=True)
                        wait("laX_ready")
                        for g in range(B):
                            ins = pe.matmul(bank(5)[:, 32 + g * NB:32 + (g + 1) * NB], laX[:, g, :], in_block,
                                            start=True, stop=True)
                        ins.then_inc(S("dec_summed"), 1)
                        for i in range(3):
                            wait(f"silu{i}_ready")
                            for g in range(B):
                                ins = pe.transpose(bank(1 + i)[:, g * P:(g + 1) * P], cy[:, i, g, :], ident[:, :])
                            ins.then_inc(S(f"tok{i}_turned"), 1)
                for t in range(FT):
                    wait(f"h{t}_ready")
                for g in range(B):
                    for t in range(FT):
                        ins = pe.matmul(bank(0)[:, g * P:(g + 1) * P], hT[:, t, g * P:(g + 1) * P], w2T[:, t, :],
                                        start=(t == 0), stop=(t == FT - 1))
                ins.then_inc(S("ffn_out"), 1)
                wait("kn_ready")
                for i, name in ((1, "kn_turned"), (0, "qn_turned")):
                    for g in range(B):
                        ins = pe.transpose(bank(7 - i)[:, g * P:(g + 1) * P], qk_n[:, i, g, :], ident[:, :])
                    ins.then_inc(S(name), 1)
                wait_small("kT_ready", "qT_ready", "tok_ready", "acc_ready")
                for g in range(B):
                    for q in range(NB):
                        for h in range(H1):
                            r, c = slice(h * E1, (h + 1) * E1), slice(q * SUB, (q + 1) * SUB)
                            ins = pe.matmul(bank(h)[c, g * 64:(g + 1) * 64].rearrange("p (a j) -> p a j", a=2),
                                            kqT[r, g, 0, c], kqT[r, g, :, c], start=True, stop=True)
                ins.then_inc(S("kk_done"), 1)

                def systems(dst, lhs, rhs, n):
                    for i in range(GH):
                        ins = pe.matmul(dst(i), lhs[:, i, :], rhs[:, i, 0:n], start=True, stop=True)
                    return ins

                for k in range(4):
                    wait(f"Bx{k}_ready", f"Z{k}_ready")
                    systems(lambda i: bank(4)[:, i * SUB:(i + 1) * SUB], Bx[:, k % 2, :, :], Zc[:, k % 2, :, :], SUB).then_inc(S(f"Y{k}_done"), 1)
                    wait(f"Y{k}_ready", f"Tx{k}_ready")
                    systems(lambda i: bank(5)[:, i * SUB:(i + 1) * SUB], Tx[:, :, :], Yc[:, :, :], SUB).then_inc(S(f"ZY{k}_done"), 1)
                wait("Tx4_ready", "Rv_ready")
                systems(lambda i: bank(6 + i // 8)[:, (i % 8) * 64:(i % 8 + 1) * 64], Tx[:, :, :], Rv[:, :, :], 64).then_inc(S("W_done"), 1)
                wait("Wv_ready", "Px_ready")
                systems(lambda i: bank(i // 8)[:, (i % 8) * 64:(i % 8 + 1) * 64], Px[:, :, :], Wv[:, :, :], 64).then_inc(S("PW_done"), 1)
                wait_small("Kd_ready", "Wv_ready")
                for g in range(B):
                    for h in range(H1):
                        for q in range(NB):
                            r, c = slice(q * SUB, (q + 1) * SUB), slice(h * E1, (h + 1) * E1)
                            ins = pe.matmul(bank(3 + q)[c, g * 64:(g + 1) * 64], Kd[r, g * H1 + h, :], Wv[r, g * H1 + h, :],
                                            start=True, stop=True)
                ins.then_inc(S("AB_done"), 1)
                wait("Mo_ready")
                for g in range(B):
                    ins = pe.transpose(bank(2)[:, g * P:(g + 1) * P], Mo[:, g * H1:(g + 1) * H1, :].rearrange("p h e -> p (h e)"), ident[:, :])
                ins.then_inc(S("Mo_turned"), 1)
                wait("Ax_ready", "Bc_ready")
                for q in range(NB):
                    wait(f"St{q}_ready")
                    for g in range(B):
                        ins = pe.matmul(bank(7)[:, q * P + g * SUB:q * P + (g + 1) * SUB], Ax[:, q, g, :], St[:, q, g, :],
                                        start=True, stop=True)
                    ins.then_inc(S(f"AS{q}_done"), 1)
                wait_small("MoT_ready", "St4_ready")
                for g in range(B):
                    for q in range(NB):
                        for h in range(H1):
                            r, c = slice(h * E1, (h + 1) * E1), slice(q * SUB, (q + 1) * SUB)
                            ins = pe.matmul(bank(h)[c, g * SUB:(g + 1) * SUB], MoT[r, g, c], St[r, q, g, :],
                                            start=True, stop=True)
                ins.then_inc(S("MS_done"), 1)
                wait("rdn_ready")
                for g in range(B):
                    ins = pe.transpose(bank(4)[:, g * P:(g + 1) * P], rdn[:, g, :], ident[:, :])
                ins.then_inc(S("rd_turned"), 1)
                wait("rdT_ready")
                for g in range(B):
                    ins = pe.matmul(bank(5)[:, g * P:(g + 1) * P], rdT[:, g, :], w_out[:, :], start=True, stop=True)
                ins.then_inc(S("out_done"), 1)

        @block.vector
        def _(v):
            def row_moments(name, raw="stats_raw"):
                even, odd = stats[:, :, 1], stats[:, :, 4]
                v.wait_ge(S(raw), QUADS)
                v.tensor_tensor(mean[:, :], even, odd, ALU.add).then_inc(S(name), 1)
                v.tensor_tensor(ve[:, :], even, odd, ALU.subtract).then_inc(S(name), 1)
                v.tensor_tensor(rms2[:, :], stats[:, :, 2], stats[:, :, 5], ALU.add).then_inc(S(name), 1)
                v.wait_ge(S(name), 2)
                v.tensor_scalar(mean[:, :], mean[:, :], 0.5, None, ALU.mult)
                v.scalar_tensor_tensor(ve[:, :], ve[:, :], 0.25, ve[:, :], ALU.mult, ALU.mult).then_inc(S(name), 1)
                v.wait_ge(S(name), 4)
                v.scalar_tensor_tensor(var[:, :], rms2[:, :], 1.0 / D, ve[:, :], ALU.mult, ALU.add).then_inc(S("stats_done"), 1)

            v.wait_ge(S("w12_loaded"), 32)
            v.tensor_reduce(alpha[:, 0:FT], w12[:, 0, :].rearrange("p (t d) -> p t d", t=FT), AX.X, ALU.add,
                            apply_absolute_value=True)
            v.tensor_reduce(alpha[:, FT:FT + 1], w12[:, 1, :], AX.X, ALU.add, apply_absolute_value=True).then_inc(S("alpha_sum"), 1)
            v.wait_ge(S("alpha_sum"), 1)
            v.tensor_scalar(alpha[:, 0:FT], alpha[:, 0:FT], 1.0 / D, None, ALU.mult).then_inc(S("alpha_ready"), 1)
            v.tensor_scalar(alpha[:, FT:FT + 1], alpha[:, FT:FT + 1], 1.0 / (FT * P), None, ALU.mult).then_inc(S("alpha_ready"), 1)
            v.wait_ge(S("sign_ready"), 3)
            v.tensor_scalar(ramp[:, :], ramp[:, :], 1.0, None, ALU.add).then_inc(S("ramp_step"), 1)
            v.wait_ge(S("ramp_step"), 1)
            v.reciprocal(ramp[:, :], ramp[:, :]).then_inc(S("ramp_ready"), 1)
            v.wait_ge(S("x_loaded"), 16 * B)
            with v.Fori(0, QUADS) as q:
                for t in range(4):
                    ins = v.bn_stats(stats[:, ds(q * 4 + t, 1), :].rearrange("p a s -> p (a s)"),
                                     X[:, ds(q * 4 + t, 1), :].rearrange("p a d -> p (a d)"))
                ins.then_inc(S("stats_raw"), 1)
            row_moments("row_step")
            v.memset(rg[:, 0:1], 0.0).then_inc(S("V_credit"), 1)
            v.wait_ge(S("rms_loaded"), 16)
            v.wait_ge(S("mu_loaded"), 32)
            v.wait_ge(S("rstd_step"), 6)
            with v.Fori(0, B) as b:
                for qd in range(2):
                    w = b * 2 + (qd + 1)
                    q4 = b * 8 + qd * 4
                    for t in range(4):
                        ins = v.tensor_scalar(xn[:, t, :], X[:, ds(q4 + t, 1), :].rearrange("p a d -> p (a d)"),
                                              mean[:, ds(q4 + t, 1)], rstd[:, ds(q4 + t, 1)],
                                              ALU.subtract, ALU.mult)
                    ins.then_inc(S("xn_ready"), 1)
                    v.wait_ge(S("xn_ready"), w)
                    for t in range(4):
                        ins = v.tensor_scalar(tn[:, t, :], xn[:, t, :], rrms[:, ds(q4 + t, 1)], None, ALU.mult)
                    ins.then_inc(S("tn_ready"), 1)
                    v.wait_ge(S("tn_turned"), w)
                    v.tensor_scalar(tS, bank(1), rms_w[:, 0:1], None, ALU.mult).then_inc(S("tS_ready"), 1)
                    v.wait_ge(S("shift_ready"), w)
                    v.scalar_tensor_tensor(xr, xT[:, qd, 1:513], mu[:, 0:1], tmr, ALU.mult, ALU.add)
                    v.scalar_tensor_tensor(xk, xT[:, qd, 1:513], mu[:, 2:3], tmk, ALU.mult, ALU.add).then_inc(S("xrk_ready"), 1)
                    v.wait_ge(S("gates_done"), w)
                    v.tensor_scalar(eg[:, :], bank(5)[:, 0:32], Z_MIN, None, ALU.max).then_inc(S("z_ready"), 1)
                    v.wait_ge(S("r_done"), w)
                    v.tensor_scalar(er, bank(3), Z_MIN, None, ALU.max).then_inc(S("z_ready"), 1)
                    v.wait_ge(S("eg_ready"), w)
                    v.tensor_scalar(rg[:, :], eg[:, :], 1.0, None, ALU.add).then_inc(S("sig_step"), 1)
                    v.wait_ge(S("er_ready"), w)
                    v.tensor_scalar(rr, er, 1.0, None, ALU.add).then_inc(S("sig_step"), 1)
                    v.wait_ge(S("sig_step"), w * 4 - 2)
                    v.reciprocal(rg[:, :], rg[:, :]).then_inc(S("sig_step"), 1)
                    v.reciprocal(rr, rr).then_inc(S("sig_step"), 1)
                    v.wait_ge(S("sig_step"), w * 4)
                    v.tensor_scalar(G[:, ds(q4, 4), :], rg[:, :].rearrange("p (t h) -> p t h", t=4), 1.0, None,
                                    ALU.mult).then_inc(S("G_ready"), 1)
                    v.wait_ge(S("v2_done"), w)
                    v.tensor_tensor(fo, bank(4), rr, ALU.mult).then_inc(S("fo_ready"), 1)
                    v.wait_ge(S("fo_ready"), w)
                    v.tensor_tensor(X[:, ds(q4, 4), :], X[:, ds(q4, 4), :], fo.rearrange("p (t d) -> p t d", t=4),
                                    ALU.add).then_inc(S("x_ffn"), 1)

            def copy_v(i, pr):
                v.tensor_scalar(Vp[:, :, :], V[:, ds((i // PAIRS) * NT, NT), ds(pr * 2 * E, 2 * E)], 1.0, None,
                                ALU.mult).then_inc(S("Vp_ready"), 1)

            v.wait_ge(S("V_ready"), TILES)
            v.tensor_scalar(Vp[:, :, :], V[:, 0:NT, 0:2 * E], 1.0, None, ALU.mult).then_inc(S("Vp_ready"), 1)
            v.wait_ge(S("proj_done"), 1)
            v.tensor_copy(K[:, :], bank(2, 2)).then_inc(S("qk_dve"), 1)
            v.wait_ge(S("x_ffn"), QUADS)
            v.memset(gs[:, 0, 0:1], 0.0).then_inc(S("x1_done"), 1)
            with v.Fori(0, STEPS) as n:
                nxt = v.snap((n + 1) % STEPS)
                nxt_pair = v.snap((n + 1) % PAIRS)
                pr = v.snap(n % PAIRS)
                tile0 = v.snap((n // PAIRS) * NT)
                for k in range(UNITS + 2):
                    if k < UNITS:
                        W = (k // 2 + 1) * P
                        v.wait_ge(S("scores_done"), n * UNITS + (k + 1))
                        v.tensor_reduce(nb[:, k:k + 1], bank(2 * (k % 2), 2)[:, 0:W], AX.X, ALU.max,
                                        negate=True).then_inc(S("max_ready"), 1)
                    if k >= 2:
                        u = k - 2
                        W = min(512, (u // 2 + 1) * P)
                        if u >= 2:
                            v.wait_ge(S("pv_done"), n * UNITS + (u - 1))
                        v.wait_ge(S("PT_turned"), n * UNITS + (u + 1))
                        v.tensor_copy(PT[:, u % 2, 0:W], bank(4)[:, 0:W]).then_inc(S("PT_lo"), 1)
                    if k in (9, UNITS + 1):
                        half = int(k != 9)
                        v.wait_ge(S("exp_done"), n * UNITS + (8 * half + 8))
                        v.reciprocal(rinv[:, 8 * half:8 * half + 8], rs[:, 8 * half:8 * half + 8]).then_inc(S("gs_step"), 1)
                        v.wait_ge(S("gs_step"), n * 4 + (2 * half + 1))
                        v.tensor_tensor(gs[:, :, :], rinv[:, 8 * half:8 * half + 8].rearrange("p (t h) -> p t h", h=2),
                                        G[:, ds(tile0 + 4 * half, 4), ds(pr * 2, 2)], ALU.mult).then_inc(S("gs_step"), 1)
                        v.wait_ge(S("gs_step"), n * 4 + (2 * half + 2))
                        v.tensor_copy(Sx[:, :, :, :], gs[:, :, :].unsqueeze(3).to_broadcast([P, 4, 2, E])).then_inc(S("Sx_ready"), 1)
                    if k == 12:
                        v.wait_ge(S("pv_done"), n * UNITS + 8)
                        v.wait_ge(S("R_ready"), n * 2 + 1)
                        v.tensor_tensor(OT[:, 0:512], bank(6), R[:, 0, :], ALU.mult).then_inc(S("OT_ready"), 1)
                v.wait_ge(S("proj_done"), n + 2)
                v.tensor_copy(K[:, :], bank(2, 2)).then_inc(S("qk_dve"), 1)
                v.wait_ge(S("pv_done"), n * UNITS + UNITS)
                v.wait_ge(S("R_ready"), n * 2 + 2)
                v.tensor_tensor(OT[:, 512:1024], bank(7), R[:, 1, :], ALU.mult).then_inc(S("OT_ready"), 1)
                copy_v(nxt, nxt_pair)
                v.wait_ge(S("wo_done"), n + 1)
                v.tensor_tensor(X[:, ds(tile0, NT), :], X[:, ds(tile0, NT), :],
                                bank(4, 2).rearrange("p (t d) -> p t d", t=NT), ALU.add).then_inc(S("x1_done"), 1)


            v.wait_ge(S("x1_done"), 1 + STEPS)
            with v.Fori(0, QUADS) as q:
                for t in range(4):
                    ins = v.bn_stats(stats[:, ds(q * 4 + t, 1), :].rearrange("p a s -> p (a s)"),
                                     X[:, ds(q * 4 + t, 1), :].rearrange("p a d -> p (a d)"))
                ins.then_inc(S("stats_raw2"), 1)
            row_moments("row_step2", "stats_raw2")
            v.wait_ge(S("bin_done"), 1)
            v.tensor_copy(w1T[:, :], bank(0)).then_inc(S("bin_turned"), 1)
            v.tensor_copy(w2T[:, :, :].rearrange("p t d -> p (t d)"), bank(1)).then_inc(S("bin_turned"), 1)
            v.wait_ge(S("rstd_step"), 8)
            v.wait_ge(S("l1_zero"), 1)
            XS = X[:, :, :].rearrange("p (g t) d -> p g t d", g=B)
            MS = mean[:, :].rearrange("p (g t) -> p g t", g=B)
            RS = rstd[:, :].rearrange("p (g t) -> p g t", g=B)
            with v.Fori(0, NT) as s:

                def wait(*names):
                    for name in names:
                        v.wait_ge(S(name), count(name, s))

                def over(ap, shape, at):
                    return ap.unsqueeze(at).to_broadcast(shape)

                G3 = [P, GH, SUB]
                G4 = [P, B, H1, SUB]
                for g in range(B):
                    ins = v.tensor_scalar(xn1[:, g, :], XS[:, g, ds(s, 1), :].rearrange("p a d -> p (a d)"),
                                          MS[:, g, ds(s, 1)], RS[:, g, ds(s, 1)], ALU.subtract, ALU.mult)
                ins.then_inc(S("xn1_ready"), 1)
                wait("ctrl_done")
                for i in range(2):
                    ins = v.tensor_tensor(ctl[:, 2 * i:2 * i + 2, :], bank(4 + i)[:, 0:2 * CT].rearrange("p (g c) -> p g c", g=2),
                                          over(b_ctrl[:, :], [P, 2, CT], 1), ALU.add)
                ins.then_inc(S("ctl_raw"), 1)
                wait("ctl_raw")
                v.tensor_scalar(ctl[:, :, :], ctl[:, :, :], Z_MIN, None, ALU.max).then_inc(S("ctl_ready"), 1)
                wait("esg_ready")
                v.tensor_scalar(ctl[:, :, :], sg[:, :, :], 1.0, None, ALU.add).then_inc(S("sg1"), 1)
                wait("sg1")
                v.reciprocal(sg[:, :, :], ctl[:, :, :]).then_inc(S("sg_ready"), 1)
                wait("sg_ready")
                v.tensor_scalar(al[:, :, :], sg[:, :, 0:H1], 0.98, 0.01, ALU.mult, ALU.add).then_inc(S("al_ready"), 1)
                for k in (2, 1, 0):
                    for i in range(3):
                        wait(f"qkv{i}_ready" if k == 2 else f"conv{i}_{k + 1}")
                        v.scalar_tensor_tensor(cy[:, i, :, :], qkv_in[:, i, :, k:k + P], conv_w[:, i, k:k + 1],
                                               cy[:, i, :, :], ALU.mult, ALU.add).then_inc(S(f"conv{i}_{k}"), 1)
                for i in range(3):
                    wait(f"conv{i}_0")
                    v.tensor_scalar(ce[:, i, :, :], cy[:, i, :, :], Z_MIN, None, ALU.max).then_inc(S(f"conv{i}_done"), 1)
                for i in range(3):
                    wait(f"ce{i}_ready")
                    v.tensor_scalar(ce[:, i, :, :], ce[:, i, :, :], 1.0, None, ALU.add).then_inc(S(f"silu{i}_a"), 1)
                for i in range(3):
                    wait(f"silu{i}_a")
                    v.reciprocal(ce[:, i, :, :], ce[:, i, :, :]).then_inc(S(f"silu{i}_b"), 1)
                for i in range(3):
                    wait(f"silu{i}_b")
                    v.tensor_tensor(cy[:, i, :, :], cy[:, i, :, :], ce[:, i, :, :], ALU.mult).then_inc(S(f"silu{i}_ready"), 1)
                for i in range(3):
                    wait(f"tok{i}_turned")
                    ins = v.tensor_copy(tok[:, i, :, :].rearrange("p g d -> p (g d)"), bank(1 + i))
                ins.then_inc(S("tok_ready"), 1)
                wait("ffn_out")
                v.tensor_tensor(acc[:, :, :].unsqueeze(2), XS[:, :, ds(s, 1), :], bank(0).rearrange("p (g a d) -> p g a d", g=B, a=1),
                                ALU.add).then_inc(S("acc_ready"), 1)
                wait("acc_ready")
                v.tensor_tensor(acc[:, :, :], acc[:, :, :], over(b2row[:, :], [P, B, D], 1), ALU.add).then_inc(S("acc2_ready"), 1)
                wait("sq_ready")
                v.tensor_reduce(ss[:, :, :], sq[:, :, :, :].rearrange("p i g (h e) -> p i (g h) e", e=E1), AX.X, ALU.add).then_inc(S("ss_raw"), 1)
                wait("ss_raw")
                v.tensor_scalar(ss[:, :, :], ss[:, :, :], 1e-12, None, ALU.max).then_inc(S("ss_ready"), 1)
                wait("rn_ready")
                for i in range(2):
                    ins = v.tensor_tensor(qk_n[:, i, :, :].rearrange("p g (h e) -> p (g h) e", e=E1),
                                          tok[:, i, :, :].rearrange("p g (h e) -> p (g h) e", e=E1), over(rn[:, i, :], G3, 2), ALU.mult)
                ins.then_inc(S("kn_ready"), 1)
                wait("gam_m_ready")
                v.transpose(gam_t[:, :, :].rearrange("p g j -> p (g j)"), gam_m[:, :, :].rearrange("p g j -> p (g j)")).then_inc(S("gam_t_ready"), 1)
                wait("kk_done", "gam_b_ready")
                kkp = ps_all[:, 0:4, 0:256].rearrange("p h (g a j) -> p h g a j", g=B, a=2)

                def by_head(t, h):
                    return t[:, :, :].rearrange("p (g h) j -> p g h j", g=B)[:, :, h, :]

                for h in range(H1):
                    ins = v.tensor_tensor(by_head(Lc, h), kkp[:, h, :, 0, :], by_head(gam_b, h), ALU.mult)
                ins.then_inc(S("Lc_ready"), 1)
                wait("gam_t_ready")
                for h in range(H1):
                    ins = v.tensor_tensor(by_head(Pc, h), kkp[:, h, :, 1, :], by_head(gam_t, h), ALU.mult)
                ins.then_inc(S("Pc_ready"), 1)
                wait("Lc_ready")
                v.tensor_tensor(Tc[:, :, :], Lc[:, :, :], over(merge[:, 0, :], G3, 1), ALU.mult).then_inc(S("T2_raw"), 1)
                wait("T2_raw")
                v.tensor_tensor(Tc[:, :, :], over(eye, G3, 1), Tc[:, :, :], ALU.subtract).then_inc(S("T0_ready"), 1)
                wait("T0_ready")
                v.transpose(Zc[:, 0, :, :].rearrange("p g j -> p (g j)"), Tc[:, :, :].rearrange("p g j -> p (g j)")).then_inc(S("Z0_ready"), 1)

                def spread(src, name):
                    for q in range(NB):
                        r = slice(q * SUB, (q + 1) * SUB)
                        ins = v.tensor_copy(Tx[r, :, q * SUB:(q + 1) * SUB], src[r, :, :])
                    ins.then_inc(S(name), 1)

                spread(Tc, "Tx0_ready")
                for k in range(4):
                    wait(f"ZY{k}_done")
                    v.tensor_tensor(Zc[:, (k + 1) % 2, :, :], Zc[:, k % 2, :, :], bank(5).rearrange("p (g j) -> p g j", g=GH),
                                    ALU.subtract).then_inc(S(f"Z{k + 1}_ready"), 1)
                    wait(f"Z{k + 1}_ready")
                    if k < 3:
                        v.transpose(Tc[:, :, :].rearrange("p g j -> p (g j)"),
                                    Zc[:, (k + 1) % 2, :, :].rearrange("p g j -> p (g j)")).then_inc(S(f"T{k + 1}_ready"), 1)
                        wait(f"T{k + 1}_ready")
                        spread(Tc, f"Tx{k + 1}_ready")
                    else:
                        spread(Zc[:, 0, :, :], "Tx4_ready")
                wait("PW_done")
                pw = bank(0, 2).rearrange("p (g j) -> p g j", g=GH)
                wait("Qd_ready")
                v.tensor_tensor(Mo[:, :, :], Qd[:, :, :], pw[:, :, SUB:], ALU.subtract).then_inc(S("Mo_ready"), 1)
                v.tensor_copy(Ov[:, :, :], pw[:, :, 0:SUB]).then_inc(S("Ov_ready"), 1)
                wait("AB_done", "dec_ready")
                abp = ps_all[:, 3:7, 0:256].rearrange("p q (g a j) -> p q g a j", g=B, a=2)
                for q in range(NB):
                    for g in range(B):
                        ins = v.scalar_tensor_tensor(At[:, q, g, :], eye, dec[:, 32 + g * NB + q:33 + g * NB + q],
                                                     abp[:, q, g, 1, :], ALU.mult, ALU.subtract)
                ins.then_inc(S("At_ready"), 1)
                for q in range(NB):
                    ins = v.tensor_copy(Bc[:, q, :, :], abp[:, q, :, 0, :])
                ins.then_inc(S("Bc_ready"), 1)
                wait("At_ready")
                v.transpose(Ac[:, :, :, :].rearrange("p q g e -> p (q g e)"), At[:, :, :, :].rearrange("p q g e -> p (q g e)")).then_inc(S("Ac_ready"), 1)
                v.tensor_copy(St[:, 0, :, :], St[:, NB, :, :]).then_inc(S("St0_ready"), 1)
                wait("St0_ready", "Bc_ready")
                for q in range(NB):
                    wait(f"AS{q}_done")
                    v.tensor_tensor(St[:, q + 1, :, :], bank(7)[:, q * P:(q + 1) * P].rearrange("p (g j) -> p g j", g=B),
                                    Bc[:, q, :, :], ALU.add).then_inc(S(f"St{q + 1}_ready"), 1)
                wait("MS_done", "Ov_ready")
                for h in range(H1):
                    ins = v.tensor_tensor(by_head(rd, h), bank(h)[:, 0:P].rearrange("p (g j) -> p g j", g=B), by_head(Ov, h), ALU.add)
                ins.then_inc(S("rd_ready"), 1)
                wait("rsq_ready")
                v.tensor_reduce(rss[:, :], rsq[:, :, :], AX.X, ALU.add).then_inc(S("rss_raw"), 1)
                wait("rss_raw")
                v.tensor_scalar(rss[:, :], rss[:, :], 1.0 / E1, 1e-6, ALU.mult, ALU.add).then_inc(S("rss_ready"), 1)
                wait("rrs_ready")
                v.tensor_tensor(rdn[:, :, :].rearrange("p g (h e) -> p (g h) e", e=E1), rd[:, :, :], over(rrs[:, :], G3, 2),
                                ALU.mult).then_inc(S("rdn_ready"), 1)
                wait("out_done")
                v.tensor_tensor(ao[:, :, :], bank(5).rearrange("p (g d) -> p g d", g=B), over(b_out[:, :], [P, B, D], 1),
                                ALU.add).then_inc(S("ao1"), 1)
                wait("ao1", "ogr_ready")
                v.tensor_tensor(ao[:, :, :], ao[:, :, :], ogr[:, :, :], ALU.mult).then_inc(S("ao2"), 1)
                v.wait_ge(S("stored"), s * 16 + 16)
                wait("ao2", "acc2_ready")
                v.tensor_tensor(res[:, :, :], acc[:, :, :], ao[:, :, :], ALU.add).then_inc(S("res_ready"), 1)


_INS = ['L0_attn_tokens', 'L0_attn_wq', 'L0_attn_wk', 'L0_attn_wv', 'L0_attn_wo', 'L0_attn_w_gates', 'L0_attn_rms_w',
        'L0_ffn_W_r', 'L0_ffn_W_k', 'L0_ffn_W_v', 'L0_ffn_mu_r', 'L0_ffn_mu_k', 'L1_attn_W_in', 'L1_attn_W_ctrl',
        'L1_attn_b_ctrl', 'L1_attn_w_q', 'L1_attn_w_k', 'L1_attn_w_v', 'L1_attn_W_out', 'L1_attn_b_out',
        'L1_attn_ramp_logit', 'L1_ffn_w1', 'L1_ffn_b1', 'L1_ffn_w2', 'L1_ffn_b2']
_OUTS = [((4, 1024, 128), 'float32')]


def _masks():
    import numpy as _np

    n, sub = 128, 32
    r, c = _np.arange(n)[:, None], _np.arange(n)[None, :]
    j = _np.arange(sub)[None, :]
    i = r % sub
    parts = [(r // sub == c // sub) & (r <= c), (r // sub == c // sub) & (r > c),
             r // sub == _np.arange(n // sub)[None, :], i == j, j < i, j <= i]
    for m in (1, 2, 4, 8, 16):
        parts.append((i // (2 * m) == j // (2 * m)) & (i % (2 * m) >= m) & (j % (2 * m) < m))
    return _np.concatenate(parts, axis=1).astype(_np.float32)


def kernel(**inputs):
    import numpy as _np
    import concourse.bacc as _bacc
    from concourse import mybir as _mybir
    from concourse.bass_utils import run_bass_kernel_spmd as _run

    nc = _bacc.Bacc("TRN2", target_bir_lowering=False, num_devices=1)
    arrays, aps = {}, {}
    for name in _INS:
        a = _np.ascontiguousarray(inputs[name])
        arrays[f"in_{name}_dram"] = a
        aps[name] = nc.dram_tensor(f"in_{name}_dram", a.shape, _mybir.dt.from_np(a.dtype), kind="ExternalInput").ap()
    arrays["masks_dram"] = _masks()
    aps["masks"] = nc.dram_tensor("masks_dram", arrays["masks_dram"].shape, _mybir.dt.float32, kind="ExternalInput").ap()
    outs = []
    for i, (shape, dtype) in enumerate(_OUTS):
        dt = _mybir.dt.from_np(_np.dtype(dtype))
        outs.append(nc.dram_tensor(f"out_{i}_dram", shape, dt, kind="ExternalOutput").ap())
    build(nc, aps, outs[0])
    r = _run(nc, [arrays], core_ids=[0])
    return r.results[0]["out_0_dram"]
```

```python
from contextlib import ExitStack

import concourse.bass as bass
from concourse import mybir

ALU = mybir.AluOpType
ACT = mybir.ActivationFunctionType
AX = mybir.AxisListType
F32 = mybir.dt.float32
BF16 = mybir.dt.bfloat16
ds = bass.ds

P = 128
EPS_LN = 1e-5
EPS_RMS = 1.1920928955078125e-07
MASKED = -1e30
Z_MIN = -44.0


def build(nc, A, out):
    B, N, D = A["L0_attn_tokens"].shape
    H, _, E = A["L0_attn_wq"].shape
    NT = N // P
    TILES = B * NT
    QUADS = TILES // 4
    PAIRS = H // 2
    STEPS = B * PAIRS
    UNITS = 2 * NT
    SCALE = float(E) ** -0.5
    H1 = 4
    E1 = D // H1
    SUB = 32
    NB = P // SUB
    GH = B * H1
    CT = A["L1_attn_W_ctrl"].shape[1]
    FT = A["L1_ffn_w1"].shape[0] // P
    assert E1 == SUB == 32 and B == 4 and NB == 4

    x_dram = A["L0_attn_tokens"].rearrange("b (t p) d -> p (b t) d", p=P)
    out_dram = out.rearrange("b (t p) d -> p (b t) d", p=P)

    with ExitStack() as ctx:
        def sb(name, shape, dt=F32):
            return ctx.enter_context(nc.sbuf_tensor(name, shape, dt))

        sems = {}
        shared = {}
        for family, steps in {
            "conv": [f"conv{i}_{k}" for k in (2, 1, 0) for i in range(3)] + [f"conv{i}_done" for i in range(3)],
            "join": ["T2_raw", "T0_ready", "Z0_ready", "Tx0_ready"]
            + [f"{x}{k}_ready" for k in (1, 2, 3) for x in ("Z", "T", "Tx")] + ["Z4_ready", "Tx4_ready"],
            "state": ["St0_ready", "St1_ready", "St2_ready", "St3_ready"],
            "norm": ["sq_ready", "ss_raw", "ss_ready", "rn_a", "rn_b", "rn_ready"],
            "control": ["ctl_raw", "ctl_ready", "al_ready"],
            "read": ["rd_ready", "rsq_ready", "rss_raw", "rss_ready", "rrs_a", "rrs_b", "rrs_ready", "rdn_ready"],
            "qkv_done": [f"qkv{i}_done" for i in range(3)],
            "ffn_done": [f"ffn{t}_done" for t in range(FT)],
            "tok_turned": [f"tok{i}_turned" for i in range(3)],
            "join_products": [f"{x}{k}_done" for k in range(4) for x in ("Y", "ZY")],
            "AS_done": [f"AS{q}_done" for q in range(NB)],
            "qkv_ready": [f"qkv{i}_ready" for i in range(3)],
            "sigmoid": ["sg_e", "sg_l", "sg_ready"],
            "ce": [f"ce{i}_{x}" for x in ("e", "l", "s") for i in range(3)],
            "silu": [f"silu{i}_ready" for i in range(3)],
            "h_ready": [f"h{t}_ready" for t in range(FT)],
            "Bx_ready": [f"Bx{k}_ready" for k in range(4)],
            "Y_ready": [f"Y{k}_ready" for k in range(4)],
            "Bm_ready": [f"Bm{k}_ready" for k in range(4)],
            "roots": ["rn_l", "rn_e"],
            "read_roots": ["rrs_l", "rrs_e"],
        }.items():
            for i, step in enumerate(steps):
                shared[step] = (family, len(steps), i)

        def count(name, s):
            _, per, i = shared.get(name, (name, 1, 0))
            return s * per + (i + 1)

        def S(name):
            name = shared.get(name, (name,))[0]
            if name not in sems:
                sems[name] = ctx.enter_context(nc.semaphore(name))
            return sems[name]

        ps_all = ctx.enter_context(nc.psum_tensor("ps_all", [P, 8, 512], F32))

        def bank(i, n=1):
            return ps_all[:, i, :] if n == 1 else ps_all[:, i:i + n, :].rearrange("p b n -> p (b n)")

        X = sb("X", [P, TILES, D])
        stats = sb("stats", [P, TILES, 6])
        mean = sb("mean", [P, TILES])
        var = sb("var", [P, TILES])
        ve = sb("ve", [P, TILES])
        rstd = sb("rstd", [P, TILES])
        rms2 = sb("rms2", [P, TILES])
        rrms = sb("rrms", [P, TILES])
        neg_half = sb("neg_half", [P, TILES])
        ident = sb("ident", [P, P])
        identb = sb("identb", [P, P], BF16)
        causal = sb("causal", [P, P], BF16)
        w_in = sb("w_in", [P, 3 * D])
        w_ctrl = sb("w_ctrl", [P, CT])
        w_out = sb("w_out", [P, D])
        b_ctrl = sb("b_ctrl", [P, CT])
        b_out_sb = sb("b_out", [P, D])
        ramp = sb("ramp", [P, D])
        b2row = sb("b2row", [P, D])
        b1col = sb("b1col", [P, FT])
        conv_w = sb("conv_w", [P, 3, 4])
        w1T = sb("w1T", [P, FT * P])
        w2T = sb("w2T", [P, FT, D])
        masks = sb("masks", [P, 2 * P + NB + 8 * SUB])
        upto = masks[:, 0:P]
        beyond = masks[:, P:2 * P]
        in_block = masks[:, 2 * P:2 * P + NB]
        compact = masks[:, 2 * P + NB:].rearrange("p (k j) -> p k j", j=SUB)
        eye, below, upto_c = compact[:, 0, :], compact[:, 1, :], compact[:, 2, :]
        merge = compact[:, 3:8, :]
        persistent = sb
        l0 = ExitStack()

        def sb(name, shape, dt=F32):
            return l0.enter_context(nc.sbuf_tensor(name, shape, dt))

        wv_sb = sb("wv_sb", [P, H, E])
        wg_sb = sb("wg_sb", [P, H])
        rms_w = sb("rms_w", [P, 1])
        wqk = sb("wqk", [P, 2, 2 * E])
        wo_sb = sb("wo_sb", [P, PAIRS, D])
        w3 = sb("w3", [P, 3, D])
        w3T = sb("w3T", [P, 3, D])
        mu = sb("mu", [P, 4])
        TT = sb("TT", [P, B * N])
        V = sb("V", [P, TILES, H * E])
        G = sb("G", [P, TILES, H])

        Pbuf = sb("Pbuf", [P, 4, N])
        PT = sb("PT", [P, 2, N])
        Qp = sb("Qp", [P, 2, N])
        K = sb("K", [P, N])
        Vp = sb("Vp", [P, NT, 2 * E])
        OT = sb("OT", [P, N])
        R = sb("R", [P, 2, 512])
        Sx = sb("Sx", [P, 4, 2, E])
        nb = sb("nb", [P, UNITS])
        rs = sb("rs", [P, UNITS])
        rinv = sb("rinv", [P, UNITS])
        gs = sb("gs", [P, 4, 2])

        xn = Pbuf[:, 0, 0:512].rearrange("p (t d) -> p t d", t=4)
        tn = Pbuf[:, 0, 512:1024].rearrange("p (t d) -> p t d", t=4)
        xT = sb("xT", [P, 2, 1 + 512])
        tS = Pbuf[:, 1, 0:512]
        xr = Pbuf[:, 1, 512:1024]
        xk = Pbuf[:, 2, 0:512]
        tmr = Pbuf[:, 2, 512:1024]
        tmk = Pbuf[:, 3, 0:512]
        kr = Pbuf[:, 3, 512:1024]
        ka = PT[:, 0, 0:512]
        er = PT[:, 0, 512:1024]
        rr = PT[:, 1, 0:512]
        fo = PT[:, 1, 512:1024]
        eg = sb("eg", [P, 32])
        rg = sb("rg", [P, 32])

        w12 = sb("w12", [P, 2, 512])
        w12s = sb("w12s", [P, 2, 512])
        alpha = sb("alpha", [P, FT + 1])
        l0.close()
        sb = persistent

        xn1 = sb("xn1", [P, B, D])
        x1T = sb("x1T", [P, 512])
        qkv_in = sb("qkv_in", [P, 3, B, 3 + P])
        cy = sb("cy", [P, 3, B, P])
        ce = sb("ce", [P, 3, B, P])
        tok = sb("tok", [P, 3, B, D])
        sq = sb("sq", [P, 2, B, D])
        ss = sb("ss", [P, 2, GH])
        rn = sb("rn", [P, 2, GH])
        rt = sb("rt", [P, 2, GH])
        qk_n = sb("qk_n", [P, 2, B, D])
        kqT = sb("kqT", [P, B, 2, P])
        ctl = sb("ctl", [P, B, CT])
        sg = sb("sg", [P, B, CT])
        al = sb("al", [P, B, H1])
        la_wide = sb("la_wide", [P, P])
        la = la_wide[:, 0:GH].rearrange("p (g h) -> p g h", g=B)
        ogr = sb("ogr", [P, 2, B, D])
        laG = sb("laG", [P, GH, SUB])
        laX = sb("laX", [P, B, D])
        ones = sb("ones", [P, SUB])
        gam = sb("gam", [P, GH, SUB])
        gam_b = sb("gam_b", [P, GH, SUB])
        gam_t = sb("gam_t", [P, GH, SUB])
        gam_m = laG
        dec = sb("dec", [P, 2, 48])
        bD = sb("bD", [P, GH])
        Lc = sb("Lc", [P, 2, GH, SUB])
        Pc = sb("Pc", [P, 2, GH, SUB])
        Bm = sb("Bm", [P, 4, GH, SUB])
        Bx = sb("Bx", [P, 2, GH, P])
        Tx = sb("Tx", [P, GH, P])
        Tc = sb("Tc", [P, GH, SUB])
        Zc = sb("Zc", [P, 2, GH, SUB])
        Yc = sb("Yc", [P, GH, SUB])
        Rv = sb("Rv", [P, 2, GH, 2 * SUB])
        Wv = sb("Wv", [P, GH, 2 * SUB])
        Px = sb("Px", [P, GH, P])
        Qd = sb("Qd", [P, 2, GH, SUB])
        Kd = sb("Kd", [P, 2, GH, SUB])
        Mo = sb("Mo", [P, GH, SUB])
        MoT = sb("MoT", [P, B, P])
        Ov = sb("Ov", [P, GH, SUB])
        Ac = sb("Ac", [P, NB, B, SUB])
        At = Yc[:, :, :].rearrange("p (q g) e -> p q g e", q=NB)
        Ax = sb("Ax", [P, NB, B, P])
        Bc = sb("Bc", [P, NB, B, SUB])
        St = sb("St", [P, NB + 1, B, SUB])
        rd = sb("rd", [P, GH, SUB])
        rsq = Ac[:, :, :, :].rearrange("p q g e -> p (q g) e")
        rss = sb("rss", [P, GH])
        rrs = sb("rrs", [P, GH])
        rrt = sb("rrt", [P, GH])
        rdn = sb("rdn", [P, B, D])
        rdT = sb("rdT", [P, B, P])
        hT = sb("hT", [P, FT, 512])
        acc = sb("acc", [P, 2, B, D])
        ao = rdn
        res = sb("res", [P, B, D])

        block = ctx.enter_context(nc.Block())

        @block.sync
        def _(sp):
            for b in range(B):
                sp.dma_start(X[:, b * NT:(b + 1) * NT, :], x_dram[:, b * NT:(b + 1) * NT, :]).then_inc(S("x_loaded"), 16)
            for i, name in enumerate(("W_r", "W_k", "W_v")):
                sp.dma_start(w3[:, i, :], A["L0_ffn_" + name]).then_inc(S("w3_loaded"), 16)
            sp.dma_start(mu[:, 0:1], A["L0_ffn_mu_r"].rearrange("(d a) -> d a", a=1)).then_inc(S("mu_loaded"), 16)
            sp.dma_start(mu[:, 2:3], A["L0_ffn_mu_k"].rearrange("(d a) -> d a", a=1)).then_inc(S("mu_loaded"), 16)
            sp.dma_start(rms_w[:, :], A["L0_attn_rms_w"].rearrange("(d a) -> d a", a=1)).then_inc(S("rms_loaded"), 16)
            sp.dma_start(wv_sb[:, :, :], A["L0_attn_wv"].rearrange("h d e -> d h e")).then_inc(S("wv_loaded"), 16)
            sp.dma_start(wg_sb[:, :], A["L0_attn_w_gates"]).then_inc(S("wv_loaded"), 16)
            sp.dma_start(wo_sb[:, :, :], A["L0_attn_wo"].rearrange("(a h) e d -> (h e) a d", h=2)).then_inc(S("wo_loaded"), 16)

            for name, dst in (("W_in", w_in), ("W_ctrl", w_ctrl), ("W_out", w_out)):
                sp.dma_start(dst[:, :], A["L1_attn_" + name]).then_inc(S("l1_loaded"), 16)
            for name, dst in (("L1_attn_b_ctrl", b_ctrl), ("L1_attn_b_out", b_out_sb), ("L1_attn_ramp_logit", ramp),
                              ("L1_ffn_b2", b2row)):
                sp.dma_start(dst[:, :], A[name].partition_broadcast(P)).then_inc(S("l1_loaded"), 16)
            sp.dma_start(masks[:, :], A["masks"]).then_inc(S("l1_loaded"), 16)
            for t in range(FT):
                sp.dma_start(b1col[:, t:t + 1], A["L1_ffn_b1"][t * P:(t + 1) * P].rearrange("(p a) -> p a", a=1)).then_inc(S("l1_loaded"), 16)
            for i, name in enumerate(("w_q", "w_k", "w_v")):
                sp.dma_start(conv_w[:, i, :], A["L1_attn_" + name].rearrange("d a k -> d (a k)")).then_inc(S("l1_loaded"), 16)
            sp.dma_start(w12[:, 0, :].rearrange("p (t d) -> p t d", t=FT),
                         A["L1_ffn_w1"].rearrange("(t p) d -> p t d", p=P)).then_inc(S("w12_loaded"), 16)
            sp.dma_start(w12[:, 1, :], A["L1_ffn_w2"]).then_inc(S("w12_loaded"), 16)

            def load_qk(p):
                sp.dma_start(wqk[:, 0, :].rearrange("d (h e) -> d h e", h=2),
                             A["L0_attn_wq"][ds(p * 2, 2)].rearrange("h d e -> d h e")).then_inc(S("wqk_loaded"), 16)
                sp.dma_start(wqk[:, 1, :].rearrange("d (h e) -> d h e", h=2),
                             A["L0_attn_wk"][ds(p * 2, 2)].rearrange("h d e -> d h e")).then_inc(S("wqk_loaded"), 16)

            load_qk(0)
            with sp.Fori(0, STEPS) as n:
                nxt = sp.snap(((n + 1) % PAIRS))
                sp.wait_ge(S("proj_done"), n + 1)
                load_qk(nxt)
            sp.wait_ge(S("wqk_loaded"), 32 * (STEPS + 1))
            with sp.Fori(0, NT) as s:
                sp.wait_ge(S("res_ready"), s + 1)
                sp.dma_start(out_dram.rearrange("p (g t) d -> p g t d", g=B)[:, :, ds(s, 1), :].rearrange("p g a d -> p g (a d)"),
                             res[:, :, :]).then_inc(S("stored"), 16)
            sp.wait_ge(S("stored"), 16 * (NT + 1))

        @block.gpsimd
        def _(g):
            g.memset(neg_half[:, :], -0.5).then_inc(S("half_set"), 1)
            g.memset(ident[:, :], 0.0).then_inc(S("ident_zero"), 1)
            g.memset(causal[:, :], 0.0).then_inc(S("ident_zero"), 1)
            g.memset(Qp[:, :, :], 0.0).then_inc(S("q_zero"), 1)
            g.memset(xT[:, 0, 0:1], 0.0).then_inc(S("halo_zero"), 1)
            g.wait_ge(S("ident_zero"), 2)
            g.affine_select(out=ident[:, :], in_=ident[:, :], compare_op=ALU.not_equal, fill=1.0,
                            base=0, pattern=[[-1, P]], channel_multiplier=1).then_inc(S("ident_set"), 1)
            g.affine_select(out=causal[:, :], in_=causal[:, :], compare_op=ALU.is_ge, fill=MASKED,
                            base=0, pattern=[[-1, P]], channel_multiplier=1).then_inc(S("causal_set"), 1)
            g.wait_ge(S("ident_set"), 1)
            g.tensor_copy(identb[:, :], ident[:, :]).then_inc(S("causal_set"), 1)
            g.wait_ge(S("mu_loaded"), 32)
            for c in (0, 2):
                g.tensor_scalar(mu[:, c + 1:c + 2], mu[:, c:c + 1], -1.0, 1.0, ALU.mult, ALU.add).then_inc(S("mu_set"), 1)
            g.wait_ge(S("mu_set"), 2)
            g.wait_ge(S("half_set"), 1)
            g.wait_ge(S("stats_done"), 1)
            g.tensor_scalar(ve[:, :], var[:, :], EPS_LN, None, ALU.add).then_inc(S("rstd_step"), 1)
            g.wait_ge(S("rstd_step"), 1)
            g.tensor_tensor(rstd[:, :], ve[:, :], neg_half[:, :], ALU.pow).then_inc(S("rstd_step"), 1)
            g.wait_ge(S("rstd_step"), 2)
            g.tensor_tensor(rms2[:, :], rstd[:, :], rstd[:, :], ALU.mult).then_inc(S("rstd_step"), 1)
            g.wait_ge(S("rstd_step"), 3)
            g.tensor_tensor(ve[:, :], rms2[:, :], var[:, :], ALU.mult).then_inc(S("rstd_step"), 1)
            g.wait_ge(S("rstd_step"), 4)
            g.tensor_scalar(rms2[:, :], ve[:, :], EPS_RMS, None, ALU.add).then_inc(S("rstd_step"), 1)
            g.wait_ge(S("rstd_step"), 5)
            g.tensor_tensor(rrms[:, :], rms2[:, :], neg_half[:, :], ALU.pow).then_inc(S("rstd_step"), 1)
            with g.Fori(0, B) as b:
                for qd in range(2):
                    w = b * 2 + (qd + 1)
                    g.wait_ge(S("xT_ready"), w)
                    g.tensor_tensor(tmr, xT[:, qd, 0:512], mu[:, 1:2].to_broadcast([P, 512]), ALU.mult)
                    g.tensor_tensor(tmk, xT[:, qd, 0:512], mu[:, 3:4].to_broadcast([P, 512]), ALU.mult).then_inc(S("shift_ready"), 1)
                    g.wait_ge(S("tS_ready"), w)
                    g.tensor_copy(TT[:, ds(b * N + qd * 512, 512)], tS).then_inc(S("TT_ready"), 1)
                    g.wait_ge(S("kr_ready"), w)
                    g.tensor_tensor(ka, kr, kr, ALU.mult).then_inc(S("ka_ready"), 1)

            g.wait_ge(S("sign_ready"), 3)
            g.wait_ge(S("alpha_ready"), 2)
            for t in range(FT):
                g.tensor_tensor(w12s[:, 0, t * D:(t + 1) * D], w12s[:, 0, t * D:(t + 1) * D],
                                alpha[:, t:t + 1].to_broadcast([P, D]), ALU.mult)
            g.tensor_tensor(w12s[:, 1, :], w12s[:, 1, :], alpha[:, FT:FT + 1].to_broadcast([P, FT * P]),
                            ALU.mult).then_inc(S("bin_step"), 1)
            g.wait_ge(S("bin_step"), 1)
            g.tensor_tensor(w12s[:, :, :], w12s[:, :, :], w12[:, :, :], ALU.subtract).then_inc(S("bin_step"), 1)
            g.wait_ge(S("bin_step"), 2)
            g.tensor_tensor(w12[:, :, :], w12[:, :, :], w12s[:, :, :], ALU.add).then_inc(S("bin_ready"), 1)

            g.wait_ge(S("x1_done"), 1 + STEPS)
            g.wait_ge(S("bin_turned"), 2)
            g.wait_ge(S("ramp_ready"), 1)
            g.memset(la_wide[:, :], 0.0).then_inc(S("out_read"), 1)
            g.memset(ones[:, :], 1.0)
            g.memset(qkv_in[:, :, :, :], 0.0)
            g.memset(Bx[:, :, :, :], 0.0)
            g.memset(Tx[:, :, :], 0.0)
            g.memset(Px[:, :, :], 0.0)
            g.memset(Ax[:, :, :, :], 0.0)
            g.memset(St[:, :, :, :], 0.0)
            g.memset(res[:, :, :], 0.0).then_inc(S("stored"), 16)
            g.memset(gam_t[:, :, :], 0.0).then_inc(S("l1_zero"), 1)
            g.wait_ge(S("l1_zero"), 1)
            g.wait_ge(S("stats_done"), 2)
            g.tensor_scalar(ve[:, :], var[:, :], EPS_LN, None, ALU.add).then_inc(S("rstd_step"), 1)
            g.wait_ge(S("rstd_step"), 7)
            g.tensor_tensor(rstd[:, :], ve[:, :], neg_half[:, :], ALU.pow).then_inc(S("rstd_step"), 1)

            def tt(out, a, b, op, done=None):
                ins = g.tensor_tensor(out, a, b, op)
                if done:
                    ins.then_inc(S(done), 1)

            def over(ap, shape, at):
                return ap.unsqueeze(at).to_broadcast(shape)

            G3 = [P, GH, SUB]
            G4 = [P, B, H1, SUB]

            def front_gates(s, p):
                for i in range(3):
                    g.wait_ge(S(f"ce{i}_s"), count(f"ce{i}_s", s))
                    tt(cy[:, i, :, :], cy[:, i, :, :], ce[:, i, :, :], ALU.mult, f"silu{i}_ready")
                bt = sg[:, :, H1:2 * H1]
                tt(gam_b[:, :, :].rearrange("p (g h) j -> p g h j", g=B), over(bt, G4, 3),
                   below.unsqueeze(1).unsqueeze(1).to_broadcast(G4), ALU.mult, "bm_ready")
                tt(ogr[:, p, :, :], sg[:, :, 2 * H1:], over(ramp[:, :], [P, B, D], 1), ALU.mult, "ogr_ready")
                g.wait_ge(S("tok_ready"), count("tok_ready", s))
                R4 = Rv[:, p, :, :].rearrange("p (g h) j -> p g h j", g=B)
                tt(R4[:, :, :, 0:SUB], tok[:, 2, :, :].rearrange("p g (h e) -> p g h e", h=H1), over(bt, G4, 3), ALU.mult)
                g.wait_ge(S("la_ready"), count("la_ready", s))
                tt(laG[:, :, :], over(la.rearrange("p g h -> p (g h)"), G3, 2), over(below, G3, 1), ALU.mult, "laG_ready")
                tt(laX[:, :, :].rearrange("p g (h e) -> p g h e", h=H1), over(la, G4, 3),
                   ones[:, :].unsqueeze(1).unsqueeze(1).to_broadcast(G4), ALU.mult, "laX_ready")

            def front_decays(s, p):
                bt = sg[:, :, H1:2 * H1]
                g.wait_ge(S("gam_ready"), count("gam_ready", s))
                g.wait_ge(S("bm_ready"), count("bm_ready", s))
                tt(gam_m[:, :, :], gam[:, :, :], over(upto_c, G3, 1), ALU.mult, "gam_m_ready")
                tt(gam_b[:, :, :], gam_b[:, :, :], gam[:, :, :], ALU.mult, "gam_b_ready")
                g.wait_ge(S("dec_ready"), count("dec_ready", s))
                tt(bD[:, :].rearrange("p (g h) -> p g h", g=B), bt, dec[:, p, 0:16].rearrange("p (g h) -> p g h", g=B), ALU.mult, "bD_ready")
                g.wait_ge(S("kn_ready"), count("kn_ready", s))
                g.wait_ge(S("bD_ready"), count("bD_ready", s))
                kn = qk_n[:, 1, :, :].rearrange("p g (h e) -> p (g h) e", h=H1)
                qn = qk_n[:, 0, :, :].rearrange("p g (h e) -> p (g h) e", h=H1)
                tt(Rv[:, p, :, SUB:], kn, over(bD[:, :], G3, 2), ALU.mult, "Rv_ready")
                tt(Qd[:, p, :, :], qn, over(dec[:, p, 0:16], G3, 2), ALU.mult, "Qd_ready")
                tt(Kd[:, p, :, :], kn, over(dec[:, p, 16:32], G3, 2), ALU.mult, "Kd_ready")

            def back_joins(s, p):
                g.wait_ge(S("Lc_ready"), count("Lc_ready", s))
                for k in range(4):
                    tt(Bm[:, k, :, :], Lc[:, p, :, :], over(merge[:, k + 1, :], G3, 1), ALU.mult, f"Bm{k}_ready")

            def front(s, p):
                front_gates(s, p)
                front_decays(s, p)
                back_joins(s, p)

            front(0, 0)
            with g.Fori(0, NT // 2 - 1) as i:
                front(i * 2 + 1, 1)
                front(i * 2 + 2, 0)
            front(NT - 1, 1)

        @block.scalar
        def _(act):
            act.wait_ge(S("w3_turned"), 1)
            act.activation(w3T[:, :, :], bank(0)[:, 0:384].rearrange("p (i d) -> p i d", i=3), ACT.Copy).then_inc(S("w3T_ready"), 1)
            act.wait_ge(S("w12_loaded"), 32)
            act.wait_ge(S("l1_loaded"), 16 * 15)
            act.activation(w12s[:, 0, :], w12[:, 0, :], ACT.Sign).then_inc(S("sign_ready"), 1)
            act.activation(w12s[:, 1, :], w12[:, 1, :], ACT.Sign).then_inc(S("sign_ready"), 1)
            act.activation(ramp[:, :], ramp[:, :], ACT.Exp, scale=-1.0).then_inc(S("sign_ready"), 1)
            act.wait_ge(S("halo_zero"), 1)
            with act.Fori(0, B) as b:
                for qd in range(2):
                    w = b * 2 + (qd + 1)
                    act.wait_ge(S("xn_turned"), w)
                    if qd == 1:
                        act.wait_ge(S("xT_ready"), w - 1)
                        act.activation(xT[:, 1, 0:1], xT[:, 0, 512:513], ACT.Copy)
                    act.activation(xT[:, qd, 1:513], bank(0), ACT.Copy).then_inc(S("xT_ready"), 1)
                    act.wait_ge(S("z_ready"), (b * 2 + qd) * 2 + 1)
                    act.activation(eg[:, :], eg[:, :], ACT.Exp, scale=-1.0).then_inc(S("eg_ready"), 1)
                    act.wait_ge(S("k_done"), w)
                    act.activation(kr, bank(2), ACT.Relu).then_inc(S("kr_ready"), 1)
                    act.wait_ge(S("z_ready"), (b * 2 + qd) * 2 + 2)
                    act.activation(er, er, ACT.Exp, scale=-1.0).then_inc(S("er_ready"), 1)
                    for t in range(4):
                        act.wait_ge(S("v_done"), (b * 2 + qd) * 4 + (t + 1))
                        act.activation(V[:, ds((b * 2 + qd) * 4 + t, 1), :].rearrange("p a n -> p (a n)"),
                                       bank(6 + t % 2), ACT.Copy).then_inc(S("V_ready"), 1)

            def qk_evac(nth):
                act.wait_ge(S("proj_done"), nth)
                act.activation(Qp[0:64, 0, :], bank(0, 2)[0:64, :], ACT.Copy, scale=SCALE)
                act.activation(Qp[64:128, 1, :], bank(0, 2)[64:128, :], ACT.Copy, scale=SCALE).then_inc(S("qk_act"), 1)

            act.wait_ge(S("q_zero"), 1)
            qk_evac(1)
            with act.Fori(0, STEPS) as n:
                for k in range(UNITS + 2):
                    if k < UNITS:
                        W = (k // 2 + 1) * P
                        if k >= 4:
                            act.wait_ge(S("PT_turned"), n * UNITS + (k - 3))
                        act.wait_ge(S("max_ready"), n * UNITS + (k + 1))
                        act.activation(Pbuf[:, k % 4, 0:W], bank(2 * (k % 2), 2)[:, 0:W], ACT.Exp,
                                       bias=nb[:, k:k + 1], accum_out=rs[:, k:k + 1]).then_inc(S("exp_done"), 1)
                    if k >= 2 and (k - 2) // 2 >= 4:
                        u = k - 2
                        W = (u // 2 + 1) * P
                        act.wait_ge(S("PT_turned"), n * UNITS + (u + 1))
                        act.wait_ge(S("pv_done"), n * UNITS + (u - 1))
                        act.activation(PT[:, u % 2, 512:W], bank(5)[:, 0:W - 512], ACT.Copy).then_inc(S("PT_hi"), 1)
                    if k in (10, UNITS + 1):
                        half = int(k != 10)
                        act.wait_ge(S("R_turned"), n * 2 + (half + 1))
                        act.activation(R[:, half, :], bank(7 - half), ACT.Copy).then_inc(S("R_ready"), 1)
                qk_evac(n + 2)

            act.wait_ge(S("x1_done"), 1 + STEPS)
            act.wait_ge(S("l1_zero"), 1)

            def cp(s, out, src, done, after=None, func=ACT.Copy, **kw):
                if after:
                    act.wait_ge(S(after), count(after, s))
                ins = act.activation(out, src, func, **kw)
                if done:
                    ins.then_inc(S(done), 1)

            def spread(s, dst, src, done, after):
                act.wait_ge(S(after), count(after, s))
                for q in range(NB):
                    r = slice(q * SUB, (q + 1) * SUB)
                    ins = act.activation(dst[r, :, q * SUB:(q + 1) * SUB], src[r, :, :], ACT.Copy)
                ins.then_inc(S(done), 1)

            def f_x1T(s):
                cp(s, x1T[:, :], bank(0), "x1T_ready", "xn1_turned")
                act.activation(qkv_in[:, :, :, 0:3].rearrange("p i g k -> p (i g) k"),
                               qkv_in[:, :, :, P:P + 3].rearrange("p i g k -> p (i g) k"), ACT.Copy).then_inc(S("halo_ready"), 1)

            def f_qkv(s):
                act.wait_ge(S("halo_ready"), count("halo_ready", s))
                for i in range(3):
                    act.wait_ge(S(f"qkv{i}_done"), count(f"qkv{i}_done", s))
                    act.activation(cy[:, i, :, :], bank(1 + i).rearrange("p (g t) -> p g t", g=B), ACT.Copy,
                                   scale=conv_w[:, i, 3:4])
                    act.activation(qkv_in[:, i, :, 3:], bank(1 + i).rearrange("p (g t) -> p g t", g=B),
                                   ACT.Copy).then_inc(S(f"qkv{i}_ready"), 1)

            def f_sigmoid_e(s):
                cp(s, sg[:, :, :], ctl[:, :, :], "sg_e", "ctl_ready", ACT.Exp, scale=-1.0)
                for i in range(3):
                    cp(s, ce[:, i, :, :], ce[:, i, :, :], f"ce{i}_e", f"conv{i}_done", ACT.Exp, scale=-1.0)

            def f_sigmoid_l(s):
                cp(s, ctl[:, :, :], sg[:, :, :], "sg_l", "sg_e", ACT.Ln, bias=1.0)
                for i in range(3):
                    cp(s, ce[:, i, :, :], ce[:, i, :, :], f"ce{i}_l", f"ce{i}_e", ACT.Ln, bias=1.0)

            def f_sigmoid_s(s):
                cp(s, sg[:, :, :], ctl[:, :, :], "sg_ready", "sg_l", ACT.Exp, scale=-1.0)
                for i in range(3):
                    cp(s, ce[:, i, :, :], ce[:, i, :, :], f"ce{i}_s", f"ce{i}_l", ACT.Exp, scale=-1.0)

            def f_decay(s, p):
                cp(s, gam[:, :, :].rearrange("p g j -> p (g j)"), bank(0), "gam_ready", "gam_summed", ACT.Exp)
                cp(s, dec[:, p, :], bank(1)[:, 0:48], "dec_ready", "dec_summed", ACT.Exp)

            def f_hidden(s):
                for t in range(FT):
                    cp(s, hT[:, t, :], bank(2 + t % 2), f"h{t}_ready", f"ffn{t}_done", ACT.Gelu, bias=b1col[:, t:t + 1])

            def f_logs(s):
                cp(s, la, al[:, :, :], "la_ready", "al_ready", ACT.Ln)
                cp(s, rt[:, :, :], ss[:, :, :], "rn_l", "ss_ready", ACT.Ln)
                cp(s, rn[:, :, :], rt[:, :, :], "rn_e", "rn_l", ACT.Exp, scale=-0.5)

            def f_keys(s):
                cp(s, kqT[:, :, 0, :], bank(0).rearrange("p (g t) -> p g t", g=B), "kT_ready", "kn_turned")
                cp(s, kqT[:, :, 1, :], bank(1).rearrange("p (g t) -> p g t", g=B), "qT_ready", "qn_turned")

            def b_first(s, p):
                spread(s, Bx[:, 0, :, :], Bm[:, 0, :, :], "Bx0_ready", "Bm0_ready")

            def b_join(s, k):
                cp(s, Yc[:, :, :].rearrange("p g j -> p (g j)"), bank(4), f"Y{k}_ready", f"Y{k}_done")
                if k < 3:
                    spread(s, Bx[:, (k + 1) % 2, :, :], Bm[:, k + 1, :, :], f"Bx{k + 1}_ready", f"Bm{k + 1}_ready")

            def b_w(s):
                cp(s, Wv[:, :, :].rearrange("p g j -> p (g j)"), bank(6, 2), "Wv_ready", "W_done")

            def b_mo(s):
                cp(s, MoT[:, :, :].rearrange("p g t -> p (g t)"), bank(6), "MoT_ready", "Mo_turned")

            def b_maps(s):
                act.wait_ge(S("Ac_ready"), count("Ac_ready", s))
                for h in range(H1):
                    r = slice(h * E1, (h + 1) * E1)
                    ins = act.activation(Ax[r, :, :, h * E1:(h + 1) * E1].rearrange("p q g e -> p (q g) e"),
                                         Ac[r, :, :, :].rearrange("p q g e -> p (q g) e"), ACT.Copy)
                ins.then_inc(S("Ax_ready"), 1)

            def round_of(s, p, ahead):
                spread(s, Px[:, :, :], Pc[:, p, :, :], "Px_ready", "Pc_ready")
                if ahead:
                    f_x1T(s + 1)
                b_join(s, 1)
                if ahead:
                    f_qkv(s + 1)
                b_join(s, 2)
                if ahead:
                    f_sigmoid_e(s + 1)
                b_join(s, 3)
                if ahead:
                    f_sigmoid_l(s + 1)
                    f_sigmoid_s(s + 1)
                b_w(s)
                if ahead:
                    f_hidden(s + 1)
                b_mo(s)
                if ahead:
                    f_logs(s + 1)
                    f_decay(s + 1, 1 - p)
                    f_keys(s + 1)
                b_maps(s)
                if ahead:
                    b_first(s + 1, 1 - p)
                cp(s, rrt[:, :], rss[:, :], "rrs_l", "rss_ready", ACT.Ln)
                if ahead:
                    cp(s + 1, Yc[:, :, :].rearrange("p g j -> p (g j)"), bank(4), "Y0_ready", "Y0_done")
                cp(s, rrs[:, :], rrt[:, :], "rrs_e", "rrs_l", ACT.Exp, scale=-0.5)
                if ahead:
                    spread(s + 1, Bx[:, 1, :, :], Bm[:, 1, :, :], "Bx1_ready", "Bm1_ready")
                cp(s, rdT[:, :, :].rearrange("p g t -> p (g t)"), bank(6), "rdT_ready", "rd_turned")

            f_x1T(0)
            f_qkv(0)
            f_sigmoid_e(0)
            f_sigmoid_l(0)
            f_sigmoid_s(0)
            f_hidden(0)
            f_logs(0)
            f_decay(0, 0)
            f_keys(0)
            b_first(0, 0)
            b_join(0, 0)
            with act.Fori(0, NT // 2 - 1) as i:
                round_of(i * 2, 0, True)
                round_of(i * 2 + 1, 1, True)
            round_of(NT - 2, 0, True)
            round_of(NT - 1, 1, False)

        @block.tensor
        def _(pe):
            pe.wait_ge(S("ident_set"), 1)
            pe.wait_ge(S("w3_loaded"), 48)
            for i in range(3):
                ins = pe.transpose(bank(0)[:, i * P:(i + 1) * P], w3[:, i, :], ident[:, :])
            ins.then_inc(S("w3_turned"), 1)
            pe.wait_ge(S("wv_loaded"), 32)
            pe.wait_ge(S("w3T_ready"), 1)
            with pe.Fori(0, B) as b:
                for qd in range(2):
                    w = b * 2 + (qd + 1)
                    pe.wait_ge(S("xn_ready"), w)
                    for t in range(4):
                        ins = pe.transpose(bank(0)[:, t * P:(t + 1) * P], xn[:, t, :], ident[:, :])
                    ins.then_inc(S("xn_turned"), 1)
                    pe.wait_ge(S("tn_ready"), w)
                    for t in range(4):
                        ins = pe.transpose(bank(1)[:, t * P:(t + 1) * P], tn[:, t, :], ident[:, :])
                    ins.then_inc(S("tn_turned"), 1)
                    pe.wait_ge(S("tS_ready"), w)
                    for t in range(4):
                        ins = pe.matmul(bank(5)[:, t * H:(t + 1) * H], tS[:, t * P:(t + 1) * P], wg_sb[:, :],
                                        start=True, stop=True)
                    ins.then_inc(S("gates_done"), 1)
                    pe.wait_ge(S("xrk_ready"), w)
                    pe.matmul(bank(2), w3T[:, 1, :], xk, start=True, stop=True).then_inc(S("k_done"), 1)
                    for t in range(4):
                        ins = pe.matmul(bank(3)[:, t * P:(t + 1) * P], xr[:, t * P:(t + 1) * P], w3T[:, 0, :],
                                        start=True, stop=True)
                    ins.then_inc(S("r_done"), 1)
                    for t in range(4):
                        pe.wait_ge(S("V_credit"), 1)
                        if t >= 2:
                            pe.wait_ge(S("V_ready"), (b * 2 + qd) * 4 + (t - 1))
                        pe.matmul(bank(6 + t % 2), tS[:, t * P:(t + 1) * P],
                                  wv_sb[:, :, :].rearrange("p h e -> p (h e)"), start=True, stop=True).then_inc(S("v_done"), 1)
                    pe.wait_ge(S("ka_ready"), w)
                    for t in range(4):
                        ins = pe.matmul(bank(4)[:, t * P:(t + 1) * P], ka[:, t * P:(t + 1) * P], w3T[:, 2, :],
                                        start=True, stop=True)
                    ins.then_inc(S("v2_done"), 1)

            def project(i, c_first):
                b_next = i // PAIRS
                for c in range(2):
                    ins = pe.matmul(bank(2 * c_first + c), wqk[:, c_first, :],
                                    TT[:, ds(b_next * N + c * 512, 512)], start=True, stop=True)
                return ins

            pe.wait_ge(S("V_ready"), TILES)
            pe.wait_ge(S("TT_ready"), QUADS)
            pe.wait_ge(S("x_ffn"), QUADS)
            pe.wait_ge(S("causal_set"), 2)
            pe.wait_ge(S("wo_loaded"), 16)
            pe.wait_ge(S("wqk_loaded"), 32)
            for c in (0, 1):
                for j in range(2):
                    ins = pe.matmul(bank(2 * c + j), wqk[:, c, :], TT[:, j * 512:(j + 1) * 512], start=True, stop=True)
            ins.then_inc(S("proj_done"), 1)
            with pe.Fori(0, STEPS) as n:
                nxt = pe.snap((n + 1) % STEPS)
                pr = pe.snap(n % PAIRS)
                for k in range(UNITS + 3):
                    if k < UNITS:
                        ib, hh = divmod(k, 2)
                        if k == 0:
                            pe.wait_ge(S("qk_act"), n + 1)
                            pe.wait_ge(S("qk_dve"), n + 1)
                        if k >= 2:
                            pe.wait_ge(S("exp_done"), n * UNITS + (k - 1))
                        for c in range(ib // 4 + 1):
                            w = min(512, (ib + 1) * P - c * 512)
                            last = c == ib // 4
                            ins = pe.matmul(bank(2 * (k % 2) + c)[:, 0:w], Qp[:, hh, ib * P:(ib + 1) * P],
                                            K[:, c * 512:c * 512 + w], start=True, stop=not last)
                        d0 = (ib % 4) * P
                        ins = pe.matmul(bank(2 * (k % 2) + ib // 4)[:, d0:d0 + P], identb[:, :], causal[:, :],
                                        start=False, stop=True)
                        ins.then_inc(S("scores_done"), 1)
                    if k == UNITS:
                        pe.wait_ge(S("wqk_loaded"), n * 32 + 64)
                        pe.wait_ge(S("exp_done"), n * UNITS + (UNITS - 1))
                        project(nxt, 0)
                    if 2 <= k < UNITS + 2:
                        u = k - 2
                        if u == 0:
                            pe.wait_ge(S("x1_done"), n + 1)
                        else:
                            pe.wait_ge(S("PT_lo"), n * UNITS + u)
                            if u - 1 >= 8:
                                pe.wait_ge(S("PT_hi"), n * 8 + (u - 8))
                        pe.wait_ge(S("exp_done"), n * UNITS + (u + 1))
                        for j in range(u // 2 + 1):
                            ins = pe.transpose(bank(4 + j // 4)[:, (j % 4) * P:(j % 4 + 1) * P],
                                               Pbuf[:, u % 4, j * P:(j + 1) * P], ident[:, :])
                        ins.then_inc(S("PT_turned"), 1)
                    if k == UNITS + 1:
                        project(nxt, 1).then_inc(S("proj_done"), 1)
                    if k in (10, UNITS + 1):
                        half = int(k != 10)
                        pe.wait_ge(S("Sx_ready"), n * 2 + (half + 1))
                        if half:
                            pe.wait_ge(S("OT_ready"), n * 2 + 1)
                        for t in range(4):
                            ins = pe.transpose(bank(7 - half)[:, t * P:(t + 1) * P],
                                               Sx[:, t, :, :].rearrange("p h e -> p (h e)"), ident[:, :])
                        ins.then_inc(S("R_turned"), 1)
                    if 3 <= k:
                        u = k - 3
                        ib, hh = divmod(u, 2)
                        pe.wait_ge(S("causal_set"), 2)
                        if u == 0:
                            pe.wait_ge(S("Vp_ready"), n + 1)
                        if u == 8:
                            pe.wait_ge(S("R_ready"), n * 2 + 1)
                        pe.wait_ge(S("PT_lo"), n * UNITS + (u + 1))
                        if u >= 8:
                            pe.wait_ge(S("PT_hi"), n * 8 + (u - 7))
                        for j in range(ib + 1):
                            ins = pe.matmul(bank(6 + ib // 4)[64 * hh:64 * hh + 64, (ib % 4) * P:(ib % 4 + 1) * P],
                                            Vp[:, j, 64 * hh:64 * hh + 64], PT[:, u % 2, j * P:(j + 1) * P],
                                            start=(j == 0), stop=(j == ib))
                        ins.then_inc(S("pv_done"), 1)
                for ib in range(NT):
                    if ib % 4 == 0:
                        pe.wait_ge(S("OT_ready"), n * 2 + (ib // 4 + 1))
                    ins = pe.matmul(bank(4 + ib // 4)[:, (ib % 4) * P:(ib % 4 + 1) * P], OT[:, ib * P:(ib + 1) * P],
                                    wo_sb[:, ds(pr, 1), :].rearrange("p a d -> p (a d)"), start=True, stop=True)
                ins.then_inc(S("wo_done"), 1)

            pe.wait_ge(S("x1_done"), 1 + STEPS)
            pe.wait_ge(S("bin_ready"), 1)
            pe.wait_ge(S("qk_act"), STEPS + 1)
            pe.wait_ge(S("qk_dve"), STEPS + 1)
            for i in range(2):
                for t in range(FT):
                    ins = pe.transpose(bank(i)[:, t * P:(t + 1) * P], w12[:, i, t * P:(t + 1) * P], ident[:, :])
            ins.then_inc(S("bin_done"), 1)
            pe.wait_ge(S("l1_loaded"), 16 * 15)
            pe.wait_ge(S("bin_turned"), 2)
            pe.wait_ge(S("l1_zero"), 1)

            def wait(s, *names):
                for name in names:
                    pe.wait_ge(S(name), count(name, s))

            def wait_small(s, *names):
                pe.wait_ge(S("l1_zero"), 1)
                wait(s, *names)

            def f_xn(s):
                wait(s, "xn1_ready")
                for g in range(B):
                    ins = pe.transpose(bank(0)[:, g * P:(g + 1) * P], xn1[:, g, :], ident[:, :])
                ins.then_inc(S("xn1_turned"), 1)

            def f_qkv(s):
                wait(s, "x1T_ready")
                for i in range(3):
                    pe.matmul(bank(1 + i), w_in[:, i * D:(i + 1) * D], x1T[:, :], start=True, stop=True).then_inc(S(f"qkv{i}_done"), 1)

            def f_control(s):
                wait(s, "qkv0_ready")
                for g in range(B):
                    ins = pe.matmul(bank(g // 2)[:, (g % 2) * CT:(g % 2 + 1) * CT], x1T[:, g * P:(g + 1) * P],
                                    w_ctrl[:, :], start=True, stop=True)
                ins.then_inc(S("ctrl_done"), 1)

            def f_hidden(s, t):
                wait(s, f"qkv{t + 1}_ready" if t < 2 else f"h{t - 2}_ready")
                if t == 3:
                    wait(s, "tok_ready")
                pe.matmul(bank(2 + t % 2), w1T[:, t * P:(t + 1) * P], x1T[:, :], start=True, stop=True).then_inc(S(f"ffn{t}_done"), 1)

            def f_decay(s):
                wait(s, "laG_ready", "tok_ready")
                pe.matmul(bank(0), upto, laG[:, :, :].rearrange("p g j -> p (g j)"), start=True, stop=True).then_inc(S("gam_summed"), 1)
                pe.matmul(bank(1)[:, 0:P], upto, la_wide[:, :], start=True, stop=True)
                pe.matmul(bank(1)[:, 16:16 + P], beyond, la_wide[:, :], start=True, stop=True)
                wait(s, "laX_ready")
                for g in range(B):
                    ins = pe.matmul(bank(1)[:, 32 + g * NB:32 + g * NB + P], laX[:, g, :], masks[:, 2 * P:3 * P],
                                    start=True, stop=True)
                ins.then_inc(S("dec_summed"), 1)

            def f_tokens(s):
                for i, after in enumerate(("ctl_raw", "ctl_raw", "h1_ready")):
                    wait(s, f"silu{i}_ready", after)
                    for g in range(B):
                        ins = pe.transpose(bank(i + i // 2)[:, g * P:(g + 1) * P], cy[:, i, g, :], ident[:, :])
                    ins.then_inc(S(f"tok{i}_turned"), 1)

            def f_ffn_out(s):
                wait(s, "h3_ready")
                for g in range(B):
                    for t in range(FT):
                        ins = pe.matmul(bank(2)[:, g * P:(g + 1) * P], hT[:, t, g * P:(g + 1) * P], w2T[:, t, :],
                                        start=(t == 0), stop=(t == FT - 1))
                ins.then_inc(S("ffn_out"), 1)

            def f_keys(s):
                wait(s, "kn_ready", "gam_ready", "dec_ready")
                for i, name in ((1, "kn_turned"), (0, "qn_turned")):
                    for g in range(B):
                        ins = pe.transpose(bank(1 - i)[:, g * P:(g + 1) * P], qk_n[:, i, g, :], ident[:, :])
                    ins.then_inc(S(name), 1)

            def f_kk(s, g):
                if g == 0:
                    wait_small(s, "kT_ready", "qT_ready", "tok_ready", "acc_ready")
                for q in range(NB):
                    for h in range(H1):
                        r, c = slice(h * E1, (h + 1) * E1), slice(q * SUB, (q + 1) * SUB)
                        ins = pe.matmul(bank(h)[c, g * 64:(g + 1) * 64].rearrange("p (a j) -> p a j", a=2),
                                        kqT[r, g, 0, c], kqT[r, g, :, c], start=True, stop=True)
                if g == B - 1:
                    ins.then_inc(S("kk_done"), 1)

            def systems(first, lhs, rhs, n):
                per = 512 // n
                flat = rhs.rearrange("p i j -> p (i j)")
                for i in range(GH):
                    m = min(P, (per - i % per) * n)
                    c = (i % per) * n
                    ins = pe.matmul(bank(first + i // per)[:, c:c + m], lhs[:, i, :], flat[:, i * n:i * n + m],
                                    start=True, stop=True)
                return ins

            def b_first(s, opened):
                if opened:
                    wait(s - 1, "rd_ready")
                b_y(s, 0)
                b_zy(s, 0)

            def b_y(s, k):
                wait(s, f"Bx{k}_ready", f"Z{k}_ready")
                systems(4, Bx[:, k % 2, :, :], Zc[:, k % 2, :, :], SUB).then_inc(S(f"Y{k}_done"), 1)

            def b_zy(s, k):
                wait(s, f"Y{k}_ready", f"Tx{k}_ready")
                systems(5, Tx[:, :, :], Yc[:, :, :], SUB).then_inc(S(f"ZY{k}_done"), 1)

            def b_w(s, p):
                wait(s, "Tx4_ready", "Rv_ready")
                systems(6, Tx[:, :, :], Rv[:, p, :, :], 64).then_inc(S("W_done"), 1)

            def b_pw(s):
                wait(s, "Wv_ready", "Px_ready")
                systems(4, Px[:, :, :], Wv[:, :, :], 64).then_inc(S("PW_done"), 1)

            def b_mo(s):
                wait(s, "Mo_ready")
                for g in range(B):
                    ins = pe.transpose(bank(6)[:, g * P:(g + 1) * P], Mo[:, g * H1:(g + 1) * H1, :].rearrange("p h e -> p (h e)"), ident[:, :])
                ins.then_inc(S("Mo_turned"), 1)

            def b_ab(s, p):
                wait_small(s, "Kd_ready", "Wv_ready", "MoT_ready", "Ov_ready")
                for g in range(B):
                    for h in range(H1):
                        for q in range(NB):
                            r, c = slice(q * SUB, (q + 1) * SUB), slice(h * E1, (h + 1) * E1)
                            ins = pe.matmul(bank(4 + q)[c, g * 64:(g + 1) * 64], Kd[r, p, g * H1 + h, :], Wv[r, g * H1 + h, :],
                                            start=True, stop=True)
                ins.then_inc(S("AB_done"), 1)

            def b_state(s, q):
                if q == 0:
                    wait(s, "Ax_ready", "Bc_ready")
                wait(s, f"St{q}_ready")
                flat = St[:, :, :, :].rearrange("p q g j -> p (q g j)")
                for g in range(B):
                    at = (q * B + g) * SUB
                    ins = pe.matmul(bank(4)[:, g * SUB:g * SUB + P], Ax[:, q, g, :], flat[:, at:at + P], start=True, stop=True)
                ins.then_inc(S(f"AS{q}_done"), 1)

            def b_ms(s):
                wait_small(s, "MoT_ready", "St4_ready")
                for g in range(B):
                    for q in range(NB):
                        for h in range(H1):
                            r, c = slice(h * E1, (h + 1) * E1), slice(q * SUB, (q + 1) * SUB)
                            ins = pe.matmul(bank(4 + h)[c, g * SUB:(g + 1) * SUB], MoT[r, g, c], St[r, q, g, :],
                                            start=True, stop=True)
                ins.then_inc(S("MS_done"), 1)

            def b_out(s):
                wait(s, "rdn_ready")
                for g in range(B):
                    ins = pe.transpose(bank(6)[:, g * P:(g + 1) * P], rdn[:, g, :], ident[:, :])
                ins.then_inc(S("rd_turned"), 1)
                wait(s, "rdT_ready")
                for g in range(B):
                    ins = pe.matmul(bank(7)[:, g * P:(g + 1) * P], rdT[:, g, :], w_out[:, :], start=True, stop=True)
                ins.then_inc(S("out_done"), 1)

            def round_of(s, p, ahead):
                if ahead:
                    f_xn(s + 1)
                b_y(s, 1)
                if ahead:
                    f_qkv(s + 1)
                b_zy(s, 1)
                if ahead:
                    f_control(s + 1)
                    f_hidden(s + 1, 0)
                b_y(s, 2)
                if ahead:
                    f_hidden(s + 1, 1)
                b_zy(s, 2)
                b_y(s, 3)
                b_zy(s, 3)
                b_w(s, p)
                if ahead:
                    f_tokens(s + 1)
                b_pw(s)
                if ahead:
                    f_hidden(s + 1, 2)
                    f_hidden(s + 1, 3)
                b_mo(s)
                if ahead:
                    f_ffn_out(s + 1)
                b_ab(s, p)
                if ahead:
                    f_decay(s + 1)
                    f_keys(s + 1)
                    f_kk(s + 1, 0)
                for q in range(NB):
                    b_state(s, q)
                    if ahead and q < NB - 1:
                        f_kk(s + 1, q + 1)
                b_ms(s)
                if ahead:
                    b_first(s + 1, True)
                b_out(s)

            f_xn(0)
            f_qkv(0)
            f_control(0)
            f_hidden(0, 0)
            f_hidden(0, 1)
            f_tokens(0)
            f_hidden(0, 2)
            f_hidden(0, 3)
            f_ffn_out(0)
            f_decay(0)
            f_keys(0)
            for g in range(B):
                f_kk(0, g)
            b_first(0, False)
            with pe.Fori(0, NT // 2 - 1) as i:
                round_of(i * 2, 0, True)
                round_of(i * 2 + 1, 1, True)
            round_of(NT - 2, 0, True)
            round_of(NT - 1, 1, False)

        @block.vector
        def _(v):
            def row_moments(name, raw="stats_raw"):
                even, odd = stats[:, :, 1], stats[:, :, 4]
                v.wait_ge(S(raw), QUADS)
                v.tensor_tensor(mean[:, :], even, odd, ALU.add).then_inc(S(name), 1)
                v.tensor_tensor(ve[:, :], even, odd, ALU.subtract).then_inc(S(name), 1)
                v.tensor_tensor(rms2[:, :], stats[:, :, 2], stats[:, :, 5], ALU.add).then_inc(S(name), 1)
                v.wait_ge(S(name), 2)
                v.tensor_scalar(mean[:, :], mean[:, :], 0.5, None, ALU.mult)
                v.scalar_tensor_tensor(ve[:, :], ve[:, :], 0.25, ve[:, :], ALU.mult, ALU.mult).then_inc(S(name), 1)
                v.wait_ge(S(name), 4)
                v.scalar_tensor_tensor(var[:, :], rms2[:, :], 1.0 / D, ve[:, :], ALU.mult, ALU.add).then_inc(S("stats_done"), 1)

            v.wait_ge(S("w12_loaded"), 32)
            v.tensor_reduce(alpha[:, 0:FT], w12[:, 0, :].rearrange("p (t d) -> p t d", t=FT), AX.X, ALU.add,
                            apply_absolute_value=True)
            v.tensor_reduce(alpha[:, FT:FT + 1], w12[:, 1, :], AX.X, ALU.add, apply_absolute_value=True).then_inc(S("alpha_sum"), 1)
            v.wait_ge(S("alpha_sum"), 1)
            v.tensor_scalar(alpha[:, 0:FT], alpha[:, 0:FT], 1.0 / D, None, ALU.mult).then_inc(S("alpha_ready"), 1)
            v.tensor_scalar(alpha[:, FT:FT + 1], alpha[:, FT:FT + 1], 1.0 / (FT * P), None, ALU.mult).then_inc(S("alpha_ready"), 1)
            v.wait_ge(S("sign_ready"), 3)
            v.tensor_scalar(ramp[:, :], ramp[:, :], 1.0, None, ALU.add).then_inc(S("ramp_step"), 1)
            v.wait_ge(S("ramp_step"), 1)
            v.reciprocal(ramp[:, :], ramp[:, :]).then_inc(S("ramp_ready"), 1)
            v.wait_ge(S("x_loaded"), 16 * B)
            with v.Fori(0, QUADS) as q:
                for t in range(4):
                    ins = v.bn_stats(stats[:, ds(q * 4 + t, 1), :].rearrange("p a s -> p (a s)"),
                                     X[:, ds(q * 4 + t, 1), :].rearrange("p a d -> p (a d)"))
                ins.then_inc(S("stats_raw"), 1)
            row_moments("row_step")
            v.memset(rg[:, 0:1], 0.0).then_inc(S("V_credit"), 1)
            v.wait_ge(S("rms_loaded"), 16)
            v.wait_ge(S("mu_loaded"), 32)
            v.wait_ge(S("rstd_step"), 6)
            with v.Fori(0, B) as b:
                for qd in range(2):
                    w = b * 2 + (qd + 1)
                    q4 = b * 8 + qd * 4
                    for t in range(4):
                        ins = v.tensor_scalar(xn[:, t, :], X[:, ds(q4 + t, 1), :].rearrange("p a d -> p (a d)"),
                                              mean[:, ds(q4 + t, 1)], rstd[:, ds(q4 + t, 1)],
                                              ALU.subtract, ALU.mult)
                    ins.then_inc(S("xn_ready"), 1)
                    v.wait_ge(S("xn_ready"), w)
                    for t in range(4):
                        ins = v.tensor_scalar(tn[:, t, :], xn[:, t, :], rrms[:, ds(q4 + t, 1)], None, ALU.mult)
                    ins.then_inc(S("tn_ready"), 1)
                    v.wait_ge(S("tn_turned"), w)
                    v.tensor_scalar(tS, bank(1), rms_w[:, 0:1], None, ALU.mult).then_inc(S("tS_ready"), 1)
                    v.wait_ge(S("shift_ready"), w)
                    v.scalar_tensor_tensor(xr, xT[:, qd, 1:513], mu[:, 0:1], tmr, ALU.mult, ALU.add)
                    v.scalar_tensor_tensor(xk, xT[:, qd, 1:513], mu[:, 2:3], tmk, ALU.mult, ALU.add).then_inc(S("xrk_ready"), 1)
                    v.wait_ge(S("gates_done"), w)
                    v.tensor_scalar(eg[:, :], bank(5)[:, 0:32], Z_MIN, None, ALU.max).then_inc(S("z_ready"), 1)
                    v.wait_ge(S("r_done"), w)
                    v.tensor_scalar(er, bank(3), Z_MIN, None, ALU.max).then_inc(S("z_ready"), 1)
                    v.wait_ge(S("eg_ready"), w)
                    v.tensor_scalar(rg[:, :], eg[:, :], 1.0, None, ALU.add).then_inc(S("sig_step"), 1)
                    v.wait_ge(S("er_ready"), w)
                    v.tensor_scalar(rr, er, 1.0, None, ALU.add).then_inc(S("sig_step"), 1)
                    v.wait_ge(S("sig_step"), w * 4 - 2)
                    v.reciprocal(rg[:, :], rg[:, :]).then_inc(S("sig_step"), 1)
                    v.reciprocal(rr, rr).then_inc(S("sig_step"), 1)
                    v.wait_ge(S("sig_step"), w * 4)
                    v.tensor_scalar(G[:, ds(q4, 4), :], rg[:, :].rearrange("p (t h) -> p t h", t=4), 1.0, None,
                                    ALU.mult).then_inc(S("G_ready"), 1)
                    v.wait_ge(S("v2_done"), w)
                    v.tensor_tensor(fo, bank(4), rr, ALU.mult).then_inc(S("fo_ready"), 1)
                    v.wait_ge(S("fo_ready"), w)
                    v.tensor_tensor(X[:, ds(q4, 4), :], X[:, ds(q4, 4), :], fo.rearrange("p (t d) -> p t d", t=4),
                                    ALU.add).then_inc(S("x_ffn"), 1)

            def copy_v(i, pr):
                v.tensor_scalar(Vp[:, :, :], V[:, ds((i // PAIRS) * NT, NT), ds(pr * 2 * E, 2 * E)], 1.0, None,
                                ALU.mult).then_inc(S("Vp_ready"), 1)

            v.wait_ge(S("V_ready"), TILES)
            v.tensor_scalar(Vp[:, :, :], V[:, 0:NT, 0:2 * E], 1.0, None, ALU.mult).then_inc(S("Vp_ready"), 1)
            v.wait_ge(S("proj_done"), 1)
            v.tensor_copy(K[:, :], bank(2, 2)).then_inc(S("qk_dve"), 1)
            v.wait_ge(S("x_ffn"), QUADS)
            v.memset(gs[:, 0, 0:1], 0.0).then_inc(S("x1_done"), 1)
            with v.Fori(0, STEPS) as n:
                nxt = v.snap((n + 1) % STEPS)
                nxt_pair = v.snap((n + 1) % PAIRS)
                pr = v.snap(n % PAIRS)
                tile0 = v.snap((n // PAIRS) * NT)
                for k in range(UNITS + 2):
                    if k < UNITS:
                        W = (k // 2 + 1) * P
                        v.wait_ge(S("scores_done"), n * UNITS + (k + 1))
                        v.tensor_reduce(nb[:, k:k + 1], bank(2 * (k % 2), 2)[:, 0:W], AX.X, ALU.max,
                                        negate=True).then_inc(S("max_ready"), 1)
                    if k >= 2:
                        u = k - 2
                        W = min(512, (u // 2 + 1) * P)
                        if u >= 2:
                            v.wait_ge(S("pv_done"), n * UNITS + (u - 1))
                        v.wait_ge(S("PT_turned"), n * UNITS + (u + 1))
                        v.tensor_copy(PT[:, u % 2, 0:W], bank(4)[:, 0:W]).then_inc(S("PT_lo"), 1)
                    if k in (9, UNITS + 1):
                        half = int(k != 9)
                        v.wait_ge(S("exp_done"), n * UNITS + (8 * half + 8))
                        v.reciprocal(rinv[:, 8 * half:8 * half + 8], rs[:, 8 * half:8 * half + 8]).then_inc(S("gs_step"), 1)
                        v.wait_ge(S("gs_step"), n * 4 + (2 * half + 1))
                        v.tensor_tensor(gs[:, :, :], rinv[:, 8 * half:8 * half + 8].rearrange("p (t h) -> p t h", h=2),
                                        G[:, ds(tile0 + 4 * half, 4), ds(pr * 2, 2)], ALU.mult).then_inc(S("gs_step"), 1)
                        v.wait_ge(S("gs_step"), n * 4 + (2 * half + 2))
                        v.tensor_copy(Sx[:, :, :, :], gs[:, :, :].unsqueeze(3).to_broadcast([P, 4, 2, E])).then_inc(S("Sx_ready"), 1)
                    if k == 12:
                        v.wait_ge(S("pv_done"), n * UNITS + 8)
                        v.wait_ge(S("R_ready"), n * 2 + 1)
                        v.tensor_tensor(OT[:, 0:512], bank(6), R[:, 0, :], ALU.mult).then_inc(S("OT_ready"), 1)
                v.wait_ge(S("proj_done"), n + 2)
                v.tensor_copy(K[:, :], bank(2, 2)).then_inc(S("qk_dve"), 1)
                v.wait_ge(S("pv_done"), n * UNITS + UNITS)
                v.wait_ge(S("R_ready"), n * 2 + 2)
                v.tensor_tensor(OT[:, 512:1024], bank(7), R[:, 1, :], ALU.mult).then_inc(S("OT_ready"), 1)
                copy_v(nxt, nxt_pair)
                v.wait_ge(S("wo_done"), n + 1)
                v.tensor_tensor(X[:, ds(tile0, NT), :], X[:, ds(tile0, NT), :],
                                bank(4, 2).rearrange("p (t d) -> p t d", t=NT), ALU.add).then_inc(S("x1_done"), 1)


            v.wait_ge(S("x1_done"), 1 + STEPS)
            with v.Fori(0, QUADS) as q:
                for t in range(4):
                    ins = v.bn_stats(stats[:, ds(q * 4 + t, 1), :].rearrange("p a s -> p (a s)"),
                                     X[:, ds(q * 4 + t, 1), :].rearrange("p a d -> p (a d)"))
                ins.then_inc(S("stats_raw2"), 1)
            row_moments("row_step2", "stats_raw2")
            v.wait_ge(S("bin_done"), 1)
            v.tensor_copy(w1T[:, :], bank(0)).then_inc(S("bin_turned"), 1)
            v.tensor_copy(w2T[:, :, :].rearrange("p t d -> p (t d)"), bank(1)).then_inc(S("bin_turned"), 1)
            v.wait_ge(S("rstd_step"), 8)
            v.wait_ge(S("l1_zero"), 1)
            XS = X[:, :, :].rearrange("p (g t) d -> p g t d", g=B)
            MS = mean[:, :].rearrange("p (g t) -> p g t", g=B)
            RS = rstd[:, :].rearrange("p (g t) -> p g t", g=B)

            def wait(s, *names):
                for name in names:
                    v.wait_ge(S(name), count(name, s))

            def over(ap, shape, at):
                return ap.unsqueeze(at).to_broadcast(shape)

            def flat(t):
                return t.rearrange("p g j -> p (g j)")

            def by_head(t, h):
                return t.rearrange("p (g h) j -> p g h j", g=B)[:, :, h, :]

            G3 = [P, GH, SUB]

            def f_xn(s):
                for g in range(B):
                    ins = v.tensor_scalar(xn1[:, g, :], XS[:, g, ds(s, 1), :].rearrange("p a d -> p (a d)"),
                                          MS[:, g, ds(s, 1)], RS[:, g, ds(s, 1)], ALU.subtract, ALU.mult)
                ins.then_inc(S("xn1_ready"), 1)

            def f_control(s):
                wait(s, "ctrl_done")
                for i in range(2):
                    ins = v.tensor_tensor(ctl[:, 2 * i:2 * i + 2, :], bank(i)[:, 0:2 * CT].rearrange("p (g c) -> p g c", g=2),
                                          over(b_ctrl[:, :], [P, 2, CT], 1), ALU.add)
                ins.then_inc(S("ctl_raw"), 1)
                wait(s, "ctl_raw")
                v.tensor_scalar(ctl[:, :, :], ctl[:, :, :], Z_MIN, None, ALU.max).then_inc(S("ctl_ready"), 1)

            def f_alpha(s):
                wait(s, "sg_ready")
                v.tensor_scalar(al[:, :, :], sg[:, :, 0:H1], 0.98, 0.01, ALU.mult, ALU.add).then_inc(S("al_ready"), 1)

            def f_conv(s, k):
                for i in range(3):
                    wait(s, f"qkv{i}_ready" if k == 2 else f"conv{i}_{k + 1}")
                    v.scalar_tensor_tensor(cy[:, i, :, :], qkv_in[:, i, :, k:k + P], conv_w[:, i, k:k + 1],
                                           cy[:, i, :, :], ALU.mult, ALU.add).then_inc(S(f"conv{i}_{k}"), 1)

            def f_clamp(s):
                for i in range(3):
                    wait(s, f"conv{i}_0")
                    v.tensor_scalar(ce[:, i, :, :], cy[:, i, :, :], Z_MIN, None, ALU.max).then_inc(S(f"conv{i}_done"), 1)

            def f_tokens(s):
                for i in range(3):
                    wait(s, f"tok{i}_turned")
                    ins = v.tensor_copy(tok[:, i, :, :].rearrange("p g d -> p (g d)"), bank(i + i // 2))
                ins.then_inc(S("tok_ready"), 1)

            def f_residual(s, p):
                wait(s, "ffn_out")
                v.tensor_tensor(acc[:, p, :, :].unsqueeze(2), XS[:, :, ds(s, 1), :], bank(2).rearrange("p (g a d) -> p g a d", g=B, a=1),
                                ALU.add).then_inc(S("acc_ready"), 1)
                wait(s, "acc_ready")
                v.tensor_tensor(acc[:, p, :, :], acc[:, p, :, :], over(b2row[:, :], [P, B, D], 1), ALU.add).then_inc(S("acc2_ready"), 1)

            def refine(y, x, t, names, s, last):
                wait(s, names[0])
                v.tensor_tensor(t, y, y, ALU.mult).then_inc(S(names[1]), 1)
                wait(s, names[1])
                v.scalar_tensor_tensor(t, t, -0.5, x, ALU.mult, ALU.mult).then_inc(S(names[2]), 1)
                wait(s, names[2])
                v.scalar_tensor_tensor(y, t, 1.5, y, ALU.add, ALU.mult).then_inc(S(last), 1)

            def f_sums(s):
                wait(s, "tok_ready")
                for i in range(2):
                    ins = v.tensor_tensor(sq[:, i, :, :], tok[:, i, :, :], tok[:, i, :, :], ALU.mult)
                ins.then_inc(S("sq_ready"), 1)
                wait(s, "sq_ready")
                v.tensor_reduce(ss[:, :, :], sq[:, :, :, :].rearrange("p i g (h e) -> p i (g h) e", e=E1), AX.X, ALU.add).then_inc(S("ss_raw"), 1)
                wait(s, "ss_raw")
                v.tensor_scalar(ss[:, :, :], ss[:, :, :], 1e-12, None, ALU.max).then_inc(S("ss_ready"), 1)

            def f_norm(s):
                refine(rn[:, :, :], ss[:, :, :], rt[:, :, :], ("rn_e", "rn_a", "rn_b"), s, "rn_ready")
                wait(s, "rn_ready")
                for i in range(2):
                    ins = v.tensor_tensor(qk_n[:, i, :, :].rearrange("p g (h e) -> p (g h) e", e=E1),
                                          tok[:, i, :, :].rearrange("p g (h e) -> p (g h) e", e=E1), over(rn[:, i, :], G3, 2), ALU.mult)
                ins.then_inc(S("kn_ready"), 1)

            def f_gam_t(s):
                wait(s, "gam_m_ready")
                v.transpose(flat(gam_t[:, :, :]), flat(gam_m[:, :, :])).then_inc(S("gam_t_ready"), 1)

            def f_kk(s, p):
                wait(s, "kk_done", "gam_b_ready")
                kkp = ps_all[:, 0:4, 0:256].rearrange("p h (g a j) -> p h g a j", g=B, a=2)
                for h in range(H1):
                    ins = v.tensor_tensor(by_head(Lc[:, p, :, :], h), kkp[:, h, :, 0, :], by_head(gam_b[:, :, :], h), ALU.mult)
                ins.then_inc(S("Lc_ready"), 1)
                wait(s, "gam_t_ready")
                for h in range(H1):
                    ins = v.tensor_tensor(by_head(Pc[:, p, :, :], h), kkp[:, h, :, 1, :], by_head(gam_t[:, :, :], h), ALU.mult)
                ins.then_inc(S("Pc_ready"), 1)

            def spread(src, name):
                for q in range(NB):
                    r = slice(q * SUB, (q + 1) * SUB)
                    ins = v.tensor_copy(Tx[r, :, q * SUB:(q + 1) * SUB], src[r, :, :])
                ins.then_inc(S(name), 1)

            def b_pairs(s, p):
                wait(s, "Lc_ready")
                v.tensor_tensor(Tc[:, :, :], Lc[:, p, :, :], over(merge[:, 0, :], G3, 1), ALU.mult).then_inc(S("T2_raw"), 1)
                wait(s, "T2_raw")
                v.tensor_tensor(Tc[:, :, :], over(eye, G3, 1), Tc[:, :, :], ALU.subtract).then_inc(S("T0_ready"), 1)
                wait(s, "T0_ready")
                v.transpose(flat(Zc[:, 0, :, :]), flat(Tc[:, :, :])).then_inc(S("Z0_ready"), 1)

            def b_join(s, k):
                wait(s, f"ZY{k}_done")
                v.tensor_tensor(Zc[:, (k + 1) % 2, :, :], Zc[:, k % 2, :, :], bank(5).rearrange("p (g j) -> p g j", g=GH),
                                ALU.subtract).then_inc(S(f"Z{k + 1}_ready"), 1)
                wait(s, f"Z{k + 1}_ready")
                if k < 3:
                    v.transpose(flat(Tc[:, :, :]), flat(Zc[:, (k + 1) % 2, :, :])).then_inc(S(f"T{k + 1}_ready"), 1)
                    wait(s, f"T{k + 1}_ready")
                    spread(Tc, f"Tx{k + 1}_ready")
                else:
                    spread(Zc[:, 0, :, :], "Tx4_ready")

            def b_pw(s, p):
                wait(s, "PW_done", "Qd_ready")
                pw = bank(4, 2).rearrange("p (g j) -> p g j", g=GH)
                v.tensor_tensor(Mo[:, :, :], Qd[:, p, :, :], pw[:, :, SUB:], ALU.subtract).then_inc(S("Mo_ready"), 1)
                v.tensor_copy(Ov[:, :, :], pw[:, :, 0:SUB]).then_inc(S("Ov_ready"), 1)

            def b_maps(s, p):
                wait(s, "AB_done", "dec_ready")
                abp = ps_all[:, 4:8, 0:256].rearrange("p q (g a j) -> p q g a j", g=B, a=2)
                for q in range(NB):
                    for g in range(B):
                        ins = v.scalar_tensor_tensor(At[:, q, g, :], eye, dec[:, p, 32 + g * NB + q:33 + g * NB + q],
                                                     abp[:, q, g, 1, :], ALU.mult, ALU.subtract)
                ins.then_inc(S("At_ready"), 1)
                wait(s, "At_ready")
                v.transpose(Ac[:, :, :, :].rearrange("p q g e -> p (q g e)"), At[:, :, :, :].rearrange("p q g e -> p (q g e)")).then_inc(S("Ac_ready"), 1)
                for q in range(NB):
                    ins = v.tensor_copy(Bc[:, q, :, :], abp[:, q, :, 0, :])
                ins.then_inc(S("Bc_ready"), 1)
                v.tensor_copy(St[:, 0, :, :], St[:, NB, :, :]).then_inc(S("St0_ready"), 1)

            def b_state(s):
                wait(s, "St0_ready", "Bc_ready")
                for q in range(NB):
                    wait(s, f"AS{q}_done")
                    v.tensor_tensor(St[:, q + 1, :, :], bank(4)[:, 0:P].rearrange("p (g j) -> p g j", g=B),
                                    Bc[:, q, :, :], ALU.add).then_inc(S(f"St{q + 1}_ready"), 1)

            def b_read(s):
                wait(s, "MS_done", "Ov_ready")
                for h in range(H1):
                    ins = v.tensor_tensor(by_head(rd[:, :, :], h), bank(4 + h)[:, 0:P].rearrange("p (g j) -> p g j", g=B), by_head(Ov[:, :, :], h), ALU.add)
                ins.then_inc(S("rd_ready"), 1)

            def b_read_sums(s):
                wait(s, "rd_ready")
                v.tensor_tensor(rsq, rd[:, :, :], rd[:, :, :], ALU.mult).then_inc(S("rsq_ready"), 1)
                wait(s, "rsq_ready")
                v.tensor_reduce(rss[:, :], rsq, AX.X, ALU.add).then_inc(S("rss_raw"), 1)
                wait(s, "rss_raw")
                v.tensor_scalar(rss[:, :], rss[:, :], 1.0 / E1, 1e-6, ALU.mult, ALU.add).then_inc(S("rss_ready"), 1)

            def b_read_norm(s):
                refine(rrs[:, :], rss[:, :], rrt[:, :], ("rrs_e", "rrs_a", "rrs_b"), s, "rrs_ready")
                wait(s, "rrs_ready")
                v.tensor_tensor(rdn[:, :, :].rearrange("p g (h e) -> p (g h) e", e=E1), rd[:, :, :], over(rrs[:, :], G3, 2),
                                ALU.mult).then_inc(S("rdn_ready"), 1)

            def b_out(s, p):
                wait(s, "out_done")
                v.tensor_tensor(ao[:, :, :], bank(7).rearrange("p (g d) -> p g d", g=B), over(b_out_row, [P, B, D], 1),
                                ALU.add).then_inc(S("out_read"), 1)
                v.wait_ge(S("out_read"), s + 2)
                wait(s, "ogr_ready")
                v.tensor_tensor(ao[:, :, :], ao[:, :, :], ogr[:, p, :, :], ALU.mult).then_inc(S("ao2"), 1)
                v.wait_ge(S("stored"), s * 16 + 16)
                wait(s, "ao2", "acc2_ready")
                v.tensor_tensor(res[:, :, :], acc[:, p, :, :], ao[:, :, :], ALU.add).then_inc(S("res_ready"), 1)

            b_out_row = b_out_sb[:, :]

            def round_of(s, p, ahead, after=True):
                b_join(s, 1)
                if ahead:
                    f_conv(s + 1, 2)
                    f_control(s + 1)
                    f_conv(s + 1, 1)
                    f_conv(s + 1, 0)
                    f_clamp(s + 1)
                b_join(s, 2)
                b_join(s, 3)
                if ahead:
                    f_alpha(s + 1)
                    f_tokens(s + 1)
                    f_sums(s + 1)
                b_pw(s, p)
                if ahead:
                    f_residual(s + 1, 1 - p)
                    f_norm(s + 1)
                b_maps(s, p)
                if ahead:
                    f_gam_t(s + 1)
                b_state(s)
                if ahead:
                    f_kk(s + 1, 1 - p)
                    b_pairs(s + 1, 1 - p)
                b_read(s)
                if ahead:
                    spread(Tc, "Tx0_ready")
                b_read_sums(s)
                b_read_norm(s)
                if ahead:
                    b_join(s + 1, 0)
                if after:
                    f_xn(s + 2)
                b_out(s, p)

            f_xn(0)
            f_conv(0, 2)
            f_control(0)
            f_conv(0, 1)
            f_conv(0, 0)
            f_clamp(0)
            f_alpha(0)
            f_tokens(0)
            f_sums(0)
            f_residual(0, 0)
            f_norm(0)
            f_gam_t(0)
            f_xn(1)
            f_kk(0, 0)
            b_pairs(0, 0)
            spread(Tc, "Tx0_ready")
            b_join(0, 0)
            with v.Fori(0, NT // 2 - 1) as i:
                round_of(i * 2, 0, True)
                round_of(i * 2 + 1, 1, True)
            round_of(NT - 2, 0, True, False)
            round_of(NT - 1, 1, False, False)


_INS = ['L0_attn_tokens', 'L0_attn_wq', 'L0_attn_wk', 'L0_attn_wv', 'L0_attn_wo', 'L0_attn_w_gates', 'L0_attn_rms_w',
        'L0_ffn_W_r', 'L0_ffn_W_k', 'L0_ffn_W_v', 'L0_ffn_mu_r', 'L0_ffn_mu_k', 'L1_attn_W_in', 'L1_attn_W_ctrl',
        'L1_attn_b_ctrl', 'L1_attn_w_q', 'L1_attn_w_k', 'L1_attn_w_v', 'L1_attn_W_out', 'L1_attn_b_out',
        'L1_attn_ramp_logit', 'L1_ffn_w1', 'L1_ffn_b1', 'L1_ffn_w2', 'L1_ffn_b2']
_OUTS = [((4, 1024, 128), 'float32')]


def _masks():
    import numpy as _np

    n, sub = 128, 32
    r, c = _np.arange(n)[:, None], _np.arange(n)[None, :]
    j = _np.arange(sub)[None, :]
    i = r % sub
    parts = [(r // sub == c // sub) & (r <= c), (r // sub == c // sub) & (r > c),
             r // sub == _np.arange(n // sub)[None, :], i == j, j < i, j <= i]
    for m in (1, 2, 4, 8, 16):
        parts.append((i // (2 * m) == j // (2 * m)) & (i % (2 * m) >= m) & (j % (2 * m) < m))
    return _np.concatenate(parts, axis=1).astype(_np.float32)


def kernel(**inputs):
    import numpy as _np
    import concourse.bacc as _bacc
    from concourse import mybir as _mybir
    from concourse.bass_utils import run_bass_kernel_spmd as _run

    nc = _bacc.Bacc("TRN2", target_bir_lowering=False, num_devices=1)
    arrays, aps = {}, {}
    for name in _INS:
        a = _np.ascontiguousarray(inputs[name])
        arrays[f"in_{name}_dram"] = a
        aps[name] = nc.dram_tensor(f"in_{name}_dram", a.shape, _mybir.dt.from_np(a.dtype), kind="ExternalInput").ap()
    arrays["masks_dram"] = _masks()
    aps["masks"] = nc.dram_tensor("masks_dram", arrays["masks_dram"].shape, _mybir.dt.float32, kind="ExternalInput").ap()
    outs = []
    for i, (shape, dtype) in enumerate(_OUTS):
        dt = _mybir.dt.from_np(_np.dtype(dtype))
        outs.append(nc.dram_tensor(f"out_{i}_dram", shape, dt, kind="ExternalOutput").ap())
    build(nc, aps, outs[0])
    r = _run(nc, [arrays], core_ids=[0])
    return r.results[0]["out_0_dram"]
```

```python
from contextlib import ExitStack

import concourse.bass as bass
from concourse import mybir

ALU = mybir.AluOpType
ACT = mybir.ActivationFunctionType
AX = mybir.AxisListType
F32 = mybir.dt.float32
BF16 = mybir.dt.bfloat16
ds = bass.ds

P = 128
EPS_LN = 1e-5
EPS_RMS = 1.1920928955078125e-07
MASKED = -1e30
Z_MIN = -44.0


def build(nc, A, out):
    B, N, D = A["L0_attn_tokens"].shape
    H, _, E = A["L0_attn_wq"].shape
    NT = N // P
    TILES = B * NT
    QUADS = TILES // 4
    PAIRS = H // 2
    STEPS = B * PAIRS
    UNITS = 2 * NT
    SCALE = float(E) ** -0.5
    H1 = 4
    E1 = D // H1
    SUB = 32
    NB = P // SUB
    GH = B * H1
    CT = A["L1_attn_W_ctrl"].shape[1]
    FT = A["L1_ffn_w1"].shape[0] // P
    L1_LOADS = 3 + 4 + 1 + FT + 3
    assert E1 == SUB == 32 and B == 4 and NB == 4

    x_dram = A["L0_attn_tokens"].rearrange("b (t p) d -> p (b t) d", p=P)
    out_dram = out.rearrange("b (t p) d -> p (b t) d", p=P)

    with ExitStack() as ctx:
        def sb(name, shape, dt=F32):
            return ctx.enter_context(nc.sbuf_tensor(name, shape, dt))

        sems = {}
        shared = {}
        for family, steps in {
            "conv": [f"conv{i}_{k}" for k in (2, 1, 0) for i in range(2)] + [f"conv{i}_done" for i in range(3)],
            "conv_v": [f"conv2_{x}{k}" for k in (2, 1, 0) for x in ("m", "")],
            "join": ["T2_raw", "T0_ready", "Z0_ready", "Tx0_ready"]
            + [f"{x}{k}{c}_ready" for k in (1, 2, 3) for c in "ab" for x in ("Z", "T", "Tx")]
            + [f"{x}4{c}_ready" for c in "ab" for x in ("Z", "Tx")],
            "state": ["St0_ready", "St1_ready", "St2_ready", "St3_ready"],
            "norm": ["sq_ready", "ss_raw", "ss_ready", "rn_a", "rn_b", "rn_ready"],
            "control": ["ctl_raw", "ctl_ready", "al_ready"],
            "read": ["rd_ready", "rsq_ready", "rss_raw", "rss_ready", "rrs_a", "rrs_b", "rrs_ready", "rdn_ready"],
            "qkv_done": [f"qkv{i}_done" for i in range(3)],
            "ffn_done": [f"ffn{t}_done" for t in range(FT)],
            "tok_turned": [f"tok{i}_turned" for i in range(3)],
            "join_products": [f"{x}{k}{c}_done" for k in range(4) for x in ("Y", "ZY") for c in "ab"],
            "AS_done": [f"AS{q}_done" for q in range(NB)],
            "qkv_ready": [f"qkv{i}_ready" for i in range(3)],
            "sigmoid": ["sg_e", "sg_l", "sg_ready"],
            "ce": [f"ce{i}_{x}" for x in ("e", "l", "s") for i in range(3)],
            "silu": [f"silu{i}_ready" for i in range(3)],
            "h_ready": [f"h{t}_ready" for t in range(FT)],
            "Bx_ready": [f"Bx{k}_ready" for k in range(4)],
            "Y_ready": [f"Y{k}{c}_ready" for k in range(4) for c in "ab"],
            "Bm_ready": [f"Bm{k}_ready" for k in range(4)],
            "roots": ["rn_l", "rn_e"],
            "W_done": ["Wa_done", "Wb_done"],
            "Wv_ready": ["Wva_ready", "Wvb_ready"],
            "PW_done": ["PWa_done", "PWb_done"],
            "Mo_ready": ["Moa_ready", "Mob_ready"],
            "log_decays_ready": ["laG_ready", "laX_ready"],
            "gam_masked": ["gam_m_ready", "gam_b_ready"],
            "decayed": ["Rv_ready", "Qd_ready"],
            "betas_ready": ["bm_ready", "ogr_ready"],
            "read_roots": ["rrs_l", "rrs_e"],
        }.items():
            for i, step in enumerate(steps):
                shared[step] = (family, len(steps), i)

        def count(name, s):
            _, per, i = shared.get(name, (name, 1, 0))
            return s * per + (i + 1)

        def S(name):
            name = shared.get(name, (name,))[0]
            if name not in sems:
                sems[name] = ctx.enter_context(nc.semaphore(name))
            return sems[name]

        ps_all = ctx.enter_context(nc.psum_tensor("ps_all", [P, 8, 512], F32))

        def bank(i, n=1):
            return ps_all[:, i, :] if n == 1 else ps_all[:, i:i + n, :].rearrange("p b n -> p (b n)")

        X = sb("X", [P, TILES, D])
        stats = sb("stats", [P, TILES, 6])
        mean = sb("mean", [P, TILES])
        var = sb("var", [P, TILES])
        ve = sb("ve", [P, TILES])
        rstd = sb("rstd", [P, TILES])
        rms2 = sb("rms2", [P, TILES])
        rrms = sb("rrms", [P, TILES])
        ident = sb("ident", [P, P])
        identb = sb("identb", [P, P], BF16)
        causal = sb("causal", [P, P], BF16)
        w_in = sb("w_in", [P, 3 * D])
        w_ctrl = sb("w_ctrl", [P, CT])
        w_out = sb("w_out", [P, D])
        b_ctrl = sb("b_ctrl", [P, CT])
        b_out_sb = sb("b_out", [P, D])
        ramp = sb("ramp", [P, D])
        b2row = sb("b2row", [P, D])
        b1col = sb("b1col", [P, FT])
        conv_w = sb("conv_w", [P, 3, 4])
        w1T = sb("w1T", [P, FT * P])
        w2T = sb("w2T", [P, FT, D])
        masks = sb("masks", [P, 2 * P + NB + 8 * SUB])
        upto = masks[:, 0:P]
        beyond = masks[:, P:2 * P]
        in_block = masks[:, 2 * P:2 * P + NB]
        compact = masks[:, 2 * P + NB:].rearrange("p (k j) -> p k j", j=SUB)
        eye, below, upto_c = compact[:, 0, :], compact[:, 1, :], compact[:, 2, :]
        merge = compact[:, 3:8, :]
        persistent = sb
        l0 = ExitStack()

        def sb(name, shape, dt=F32):
            return l0.enter_context(nc.sbuf_tensor(name, shape, dt))

        wv_sb = sb("wv_sb", [P, H, E])
        wg_sb = sb("wg_sb", [P, H])
        rms_w = sb("rms_w", [P, 1])
        wqk = sb("wqk", [P, 2, 2 * E])
        wo_sb = sb("wo_sb", [P, PAIRS, D])
        w3 = sb("w3", [P, 3, D])
        w3T = sb("w3T", [P, 3, D])
        mu = sb("mu", [P, 4])
        TT = sb("TT", [P, B * N])
        V = sb("V", [P, TILES, H * E])
        G = sb("G", [P, TILES, H])

        Pbuf = sb("Pbuf", [P, 4, N])
        PT = sb("PT", [P, 2, N])
        Qp = sb("Qp", [P, 2, N])
        K = sb("K", [P, N])
        Vp = sb("Vp", [P, NT, 2 * E])
        OT = sb("OT", [P, N])
        share = sb("share", [P, N])
        R = sb("R", [P, 2, 512])
        Sx = sb("Sx", [P, 4, 2, E])
        nb = sb("nb", [P, UNITS])
        rs = sb("rs", [P, UNITS])
        rinv = sb("rinv", [P, UNITS])
        gs = sb("gs", [P, 4, 2])

        xn = Pbuf[:, 0, 0:512].rearrange("p (t d) -> p t d", t=4)
        tn = Pbuf[:, 0, 512:1024].rearrange("p (t d) -> p t d", t=4)
        xT = sb("xT", [P, 2, 1 + 512])
        tS = sb("tS", [P, 2, 512])
        xr = Pbuf[:, 1, 512:1024]
        xk = Pbuf[:, 2, 0:512]
        tmr = Pbuf[:, 2, 512:1024]
        tmk = Pbuf[:, 3, 0:512]
        kr = Pbuf[:, 3, 512:1024]
        ka = PT[:, 0, 0:512]
        er = PT[:, 0, 512:1024]
        fo = PT[:, 1, 512:1024]
        eg = sb("eg", [P, 2, 32])

        w12 = sb("w12", [P, 2, 512])
        w12s = sb("w12s", [P, 2, 512])
        alpha = sb("alpha", [P, FT + 1])
        l0.close()
        sb = persistent

        xn1 = sb("xn1", [P, B, D])
        x1T = sb("x1T", [P, 512])
        qkv_in = sb("qkv_in", [P, 3, B, 3 + P])
        cy = sb("cy", [P, 3, B, P])
        ce = sb("ce", [P, 3, B, P])
        tok = sb("tok", [P, 3, B, D])
        sq = sb("sq", [P, 2, B, D])
        ss = sb("ss", [P, 2, GH])
        rn = sb("rn", [P, 2, GH])
        rt = sb("rt", [P, 2, GH])
        qk_n = sb("qk_n", [P, 2, B, D])
        kqT = sb("kqT", [P, B, 2, P])
        ctl = sb("ctl", [P, B, CT])
        sg = sb("sg", [P, B, CT])
        al = sb("al", [P, B, H1])
        la_wide = sb("la_wide", [P, P])
        la = la_wide[:, 0:GH].rearrange("p (g h) -> p g h", g=B)
        ogr = sb("ogr", [P, 2, B, D])
        laG = sb("laG", [P, GH, SUB])
        laX = sb("laX", [P, B, D])
        ones = sb("ones", [P, SUB])
        gam = sb("gam", [P, GH, SUB])
        gam_b = sb("gam_b", [P, GH, SUB])
        gam_t = sb("gam_t", [P, GH, SUB])
        gam_m = laG
        dec = sb("dec", [P, 2, 48])
        decI = sb("decI", [P, NB, B, SUB])
        bD = sb("bD", [P, GH])
        Lc = sb("Lc", [P, 2, GH, SUB])
        Pc = sb("Pc", [P, 2, GH, SUB])
        Bm = sb("Bm", [P, 4, GH, SUB])
        Bx = sb("Bx", [P, 2, GH, P])
        Tx = sb("Tx", [P, GH, P])
        Tc = sb("Tc", [P, GH, SUB])
        Zc = sb("Zc", [P, 2, GH, SUB])
        Yc = sb("Yc", [P, GH, SUB])
        Rv = sb("Rv", [P, 2, GH, 2 * SUB])
        Wv = sb("Wv", [P, GH, 2 * SUB])
        Px = sb("Px", [P, GH, P])
        Qd = sb("Qd", [P, 2, GH, SUB])
        Kd = sb("Kd", [P, 2, GH, SUB])
        Mo = sb("Mo", [P, GH, SUB])
        MoT = sb("MoT", [P, B, P])
        Ov = sb("Ov", [P, GH, SUB])
        Ac = sb("Ac", [P, NB, B, SUB])
        At = Yc[:, :, :].rearrange("p (q g) e -> p q g e", q=NB)
        Ax = sb("Ax", [P, NB, B, P])
        Bc = sb("Bc", [P, NB, B, SUB])
        St = sb("St", [P, NB + 1, B, SUB])
        rd = sb("rd", [P, GH, SUB])
        rsq = Ac[:, :, :, :].rearrange("p q g e -> p (q g) e")
        rss = sb("rss", [P, GH])
        rrs = sb("rrs", [P, GH])
        rrt = sb("rrt", [P, GH])
        rdn = sb("rdn", [P, B, D])
        rdT = sb("rdT", [P, B, P])
        hT = sb("hT", [P, FT, 512])
        acc = sb("acc", [P, 2, B, D])
        ao = rdn
        res = sb("res", [P, B, D])

        block = ctx.enter_context(nc.Block())

        @block.sync
        def _(sp):
            for b in range(B):
                sp.dma_start(X[:, b * NT:(b + 1) * NT, :], x_dram[:, b * NT:(b + 1) * NT, :]).then_inc(S("x_loaded"), 16)
            for i, name in enumerate(("W_r", "W_k", "W_v")):
                sp.dma_start(w3[:, i, :], A["L0_ffn_" + name]).then_inc(S("w3_loaded"), 16)
            sp.dma_start(mu[:, 0:1], A["L0_ffn_mu_r"].rearrange("(d a) -> d a", a=1)).then_inc(S("mu_loaded"), 16)
            sp.dma_start(mu[:, 2:3], A["L0_ffn_mu_k"].rearrange("(d a) -> d a", a=1)).then_inc(S("mu_loaded"), 16)
            sp.dma_start(rms_w[:, :], A["L0_attn_rms_w"].rearrange("(d a) -> d a", a=1)).then_inc(S("rms_loaded"), 16)
            sp.dma_start(wv_sb[:, :, :], A["L0_attn_wv"].rearrange("h d e -> d h e")).then_inc(S("wv_loaded"), 16)
            sp.dma_start(wg_sb[:, :], A["L0_attn_w_gates"]).then_inc(S("wv_loaded"), 16)
            sp.dma_start(wo_sb[:, :, :], A["L0_attn_wo"].rearrange("(a h) e d -> (h e) a d", h=2)).then_inc(S("wo_loaded"), 16)

            for name, dst in (("W_in", w_in), ("W_ctrl", w_ctrl), ("W_out", w_out)):
                sp.dma_start(dst[:, :], A["L1_attn_" + name]).then_inc(S("l1_loaded"), 16)
            for name, dst in (("L1_attn_b_ctrl", b_ctrl), ("L1_attn_b_out", b_out_sb), ("L1_attn_ramp_logit", ramp),
                              ("L1_ffn_b2", b2row)):
                sp.dma_start(dst[:, :], A[name].partition_broadcast(P)).then_inc(S("l1_loaded"), 16)
            sp.dma_start(masks[:, :], A["masks"]).then_inc(S("l1_loaded"), 16)
            for t in range(FT):
                sp.dma_start(b1col[:, t:t + 1], A["L1_ffn_b1"][t * P:(t + 1) * P].rearrange("(p a) -> p a", a=1)).then_inc(S("l1_loaded"), 16)
            for i, name in enumerate(("w_q", "w_k", "w_v")):
                sp.dma_start(conv_w[:, i, :], A["L1_attn_" + name].rearrange("d a k -> d (a k)")).then_inc(S("l1_loaded"), 16)
            sp.dma_start(w12[:, 0, :].rearrange("p (t d) -> p t d", t=FT),
                         A["L1_ffn_w1"].rearrange("(t p) d -> p t d", p=P)).then_inc(S("w12_loaded"), 16)
            sp.dma_start(w12[:, 1, :], A["L1_ffn_w2"]).then_inc(S("w12_loaded"), 16)

            def load_qk(p):
                sp.dma_start(wqk[:, 0, :].rearrange("d (h e) -> d h e", h=2),
                             A["L0_attn_wq"][ds(p * 2, 2)].rearrange("h d e -> d h e")).then_inc(S("wqk_loaded"), 16)
                sp.dma_start(wqk[:, 1, :].rearrange("d (h e) -> d h e", h=2),
                             A["L0_attn_wk"][ds(p * 2, 2)].rearrange("h d e -> d h e")).then_inc(S("wqk_loaded"), 16)

            load_qk(0)
            with sp.Fori(0, STEPS) as n:
                nxt = sp.snap(((n + 1) % PAIRS))
                sp.wait_ge(S("proj_done"), n + 1)
                load_qk(nxt)
            sp.wait_ge(S("wqk_loaded"), 32 * (STEPS + 1))
            with sp.Fori(0, NT) as s:
                sp.wait_ge(S("res_ready"), s + 1)
                sp.dma_start(out_dram.rearrange("p (g t) d -> p g t d", g=B)[:, :, ds(s, 1), :].rearrange("p g a d -> p g (a d)"),
                             res[:, :, :]).then_inc(S("stored"), 16)
            sp.wait_ge(S("stored"), 16 * (NT + 1))

        @block.gpsimd
        def _(g):
            g.memset(ident[:, :], 0.0).then_inc(S("ident_zero"), 1)
            g.memset(share[:, :], 0.0).then_inc(S("share_ready"), 1)
            g.memset(causal[:, :], 0.0).then_inc(S("ident_zero"), 1)
            g.memset(Qp[:, :, :], 0.0).then_inc(S("q_zero"), 1)
            g.memset(xT[:, 0, 0:1], 0.0).then_inc(S("halo_zero"), 1)
            g.wait_ge(S("ident_zero"), 2)
            g.affine_select(out=ident[:, :], in_=ident[:, :], compare_op=ALU.not_equal, fill=1.0,
                            base=0, pattern=[[-1, P]], channel_multiplier=1).then_inc(S("ident_set"), 1)
            g.affine_select(out=causal[:, :], in_=causal[:, :], compare_op=ALU.is_ge, fill=MASKED,
                            base=0, pattern=[[-1, P]], channel_multiplier=1).then_inc(S("causal_set"), 1)
            g.wait_ge(S("ident_set"), 1)
            g.tensor_copy(identb[:, :], ident[:, :]).then_inc(S("causal_set"), 1)
            g.wait_ge(S("mu_loaded"), 32)
            for c in (0, 2):
                g.tensor_scalar(mu[:, c + 1:c + 2], mu[:, c:c + 1], -1.0, 1.0, ALU.mult, ALU.add).then_inc(S("mu_set"), 1)
            g.wait_ge(S("mu_set"), 2)

            def shift(i, qd):
                g.wait_ge(S("xT_ready"), i + 1)
                g.tensor_tensor(tmr, xT[:, qd, 0:512], mu[:, 1:2].to_broadcast([P, 512]), ALU.mult)
                g.tensor_tensor(tmk, xT[:, qd, 0:512], mu[:, 3:4].to_broadcast([P, 512]), ALU.mult).then_inc(S("shift_ready"), 1)
                g.wait_ge(S("tS_ready"), i + 1)
                g.tensor_copy(TT[:, ds(i * 512, 512)], tS[:, qd, :]).then_inc(S("TT_ready"), 1)

            def group(i, qd, ahead=True):
                g.wait_ge(S("kr_ready"), i + 1)
                g.tensor_tensor(ka, kr, kr, ALU.mult).then_inc(S("ka_ready"), 1)
                if ahead:
                    shift(i + 1, 1 - qd)

            shift(0, 0)
            with g.Fori(0, B - 1) as b:
                group(b * 2, 0)
                group(b * 2 + 1, 1)
            group(QUADS - 2, 0)
            group(QUADS - 1, 1, False)

            g.wait_ge(S("sign_ready"), 3)
            g.wait_ge(S("alpha_ready"), 2)
            for t in range(FT):
                g.tensor_tensor(w12s[:, 0, t * D:(t + 1) * D], w12s[:, 0, t * D:(t + 1) * D],
                                alpha[:, t:t + 1].to_broadcast([P, D]), ALU.mult)
            g.tensor_tensor(w12s[:, 1, :], w12s[:, 1, :], alpha[:, FT:FT + 1].to_broadcast([P, FT * P]),
                            ALU.mult).then_inc(S("bin_step"), 1)
            g.wait_ge(S("bin_step"), 1)
            g.tensor_tensor(w12s[:, :, :], w12s[:, :, :], w12[:, :, :], ALU.subtract).then_inc(S("bin_step"), 1)
            g.wait_ge(S("bin_step"), 2)
            g.tensor_tensor(w12[:, :, :], w12[:, :, :], w12s[:, :, :], ALU.add).then_inc(S("bin_ready"), 1)

            g.wait_ge(S("x_ffn"), QUADS)
            with g.Fori(0, B) as batch:
                with g.Fori(0, PAIRS) as pr:
                    g.wait_ge(S("share_ready"), batch * PAIRS + (pr + 2))
                    rows = X[:, ds(batch * NT, NT), :]
                    g.tensor_tensor(rows, rows, share[:, :].rearrange("p (t d) -> p t d", t=NT),
                                    ALU.add).then_inc(S("x1_done"), 1)

            g.wait_ge(S("x1_done"), 1 + STEPS)
            g.wait_ge(S("bin_turned"), 2)
            g.wait_ge(S("Vp_ready"), STEPS + 1)
            g.wait_ge(S("ramp_ready"), 1)
            g.memset(ones[:, :], 1.0)
            g.memset(qkv_in[:, :, :, :], 0.0)
            g.memset(la_wide[:, :], 0.0).then_inc(S("l1_zero"), 1)
            g.memset(St[:, :, :, :], 0.0).then_inc(S("out_read"), 1)
            g.memset(res[:, :, :], 0.0).then_inc(S("stored"), 16)
            g.memset(Bx[:, 0, :, :], 0.0)
            g.memset(Tx[:, :, :], 0.0)
            g.memset(Bx[:, 1, :, :], 0.0)
            g.memset(Px[:, :, :], 0.0)
            g.memset(Ax[:, :, :, :], 0.0)
            g.memset(gam_t[:, :, :], 0.0).then_inc(S("l1_zero"), 1)
            g.wait_ge(S("l1_zero"), 1)

            def tt(out, a, b, op, done=None):
                ins = g.tensor_tensor(out, a, b, op)
                if done:
                    ins.then_inc(S(done), 1)

            def over(ap, shape, at):
                return ap.unsqueeze(at).to_broadcast(shape)

            G3 = [P, GH, SUB]
            G4 = [P, B, H1, SUB]

            def front_conv(s):
                g.wait_ge(S("qkv2_ready"), count("qkv2_ready", s))
                for k in (2, 1, 0):
                    if k < 2:
                        g.wait_ge(S(f"conv2_{k + 1}"), count(f"conv2_{k + 1}", s))
                    tt(sq[:, 0, :, :], qkv_in[:, 2, :, k:k + P], conv_w[:, 2, k:k + 1].unsqueeze(2).to_broadcast([P, B, P]), ALU.mult, f"conv2_m{k}")
                    g.wait_ge(S(f"conv2_m{k}"), count(f"conv2_m{k}", s))
                    tt(cy[:, 2, :, :], cy[:, 2, :, :], sq[:, 0, :, :], ALU.add, f"conv2_{k}")

            def front_gates(s, p):
                for i in range(3):
                    g.wait_ge(S(f"ce{i}_s"), count(f"ce{i}_s", s))
                    tt(cy[:, i, :, :], cy[:, i, :, :], ce[:, i, :, :], ALU.mult, f"silu{i}_ready")
                bt = sg[:, :, H1:2 * H1]
                tt(gam_b[:, :, :].rearrange("p (g h) j -> p g h j", g=B), over(bt, G4, 3),
                   below.unsqueeze(1).unsqueeze(1).to_broadcast(G4), ALU.mult, "bm_ready")
                tt(ogr[:, p, :, :], sg[:, :, 2 * H1:], over(ramp[:, :], [P, B, D], 1), ALU.mult, "ogr_ready")
                g.wait_ge(S("v_tok_ready"), count("v_tok_ready", s))
                R4 = Rv[:, p, :, :].rearrange("p (g h) j -> p g h j", g=B)
                tt(R4[:, :, :, 0:SUB], tok[:, 2, :, :].rearrange("p g (h e) -> p g h e", h=H1), over(bt, G4, 3), ALU.mult)
                g.wait_ge(S("la_ready"), count("la_ready", s))
                tt(laG[:, :, :], over(la.rearrange("p g h -> p (g h)"), G3, 2), over(below, G3, 1), ALU.mult, "laG_ready")
                tt(laX[:, :, :].rearrange("p g (h e) -> p g h e", h=H1), over(la, G4, 3),
                   ones[:, :].unsqueeze(1).unsqueeze(1).to_broadcast(G4), ALU.mult, "laX_ready")

            def front_decays(s, p):
                bt = sg[:, :, H1:2 * H1]
                g.wait_ge(S("gam_ready"), count("gam_ready", s))
                g.wait_ge(S("bm_ready"), count("bm_ready", s))
                tt(gam_m[:, :, :], gam[:, :, :], over(upto_c, G3, 1), ALU.mult, "gam_m_ready")
                tt(gam_b[:, :, :], gam_b[:, :, :], gam[:, :, :], ALU.mult, "gam_b_ready")
                g.wait_ge(S("dec_ready"), count("dec_ready", s))
                tt(bD[:, :].rearrange("p (g h) -> p g h", g=B), bt, dec[:, p, 0:16].rearrange("p (g h) -> p g h", g=B), ALU.mult, "bD_ready")
                g.wait_ge(S("kn_ready"), count("kn_ready", s))
                g.wait_ge(S("bD_ready"), count("bD_ready", s))
                kn = qk_n[:, 1, :, :].rearrange("p g (h e) -> p (g h) e", h=H1)
                qn = qk_n[:, 0, :, :].rearrange("p g (h e) -> p (g h) e", h=H1)
                tt(Rv[:, p, :, SUB:], kn, over(bD[:, :], G3, 2), ALU.mult, "Rv_ready")
                tt(Qd[:, p, :, :], qn, over(dec[:, p, 0:16], G3, 2), ALU.mult, "Qd_ready")
                tt(Kd[:, p, :, :], kn, over(dec[:, p, 16:32], G3, 2), ALU.mult, "Kd_ready")

            def back_joins(s, p):
                g.wait_ge(S("Lc_ready"), count("Lc_ready", s))
                for k in range(4):
                    tt(Bm[:, k, :, :], Lc[:, p, :, :], over(merge[:, k + 1, :], G3, 1), ALU.mult, f"Bm{k}_ready")
                tt(decI[:, :, :, :], dec[:, p, 32:48].rearrange("p (g q) -> p q g", g=B).unsqueeze(3).to_broadcast([P, NB, B, SUB]),
                   eye.unsqueeze(1).unsqueeze(1).to_broadcast([P, NB, B, SUB]), ALU.mult, "decI_ready")

            def front(s, p):
                front_conv(s)
                front_gates(s, p)
                front_decays(s, p)
                back_joins(s, p)

            front(0, 0)
            with g.Fori(0, NT // 2 - 1) as i:
                front(i * 2 + 1, 1)
                front(i * 2 + 2, 0)
            front(NT - 1, 1)

        @block.scalar
        def _(act):
            act.wait_ge(S("w3_turned"), 1)
            act.activation(w3T[:, :, :], bank(0)[:, 0:384].rearrange("p (i d) -> p i d", i=3), ACT.Copy).then_inc(S("w3T_ready"), 1)
            act.wait_ge(S("w12_loaded"), 32)
            act.wait_ge(S("l1_loaded"), 16 * L1_LOADS)
            act.activation(w12s[:, 0, :], w12[:, 0, :], ACT.Sign).then_inc(S("sign_ready"), 1)
            act.activation(w12s[:, 1, :], w12[:, 1, :], ACT.Sign).then_inc(S("sign_ready"), 1)
            act.activation(ramp[:, :], ramp[:, :], ACT.Exp, scale=-1.0).then_inc(S("sign_ready"), 1)

            def first_root(y, x, t, nth):
                act.wait_ge(S("root_in"), nth)
                act.activation(t, x, ACT.Ln).then_inc(S("root_log"), 1)
                act.wait_ge(S("root_log"), nth)
                act.activation(y, t, ACT.Exp, scale=-0.5).then_inc(S("root_exp"), 1)

            first_root(rstd[:, :], ve[:, :], rms2[:, :], 1)
            first_root(rrms[:, :], ve[:, :], rms2[:, :], 2)
            act.wait_ge(S("halo_zero"), 1)

            def turned_x(i, qd):
                act.wait_ge(S("xn_turned"), i + 1)
                if qd == 1:
                    act.wait_ge(S("xT_ready"), i)
                    act.activation(xT[:, 1, 0:1], xT[:, 0, 512:513], ACT.Copy)
                act.activation(xT[:, qd, 1:513], bank(0), ACT.Copy).then_inc(S("xT_ready"), 1)

            def group(i, qd, ahead=True):
                def values(k):
                    act.wait_ge(S("v_done"), i * 4 + (k * 2 + 1))
                    act.activation(V[:, ds(i * 4 + k * 2, 1), :].rearrange("p a n -> p (a n)"),
                                   bank(6), ACT.Copy).then_inc(S("V_even"), 1)

                act.wait_ge(S("k_done"), i + 1)
                act.activation(kr, bank(2), ACT.Relu).then_inc(S("kr_ready"), 1)
                act.wait_ge(S("z_ready"), i * 2 + 1)
                act.activation(eg[:, qd, :], eg[:, qd, :], ACT.Exp, scale=-1.0).then_inc(S("z_exp"), 1)
                act.wait_ge(S("z_ready"), i * 2 + 2)
                act.activation(er, er, ACT.Exp, scale=-1.0).then_inc(S("z_exp"), 1)
                if ahead:
                    turned_x(i + 1, 1 - qd)
                values(0)
                act.wait_ge(S("z_exp"), i * 2 + 2)
                act.activation(eg[:, qd, :], eg[:, qd, :], ACT.Ln, bias=1.0).then_inc(S("z_log"), 1)
                act.activation(er, er, ACT.Ln, bias=1.0).then_inc(S("z_log"), 1)
                values(1)
                act.wait_ge(S("z_log"), i * 2 + 2)
                act.activation(er, er, ACT.Exp, scale=-1.0).then_inc(S("z_sigmoid"), 1)
                act.activation(eg[:, qd, :], eg[:, qd, :], ACT.Exp, scale=-1.0).then_inc(S("z_sigmoid"), 1)

            turned_x(0, 0)
            with act.Fori(0, B - 1) as b:
                group(b * 2, 0)
                group(b * 2 + 1, 1)
            group(QUADS - 2, 0)
            group(QUADS - 1, 1, False)

            def qk_evac(nth):
                act.wait_ge(S("q_proj_done"), nth)
                act.activation(Qp[0:64, 0, :], bank(0, 2)[0:64, :], ACT.Copy, scale=SCALE)
                act.activation(Qp[64:128, 1, :], bank(0, 2)[64:128, :], ACT.Copy, scale=SCALE).then_inc(S("qk_act"), 1)

            act.wait_ge(S("q_zero"), 1)
            qk_evac(1)
            with act.Fori(0, STEPS) as n:
                for k in range(UNITS + 2):
                    if k < UNITS:
                        W = (k // 2 + 1) * P
                        if k >= 4:
                            act.wait_ge(S("PT_turned"), n * UNITS + (k - 3))
                        act.wait_ge(S("max_ready"), n * UNITS + (k + 1))
                        act.activation(Pbuf[:, k % 4, 0:W], bank(2 * (k % 2), 2)[:, 0:W], ACT.Exp,
                                       bias=nb[:, k:k + 1], accum_out=rs[:, k:k + 1]).then_inc(S("exp_done"), 1)
                    if k >= 2 and (k - 2) // 2 >= 4:
                        u = k - 2
                        W = (u // 2 + 1) * P
                        act.wait_ge(S("PT_turned"), n * UNITS + (u + 1))
                        act.wait_ge(S("pv_done"), n * UNITS + (u - 1))
                        act.activation(PT[:, u % 2, 512:W], bank(5)[:, 0:W - 512], ACT.Copy).then_inc(S("PT_hi"), 1)
                    if k in (10, UNITS + 1):
                        half = int(k != 10)
                        act.wait_ge(S("R_turned"), n * 2 + (half + 1))
                        act.activation(R[:, half, :], bank(7 - half), ACT.Copy).then_inc(S("R_ready"), 1)
                qk_evac(n + 2)
                act.wait_ge(S("x1_done"), n + 1)
                act.wait_ge(S("wo_done"), n + 1)
                act.activation(share[:, :], bank(6, 2), ACT.Copy).then_inc(S("share_ready"), 1)

            act.wait_ge(S("bin_done"), 1)
            act.activation(w1T[:, :], bank(0), ACT.Copy).then_inc(S("bin_turned"), 1)
            act.activation(w2T[:, :, :].rearrange("p t d -> p (t d)"), bank(1), ACT.Copy).then_inc(S("bin_turned"), 1)
            first_root(rstd[:, :], ve[:, :], rms2[:, :], 3)
            act.wait_ge(S("x1_done"), 1 + STEPS)
            act.wait_ge(S("l1_zero"), 1)

            def cp(s, out, src, done, after=None, func=ACT.Copy, **kw):
                if after:
                    act.wait_ge(S(after), count(after, s))
                ins = act.activation(out, src, func, **kw)
                if done:
                    ins.then_inc(S(done), 1)

            def spread(s, dst, src, done, after):
                act.wait_ge(S(after), count(after, s))
                for q in range(NB):
                    r = slice(q * SUB, (q + 1) * SUB)
                    ins = act.activation(dst[r, :, q * SUB:(q + 1) * SUB], src[r, :, :], ACT.Copy)
                ins.then_inc(S(done), 1)

            def f_x1T(s):
                cp(s, x1T[:, :], bank(0), "x1T_ready", "xn1_turned")
                act.activation(qkv_in[:, :, :, 0:3].rearrange("p i g k -> p (i g) k"),
                               qkv_in[:, :, :, P:P + 3].rearrange("p i g k -> p (i g) k"), ACT.Copy).then_inc(S("halo_ready"), 1)

            def f_qkv(s):
                act.wait_ge(S("halo_ready"), count("halo_ready", s))
                for i in range(3):
                    act.wait_ge(S(f"qkv{i}_done"), count(f"qkv{i}_done", s))
                    act.activation(cy[:, i, :, :], bank(1 + i).rearrange("p (g t) -> p g t", g=B), ACT.Copy,
                                   scale=conv_w[:, i, 3:4])
                    act.activation(qkv_in[:, i, :, 3:], bank(1 + i).rearrange("p (g t) -> p g t", g=B),
                                   ACT.Copy).then_inc(S(f"qkv{i}_ready"), 1)

            def f_sigmoid_e(s):
                cp(s, sg[:, :, :], ctl[:, :, :], "sg_e", "ctl_ready", ACT.Exp, scale=-1.0)
                for i in range(3):
                    cp(s, ce[:, i, :, :], ce[:, i, :, :], f"ce{i}_e", f"conv{i}_done", ACT.Exp, scale=-1.0)

            def f_sigmoid_l(s):
                cp(s, ctl[:, :, :], sg[:, :, :], "sg_l", "sg_e", ACT.Ln, bias=1.0)
                for i in range(3):
                    cp(s, ce[:, i, :, :], ce[:, i, :, :], f"ce{i}_l", f"ce{i}_e", ACT.Ln, bias=1.0)

            def f_sigmoid_s(s):
                cp(s, sg[:, :, :], ctl[:, :, :], "sg_ready", "sg_l", ACT.Exp, scale=-1.0)
                for i in range(3):
                    cp(s, ce[:, i, :, :], ce[:, i, :, :], f"ce{i}_s", f"ce{i}_l", ACT.Exp, scale=-1.0)

            def f_decay(s, p):
                cp(s, gam[:, :, :].rearrange("p g j -> p (g j)"), bank(0), "gam_ready", "gam_summed", ACT.Exp)
                cp(s, dec[:, p, :], bank(1)[:, 0:48], "dec_ready", "dec_summed", ACT.Exp)

            def f_hidden(s, ts):
                for t in ts:
                    cp(s, hT[:, t, :], bank(2 + t % 2), f"h{t}_ready", f"ffn{t}_done", ACT.Gelu, bias=b1col[:, t:t + 1])

            def f_logs(s):
                cp(s, la, al[:, :, :], "la_ready", "al_ready", ACT.Ln)
                cp(s, rt[:, :, :], ss[:, :, :], "rn_l", "ss_ready", ACT.Ln)
                cp(s, rn[:, :, :], rt[:, :, :], "rn_e", "rn_l", ACT.Exp, scale=-0.5)

            def f_keys(s):
                cp(s, kqT[:, :, 0, :], bank(0).rearrange("p (g t) -> p g t", g=B), "kT_ready", "kn_turned")
                cp(s, kqT[:, :, 1, :], bank(1).rearrange("p (g t) -> p g t", g=B), "qT_ready", "qn_turned")

            def b_first(s, p):
                spread(s, Bx[:, 0, :, :], Bm[:, 0, :, :], "Bx0_ready", "Bm0_ready")

            def join_copy(s, k, x):
                c, half = "ab"[x], slice(x * GH // 2, (x + 1) * GH // 2)
                cp(s, Yc[:, half, :].rearrange("p g j -> p (g j)"), bank(4 + x)[:, 0:256], f"Y{k}{c}_ready", f"Y{k}{c}_done")

            def b_join(s, k):
                join_copy(s, k, 0)
                join_copy(s, k, 1)
                if k < 3:
                    spread(s, Bx[:, (k + 1) % 2, :, :], Bm[:, k + 1, :, :], f"Bx{k + 1}_ready", f"Bm{k + 1}_ready")

            def b_w(s):
                for x, c in enumerate("ab"):
                    half = slice(x * GH // 2, (x + 1) * GH // 2)
                    cp(s, Wv[:, half, :].rearrange("p g j -> p (g j)"), bank(6 + x), f"Wv{c}_ready", f"W{c}_done")

            def b_mo(s):
                cp(s, MoT[:, :, :].rearrange("p g t -> p (g t)"), bank(6), "MoT_ready", "Mo_turned")

            def b_maps(s):
                act.wait_ge(S("Ac_ready"), count("Ac_ready", s))
                for h in range(H1):
                    r = slice(h * E1, (h + 1) * E1)
                    ins = act.activation(Ax[r, :, :, h * E1:(h + 1) * E1].rearrange("p q g e -> p (q g) e"),
                                         Ac[r, :, :, :].rearrange("p q g e -> p (q g) e"), ACT.Copy)
                ins.then_inc(S("Ax_ready"), 1)

            def round_of(s, p, ahead):
                spread(s, Px[:, :, :], Pc[:, p, :, :], "Px_ready", "Pc_ready")
                if ahead:
                    f_x1T(s + 1)
                b_join(s, 1)
                if ahead:
                    f_qkv(s + 1)
                b_join(s, 2)
                if ahead:
                    f_sigmoid_e(s + 1)
                b_join(s, 3)
                if ahead:
                    f_sigmoid_l(s + 1)
                    f_sigmoid_s(s + 1)
                b_w(s)
                if ahead:
                    f_hidden(s + 1, range(FT - 1))
                b_mo(s)
                if ahead:
                    f_hidden(s + 1, (FT - 1,))
                    f_logs(s + 1)
                    f_decay(s + 1, 1 - p)
                    f_keys(s + 1)
                b_maps(s)
                if ahead:
                    b_first(s + 1, 1 - p)
                cp(s, rrt[:, :], rss[:, :], "rrs_l", "rss_ready", ACT.Ln)
                if ahead:
                    join_copy(s + 1, 0, 0)
                cp(s, rrs[:, :], rrt[:, :], "rrs_e", "rrs_l", ACT.Exp, scale=-0.5)
                if ahead:
                    join_copy(s + 1, 0, 1)
                if ahead:
                    spread(s + 1, Bx[:, 1, :, :], Bm[:, 1, :, :], "Bx1_ready", "Bm1_ready")
                cp(s, rdT[:, :, :].rearrange("p g t -> p (g t)"), bank(1), "rdT_ready", "rd_turned")

            f_x1T(0)
            f_qkv(0)
            f_sigmoid_e(0)
            f_sigmoid_l(0)
            f_sigmoid_s(0)
            f_hidden(0, range(FT))
            f_logs(0)
            f_decay(0, 0)
            f_keys(0)
            act.wait_ge(S("l1_zero"), 2)
            b_first(0, 0)
            b_join(0, 0)
            with act.Fori(0, NT // 2 - 1) as i:
                round_of(i * 2, 0, True)
                round_of(i * 2 + 1, 1, True)
            round_of(NT - 2, 0, True)
            round_of(NT - 1, 1, False)

        @block.tensor
        def _(pe):
            pe.wait_ge(S("ident_set"), 1)
            pe.wait_ge(S("w3_loaded"), 48)
            for i in range(3):
                ins = pe.transpose(bank(0)[:, i * P:(i + 1) * P], w3[:, i, :], ident[:, :])
            ins.then_inc(S("w3_turned"), 1)
            pe.wait_ge(S("wv_loaded"), 32)
            pe.wait_ge(S("w3T_ready"), 1)

            def turn(i):
                if not isinstance(i, int) or i:
                    pe.wait_ge(S("xT_ready"), i)
                    pe.wait_ge(S("tS_ready"), i)
                pe.wait_ge(S("xn_ready"), i + 1)
                for t in range(4):
                    ins = pe.transpose(bank(0)[:, t * P:(t + 1) * P], xn[:, t, :], ident[:, :])
                ins.then_inc(S("xn_turned"), 1)
                pe.wait_ge(S("tn_ready"), i + 1)
                for t in range(4):
                    ins = pe.transpose(bank(1)[:, t * P:(t + 1) * P], tn[:, t, :], ident[:, :])
                ins.then_inc(S("tn_turned"), 1)

            def gates(i, qd):
                pe.wait_ge(S("tS_ready"), i + 1)
                for t in range(4):
                    ins = pe.matmul(bank(5)[:, t * H:(t + 1) * H], tS[:, qd, t * P:(t + 1) * P], wg_sb[:, :],
                                    start=True, stop=True)
                ins.then_inc(S("gates_done"), 1)

            def group(i, qd, ahead=True):
                pe.wait_ge(S("xrk_ready"), i + 1)
                pe.matmul(bank(2), w3T[:, 1, :], xk, start=True, stop=True).then_inc(S("k_done"), 1)
                for t in range(4):
                    ins = pe.matmul(bank(3)[:, t * P:(t + 1) * P], xr[:, t * P:(t + 1) * P], w3T[:, 0, :],
                                    start=True, stop=True)
                ins.then_inc(S("r_done"), 1)
                if ahead:
                    turn(i + 1)
                else:
                    pe.wait_ge(S("V_odd"), i * 2)
                    pe.wait_ge(S("fo_ready"), i)
                for t in range(4):
                    if t >= 2:
                        pe.wait_ge(S("V_odd" if t % 2 else "V_even"), i * 2 + 1)
                    pe.matmul(bank(6 + t % 2), tS[:, qd, t * P:(t + 1) * P],
                              wv_sb[:, :, :].rearrange("p h e -> p (h e)"), start=True, stop=True).then_inc(S("v_done"), 1)
                pe.wait_ge(S("ka_ready"), i + 1)
                for t in range(4):
                    ins = pe.matmul(bank(4)[:, t * P:(t + 1) * P], ka[:, t * P:(t + 1) * P], w3T[:, 2, :],
                                    start=True, stop=True)
                ins.then_inc(S("v2_done"), 1)
                if ahead:
                    gates(i + 1, 1 - qd)

            turn(0)
            gates(0, 0)
            with pe.Fori(0, B - 1) as b:
                group(b * 2, 0)
                group(b * 2 + 1, 1)
            group(QUADS - 2, 0)
            group(QUADS - 1, 1, False)

            def project(i, c_first):
                b_next = i // PAIRS
                for c in range(2):
                    ins = pe.matmul(bank(2 * c_first + c), wqk[:, c_first, :],
                                    TT[:, ds(b_next * N + c * 512, 512)], start=True, stop=True)
                return ins

            pe.wait_ge(S("V_even"), TILES // 2)
            pe.wait_ge(S("V_odd"), TILES // 2)
            pe.wait_ge(S("TT_ready"), QUADS)
            pe.wait_ge(S("x_ffn"), QUADS)
            pe.wait_ge(S("causal_set"), 2)
            pe.wait_ge(S("wo_loaded"), 16)
            pe.wait_ge(S("wqk_loaded"), 32)
            for c, done in ((0, "q_proj_done"), (1, "proj_done")):
                for j in range(2):
                    ins = pe.matmul(bank(2 * c + j), wqk[:, c, :], TT[:, j * 512:(j + 1) * 512], start=True, stop=True)
                ins.then_inc(S(done), 1)
            with pe.Fori(0, STEPS) as n:
                nxt = pe.snap((n + 1) % STEPS)
                pr = pe.snap(n % PAIRS)
                for k in range(UNITS + 3):
                    if k < UNITS:
                        ib, hh = divmod(k, 2)
                        if k == 0:
                            pe.wait_ge(S("qk_act"), n + 1)
                            pe.wait_ge(S("qk_dve"), n + 1)
                        if k >= 2:
                            pe.wait_ge(S("exp_done"), n * UNITS + (k - 1))
                        for c in range(ib // 4 + 1):
                            w = min(512, (ib + 1) * P - c * 512)
                            last = c == ib // 4
                            ins = pe.matmul(bank(2 * (k % 2) + c)[:, 0:w], Qp[:, hh, ib * P:(ib + 1) * P],
                                            K[:, c * 512:c * 512 + w], start=True, stop=not last)
                        d0 = (ib % 4) * P
                        ins = pe.matmul(bank(2 * (k % 2) + ib // 4)[:, d0:d0 + P], identb[:, :], causal[:, :],
                                        start=False, stop=True)
                        ins.then_inc(S("scores_done"), 1)
                    if 2 <= k < UNITS + 2:
                        u = k - 2
                        if u > 0:
                            pe.wait_ge(S("PT_lo"), n * UNITS + u)
                            if u - 1 >= 8:
                                pe.wait_ge(S("PT_hi"), n * 8 + (u - 8))
                        pe.wait_ge(S("exp_done"), n * UNITS + (u + 1))
                        for j in range(u // 2 + 1):
                            ins = pe.transpose(bank(4 + j // 4)[:, (j % 4) * P:(j % 4 + 1) * P],
                                               Pbuf[:, u % 4, j * P:(j + 1) * P], ident[:, :])
                        ins.then_inc(S("PT_turned"), 1)
                    if k == UNITS:
                        pe.wait_ge(S("wqk_loaded"), n * 32 + 64)
                        pe.wait_ge(S("exp_done"), n * UNITS + (UNITS - 1))
                        project(nxt, 0).then_inc(S("q_proj_done"), 1)
                    if k == UNITS + 1:
                        project(nxt, 1).then_inc(S("proj_done"), 1)
                    if k in (10, UNITS + 1):
                        half = int(k != 10)
                        pe.wait_ge(S("Sx_ready"), n * 2 + (half + 1))
                        if half:
                            pe.wait_ge(S("OT_ready"), n * 2 + 1)
                        for t in range(4):
                            ins = pe.transpose(bank(7 - half)[:, t * P:(t + 1) * P],
                                               Sx[:, t, :, :].rearrange("p h e -> p (h e)"), ident[:, :])
                        ins.then_inc(S("R_turned"), 1)
                    if 3 <= k:
                        u = k - 3
                        ib, hh = divmod(u, 2)
                        pe.wait_ge(S("causal_set"), 2)
                        if u == 0:
                            pe.wait_ge(S("Vp_ready"), n + 1)
                            pe.wait_ge(S("share_ready"), n + 1)
                        if u == 8:
                            pe.wait_ge(S("R_ready"), n * 2 + 1)
                        pe.wait_ge(S("PT_lo"), n * UNITS + (u + 1))
                        if u >= 8:
                            pe.wait_ge(S("PT_hi"), n * 8 + (u - 7))
                        for j in range(ib + 1):
                            ins = pe.matmul(bank(6 + ib // 4)[64 * hh:64 * hh + 64, (ib % 4) * P:(ib % 4 + 1) * P],
                                            Vp[:, j, 64 * hh:64 * hh + 64], PT[:, u % 2, j * P:(j + 1) * P],
                                            start=(j == 0), stop=(j == ib))
                        ins.then_inc(S("pv_done"), 1)
                pe.wait_ge(S("R_ready"), n * 2 + 2)
                for ib in range(NT):
                    if ib % 4 == 0:
                        pe.wait_ge(S("OT_ready"), n * 2 + (ib // 4 + 1))
                    ins = pe.matmul(bank(6 + ib // 4)[:, (ib % 4) * P:(ib % 4 + 1) * P], OT[:, ib * P:(ib + 1) * P],
                                    wo_sb[:, ds(pr, 1), :].rearrange("p a d -> p (a d)"), start=True, stop=True)
                ins.then_inc(S("wo_done"), 1)

            pe.wait_ge(S("bin_ready"), 1)
            pe.wait_ge(S("qk_act"), STEPS + 1)
            pe.wait_ge(S("qk_dve"), STEPS + 1)
            for i in range(2):
                for t in range(FT):
                    ins = pe.transpose(bank(i)[:, t * P:(t + 1) * P], w12[:, i, t * P:(t + 1) * P], ident[:, :])
            ins.then_inc(S("bin_done"), 1)
            pe.wait_ge(S("l1_loaded"), 16 * L1_LOADS)
            pe.wait_ge(S("bin_turned"), 2)
            pe.wait_ge(S("l1_zero"), 1)

            def wait(s, *names):
                for name in names:
                    pe.wait_ge(S(name), count(name, s))

            def wait_small(s, *names):
                pe.wait_ge(S("l1_zero"), 1)
                wait(s, *names)

            def f_xn(s):
                wait(s, "xn1_ready")
                for g in range(B):
                    ins = pe.transpose(bank(0)[:, g * P:(g + 1) * P], xn1[:, g, :], ident[:, :])
                ins.then_inc(S("xn1_turned"), 1)

            def f_qkv(s):
                wait(s, "x1T_ready")
                for i in range(3):
                    if i == 1 and not (isinstance(s, int) and s == 0):
                        pe.wait_ge(S("out_read"), s)
                    pe.matmul(bank(1 + i), w_in[:, i * D:(i + 1) * D], x1T[:, :], start=True, stop=True).then_inc(S(f"qkv{i}_done"), 1)

            def f_control(s):
                wait(s, "qkv0_ready")
                for g in range(B):
                    ins = pe.matmul(bank(g // 2)[:, (g % 2) * CT:(g % 2 + 1) * CT], x1T[:, g * P:(g + 1) * P],
                                    w_ctrl[:, :], start=True, stop=True)
                ins.then_inc(S("ctrl_done"), 1)

            def f_hidden(s, t):
                wait(s, f"qkv{t + 1}_ready" if t < 2 else f"h{t - 2}_ready")
                if t == 3:
                    wait(s, "v_tok_ready")
                pe.matmul(bank(2 + t % 2), w1T[:, t * P:(t + 1) * P], x1T[:, :], start=True, stop=True).then_inc(S(f"ffn{t}_done"), 1)

            def f_decay(s):
                wait(s, "laG_ready", "tok_ready")
                pe.matmul(bank(0), upto, laG[:, :, :].rearrange("p g j -> p (g j)"), start=True, stop=True).then_inc(S("gam_summed"), 1)
                pe.matmul(bank(1)[:, 0:P], upto, la_wide[:, :], start=True, stop=True)
                pe.matmul(bank(1)[:, 16:16 + P], beyond, la_wide[:, :], start=True, stop=True)
                wait(s, "laX_ready")
                for g in range(B):
                    ins = pe.matmul(bank(1)[:, 32 + g * NB:32 + g * NB + P], laX[:, g, :], masks[:, 2 * P:3 * P],
                                    start=True, stop=True)
                ins.then_inc(S("dec_summed"), 1)

            def f_tokens(s, those):
                for i in those:
                    wait(s, f"silu{i}_ready", "h1_ready" if i == 2 else "ctl_raw")
                    for g in range(B):
                        ins = pe.transpose(bank(i + i // 2)[:, g * P:(g + 1) * P], cy[:, i, g, :], ident[:, :])
                    ins.then_inc(S(f"tok{i}_turned"), 1)

            def b_ffn_out(s, part, ahead):
                if part == 0:
                    wait(s, "h3_ready")
                    if ahead:
                        wait(s + 1, "ctl_raw")
                for g in (2 * part, 2 * part + 1):
                    for t in range(FT):
                        ins = pe.matmul(bank(0)[:, g * P:(g + 1) * P], hT[:, t, g * P:(g + 1) * P], w2T[:, t, :],
                                        start=(t == 0), stop=(t == FT - 1))
                if part == 1:
                    ins.then_inc(S("ffn_out"), 1)

            def f_keys(s):
                wait(s, "kn_ready", "gam_ready", "dec_ready", "h3_ready")
                for i, name in ((1, "kn_turned"), (0, "qn_turned")):
                    for g in range(B):
                        ins = pe.transpose(bank(1 - i)[:, g * P:(g + 1) * P], qk_n[:, i, g, :], ident[:, :])
                    ins.then_inc(S(name), 1)

            def f_kk(s, g):
                if g == 0:
                    wait_small(s, "kT_ready", "qT_ready", "v_tok_ready")
                for q in range(NB):
                    for h in range(H1):
                        r, c = slice(h * E1, (h + 1) * E1), slice(q * SUB, (q + 1) * SUB)
                        ins = pe.matmul(bank(h)[c, g * 64:(g + 1) * 64].rearrange("p (a j) -> p a j", a=2),
                                        kqT[r, g, 0, c], kqT[r, g, :, c], start=True, stop=True)
                if g == B - 1:
                    ins.then_inc(S("kk_done"), 1)

            def systems(at, lhs, rhs, x):
                flat = rhs.rearrange("p i j -> p (i j)")
                n, first, last = rhs.shape[2], x * GH // 2, (x + 1) * GH // 2
                for i in range(first, last):
                    m = min(P, (last - i) * n)
                    c = (i - first) * n
                    ins = pe.matmul(bank(at)[:, c:c + m], lhs[:, i, :], flat[:, i * n:i * n + m],
                                    start=True, stop=True)
                return ins

            def b_first(s, opened):
                if opened:
                    wait(s - 1, "rd_ready")
                b_y(s, 0)
                b_zy(s, 0)

            def b_y(s, k):
                for x, c in enumerate("ab"):
                    wait(s, f"Bx{k}_ready", f"Z{k}{c}_ready" if k else "Z0_ready")
                    systems(4 + x, Bx[:, k % 2, :, :], Zc[:, k % 2, :, :], x).then_inc(S(f"Y{k}{c}_done"), 1)

            def b_zy(s, k):
                for x, c in enumerate("ab"):
                    wait(s, f"Y{k}{c}_ready", f"Tx{k}{c}_ready" if k else "Tx0_ready")
                    systems(6 + x, Tx[:, :, :], Yc[:, :, :], x).then_inc(S(f"ZY{k}{c}_done"), 1)

            def b_w(s, p):
                wait(s, "Rv_ready", "acc_ready")
                for x, c in enumerate("ab"):
                    wait(s, f"Tx4{c}_ready")
                    systems(6 + x, Tx[:, :, :], Rv[:, p, :, :], x).then_inc(S(f"W{c}_done"), 1)

            def b_pw(s):
                wait(s, "Px_ready")
                for x, c in enumerate("ab"):
                    wait(s, f"Wv{c}_ready")
                    systems(4 + x, Px[:, :, :], Wv[:, :, :], x).then_inc(S(f"PW{c}_done"), 1)

            def b_mo(s):
                for x, c in enumerate("ab"):
                    wait(s, f"Mo{c}_ready")
                    for g in range(x * B // 2, (x + 1) * B // 2):
                        ins = pe.transpose(bank(6)[:, g * P:(g + 1) * P], Mo[:, g * H1:(g + 1) * H1, :].rearrange("p h e -> p (h e)"), ident[:, :])
                ins.then_inc(S("Mo_turned"), 1)

            def b_ab(s, p):
                wait_small(s, "Kd_ready", "MoT_ready", "Ov_ready")
                for g in range(B):
                    for h in range(H1):
                        for q in range(NB):
                            r, c = slice(q * SUB, (q + 1) * SUB), slice(h * E1, (h + 1) * E1)
                            ins = pe.matmul(bank(4 + q)[c, g * 64:(g + 1) * 64], Kd[r, p, g * H1 + h, :], Wv[r, g * H1 + h, :],
                                            start=True, stop=True)
                ins.then_inc(S("AB_done"), 1)

            def b_state(s, q):
                if q == 0:
                    wait(s, "Ax_ready", "Bc_ready")
                wait(s, f"St{q}_ready")
                flat = St[:, :, :, :].rearrange("p q g j -> p (q g j)")
                for g in range(B):
                    at = (q * B + g) * SUB
                    ins = pe.matmul(bank(4)[:, g * SUB:g * SUB + P], Ax[:, q, g, :], flat[:, at:at + P], start=True, stop=True)
                ins.then_inc(S(f"AS{q}_done"), 1)

            def b_ms(s):
                wait_small(s, "MoT_ready", "St4_ready")
                for g in range(B):
                    for q in range(NB):
                        for h in range(H1):
                            r, c = slice(h * E1, (h + 1) * E1), slice(q * SUB, (q + 1) * SUB)
                            ins = pe.matmul(bank(4 + h)[c, g * SUB:(g + 1) * SUB], MoT[r, g, c], St[r, q, g, :],
                                            start=True, stop=True)
                ins.then_inc(S("MS_done"), 1)

            def b_out(s):
                wait(s, "rdn_ready")
                for g in range(B):
                    ins = pe.transpose(bank(1)[:, g * P:(g + 1) * P], rdn[:, g, :], ident[:, :])
                ins.then_inc(S("rd_turned"), 1)
                wait(s, "rdT_ready")
                for g in range(B):
                    ins = pe.matmul(bank(2)[:, g * P:(g + 1) * P], rdT[:, g, :], w_out[:, :], start=True, stop=True)
                ins.then_inc(S("out_done"), 1)

            def round_of(s, p, ahead):
                if ahead:
                    f_xn(s + 1)
                b_y(s, 1)
                if ahead:
                    f_qkv(s + 1)
                b_zy(s, 1)
                if ahead:
                    f_control(s + 1)
                    f_hidden(s + 1, 0)
                b_y(s, 2)
                if ahead:
                    f_hidden(s + 1, 1)
                b_zy(s, 2)
                b_ffn_out(s, 0, ahead)
                b_y(s, 3)
                b_ffn_out(s, 1, ahead)
                b_zy(s, 3)
                b_w(s, p)
                if ahead:
                    f_tokens(s + 1, (0, 1))
                b_pw(s)
                if ahead:
                    f_tokens(s + 1, (2,))
                    f_hidden(s + 1, 2)
                b_mo(s)
                if ahead:
                    f_hidden(s + 1, 3)
                b_ab(s, p)
                if ahead:
                    f_decay(s + 1)
                    f_keys(s + 1)
                    f_kk(s + 1, 0)
                for q in range(NB):
                    b_state(s, q)
                    if ahead and q < NB - 1:
                        f_kk(s + 1, q + 1)
                b_ms(s)
                if ahead:
                    b_first(s + 1, True)
                b_out(s)

            f_xn(0)
            f_qkv(0)
            f_control(0)
            f_hidden(0, 0)
            f_hidden(0, 1)
            f_tokens(0, range(3))
            f_hidden(0, 2)
            f_hidden(0, 3)
            f_decay(0)
            f_keys(0)
            for g in range(B):
                f_kk(0, g)
            b_first(0, False)
            with pe.Fori(0, NT // 2 - 1) as i:
                round_of(i * 2, 0, True)
                round_of(i * 2 + 1, 1, True)
            round_of(NT - 2, 0, True)
            round_of(NT - 1, 1, False)

        @block.vector
        def _(v):
            def row_moments(name, raw="stats_raw"):
                even, odd = stats[:, :, 1], stats[:, :, 4]
                v.wait_ge(S(raw), B)
                v.tensor_tensor(mean[:, :], even, odd, ALU.add).then_inc(S(name), 1)
                v.tensor_tensor(ve[:, :], even, odd, ALU.subtract).then_inc(S(name), 1)
                v.tensor_tensor(rms2[:, :], stats[:, :, 2], stats[:, :, 5], ALU.add).then_inc(S(name), 1)
                v.wait_ge(S(name), 2)
                v.tensor_scalar(mean[:, :], mean[:, :], 0.5, None, ALU.mult)
                v.scalar_tensor_tensor(ve[:, :], ve[:, :], 0.25, ve[:, :], ALU.mult, ALU.mult).then_inc(S(name), 1)
                v.wait_ge(S(name), 4)
                v.scalar_tensor_tensor(var[:, :], rms2[:, :], 1.0 / D, ve[:, :], ALU.mult, ALU.add).then_inc(S("stats_done"), 1)

            def tile_stats(q, name):
                moments, rows = stats[:, ds(q * NT, NT), :], X[:, ds(q * NT, NT), :]
                for t in range(NT):
                    ins = v.bn_stats(moments[:, t, :], rows[:, t, :])
                ins.then_inc(S(name), 1)

            def refine_root(y, x, t, nth):
                v.wait_ge(S("root_exp"), nth)
                v.tensor_tensor(t, y, y, ALU.mult).then_inc(S("root_step"), 1)
                v.wait_ge(S("root_step"), nth * 3 - 2)
                v.scalar_tensor_tensor(t, t, -0.5, x, ALU.mult, ALU.mult).then_inc(S("root_step"), 1)
                v.wait_ge(S("root_step"), nth * 3 - 1)
                v.scalar_tensor_tensor(y, t, 1.5, y, ALU.add, ALU.mult).then_inc(S("root_step"), 1)
                v.wait_ge(S("root_step"), nth * 3)

            v.wait_ge(S("x_loaded"), 16 * B)
            with v.Fori(0, B) as q:
                tile_stats(q, "stats_raw")
            row_moments("row_step")
            v.wait_ge(S("stats_done"), 1)
            v.tensor_scalar(ve[:, :], var[:, :], EPS_LN, None, ALU.add).then_inc(S("root_in"), 1)
            refine_root(rstd[:, :], ve[:, :], rms2[:, :], 1)
            v.tensor_tensor(rms2[:, :], rstd[:, :], rstd[:, :], ALU.mult).then_inc(S("rms_step"), 1)
            v.wait_ge(S("rms_step"), 1)
            v.tensor_tensor(ve[:, :], rms2[:, :], var[:, :], ALU.mult).then_inc(S("rms_step"), 1)
            v.wait_ge(S("rms_step"), 2)
            v.tensor_scalar(ve[:, :], ve[:, :], EPS_RMS, None, ALU.add).then_inc(S("root_in"), 1)
            refine_root(rrms[:, :], ve[:, :], rms2[:, :], 2)
            v.wait_ge(S("rms_loaded"), 16)
            v.wait_ge(S("mu_loaded"), 32)

            def normalise(i):
                rows = X[:, ds(i * 4, 4), :]
                means, scales, rms_scales = mean[:, ds(i * 4, 4)], rstd[:, ds(i * 4, 4)], rrms[:, ds(i * 4, 4)]
                for t in range(4):
                    ins = v.tensor_scalar(xn[:, t, :], rows[:, t, :], means[:, t:t + 1], scales[:, t:t + 1],
                                          ALU.subtract, ALU.mult)
                ins.then_inc(S("xn_ready"), 1)
                v.wait_ge(S("xn_ready"), i + 1)
                for t in range(4):
                    ins = v.tensor_scalar(tn[:, t, :], xn[:, t, :], rms_scales[:, t:t + 1], None, ALU.mult)
                ins.then_inc(S("tn_ready"), 1)

            def turned_t(i, qd):
                v.wait_ge(S("tn_turned"), i + 1)
                v.tensor_scalar(tS[:, qd, :], bank(1), rms_w[:, 0:1], None, ALU.mult).then_inc(S("tS_ready"), 1)

            def values(i, k):
                v.wait_ge(S("v_done"), i * 4 + (k * 2 + 2))
                v.tensor_copy(V[:, ds(i * 4 + (k * 2 + 1), 1), :].rearrange("p a n -> p (a n)"),
                              bank(7)).then_inc(S("V_odd"), 1)

            def mixed(i, qd):
                v.wait_ge(S("shift_ready"), i + 1)
                v.scalar_tensor_tensor(xr, xT[:, qd, 1:513], mu[:, 0:1], tmr, ALU.mult, ALU.add)
                v.scalar_tensor_tensor(xk, xT[:, qd, 1:513], mu[:, 2:3], tmk, ALU.mult, ALU.add).then_inc(S("xrk_ready"), 1)

            def group(i, qd, ahead=True):
                if ahead:
                    normalise(i + 1)
                v.wait_ge(S("gates_done"), i + 1)
                v.tensor_scalar(eg[:, qd, :], bank(5)[:, 0:32], Z_MIN, None, ALU.max).then_inc(S("z_ready"), 1)
                v.wait_ge(S("r_done"), i + 1)
                v.tensor_scalar(er, bank(3), Z_MIN, None, ALU.max).then_inc(S("z_ready"), 1)
                if ahead:
                    turned_t(i + 1, 1 - qd)
                values(i, 0)
                if ahead:
                    mixed(i + 1, 1 - qd)
                values(i, 1)
                v.wait_ge(S("z_sigmoid"), i * 2 + 1)
                v.wait_ge(S("v2_done"), i + 1)
                v.tensor_tensor(fo, bank(4), er, ALU.mult).then_inc(S("fo_ready"), 1)
                v.wait_ge(S("fo_ready"), i + 1)
                v.tensor_tensor(X[:, ds(i * 4, 4), :], X[:, ds(i * 4, 4), :], fo.rearrange("p (t d) -> p t d", t=4),
                                ALU.add).then_inc(S("x_ffn"), 1)
                v.wait_ge(S("z_sigmoid"), i * 2 + 2)
                v.tensor_scalar(G[:, ds(i * 4, 4), :], eg[:, qd, :].rearrange("p (t h) -> p t h", t=4), 1.0, None,
                                ALU.mult).then_inc(S("G_ready"), 1)

            normalise(0)
            turned_t(0, 0)
            mixed(0, 0)
            with v.Fori(0, B - 1) as b:
                group(b * 2, 0)
                group(b * 2 + 1, 1)
            group(QUADS - 2, 0)
            group(QUADS - 1, 1, False)

            v.wait_ge(S("w12_loaded"), 32)
            v.tensor_reduce(alpha[:, 0:FT], w12[:, 0, :].rearrange("p (t d) -> p t d", t=FT), AX.X, ALU.add,
                            apply_absolute_value=True)
            v.tensor_reduce(alpha[:, FT:FT + 1], w12[:, 1, :], AX.X, ALU.add, apply_absolute_value=True).then_inc(S("alpha_sum"), 1)
            v.wait_ge(S("alpha_sum"), 1)
            v.tensor_scalar(alpha[:, 0:FT], alpha[:, 0:FT], 1.0 / D, None, ALU.mult).then_inc(S("alpha_ready"), 1)
            v.tensor_scalar(alpha[:, FT:FT + 1], alpha[:, FT:FT + 1], 1.0 / (FT * P), None, ALU.mult).then_inc(S("alpha_ready"), 1)
            v.wait_ge(S("sign_ready"), 3)
            v.tensor_scalar(ramp[:, :], ramp[:, :], 1.0, None, ALU.add).then_inc(S("ramp_step"), 1)
            v.wait_ge(S("ramp_step"), 1)
            v.reciprocal(ramp[:, :], ramp[:, :]).then_inc(S("ramp_ready"), 1)

            def copy_v(i, pr):
                v.tensor_scalar(Vp[:, :, :], V[:, ds((i // PAIRS) * NT, NT), ds(pr * 2 * E, 2 * E)], 1.0, None,
                                ALU.mult).then_inc(S("Vp_ready"), 1)

            v.wait_ge(S("V_even"), TILES // 2)
            v.wait_ge(S("V_odd"), TILES // 2)
            v.tensor_scalar(Vp[:, :, :], V[:, 0:NT, 0:2 * E], 1.0, None, ALU.mult).then_inc(S("Vp_ready"), 1)
            v.wait_ge(S("proj_done"), 1)
            v.tensor_copy(K[:, :], bank(2, 2)).then_inc(S("qk_dve"), 1)
            v.wait_ge(S("x_ffn"), QUADS)
            v.memset(gs[:, 0, 0:1], 0.0).then_inc(S("x1_done"), 1)
            with v.Fori(0, B) as batch:
                tile0 = v.snap(batch * NT)
                with v.Fori(0, PAIRS) as pr:
                    n = v.snap(batch * PAIRS + pr)
                    nxt = v.snap((n + 1) % STEPS)
                    nxt_pair = v.snap((n + 1) % PAIRS)
                    for k in range(UNITS + 2):
                        if k < UNITS:
                            W = (k // 2 + 1) * P
                            v.wait_ge(S("scores_done"), n * UNITS + (k + 1))
                            v.tensor_reduce(nb[:, k:k + 1], bank(2 * (k % 2), 2)[:, 0:W], AX.X, ALU.max,
                                            negate=True).then_inc(S("max_ready"), 1)
                        if k >= 2:
                            u = k - 2
                            W = min(512, (u // 2 + 1) * P)
                            if u >= 2:
                                v.wait_ge(S("pv_done"), n * UNITS + (u - 1))
                            v.wait_ge(S("PT_turned"), n * UNITS + (u + 1))
                            v.tensor_copy(PT[:, u % 2, 0:W], bank(4)[:, 0:W]).then_inc(S("PT_lo"), 1)
                        if k in (9, UNITS + 1):
                            half = int(k != 9)
                            v.wait_ge(S("exp_done"), n * UNITS + (8 * half + 8))
                            v.reciprocal(rinv[:, 8 * half:8 * half + 8], rs[:, 8 * half:8 * half + 8]).then_inc(S("gs_step"), 1)
                            v.wait_ge(S("gs_step"), n * 4 + (2 * half + 1))
                            v.tensor_tensor(gs[:, :, :], rinv[:, 8 * half:8 * half + 8].rearrange("p (t h) -> p t h", h=2),
                                            G[:, ds(tile0 + 4 * half, 4), ds(pr * 2, 2)], ALU.mult).then_inc(S("gs_step"), 1)
                            v.wait_ge(S("gs_step"), n * 4 + (2 * half + 2))
                            v.tensor_copy(Sx[:, :, :, :], gs[:, :, :].unsqueeze(3).to_broadcast([P, 4, 2, E])).then_inc(S("Sx_ready"), 1)
                        if k == 12:
                            v.wait_ge(S("pv_done"), n * UNITS + 8)
                            v.wait_ge(S("R_ready"), n * 2 + 1)
                            v.tensor_tensor(OT[:, 0:512], bank(6), R[:, 0, :], ALU.mult).then_inc(S("OT_ready"), 1)
                    v.wait_ge(S("proj_done"), n + 2)
                    v.tensor_copy(K[:, :], bank(2, 2)).then_inc(S("qk_dve"), 1)
                    v.wait_ge(S("pv_done"), n * UNITS + UNITS)
                    v.wait_ge(S("R_ready"), n * 2 + 2)
                    v.tensor_tensor(OT[:, 512:1024], bank(7), R[:, 1, :], ALU.mult).then_inc(S("OT_ready"), 1)
                    copy_v(nxt, nxt_pair)
                v.wait_ge(S("x1_done"), batch * PAIRS + (PAIRS + 1))
                tile_stats(batch, "stats_raw2")

            v.wait_ge(S("x1_done"), 1 + STEPS)
            row_moments("row_step2", "stats_raw2")
            v.wait_ge(S("stats_done"), 2)
            v.tensor_scalar(ve[:, :], var[:, :], EPS_LN, None, ALU.add).then_inc(S("root_in"), 1)
            refine_root(rstd[:, :], ve[:, :], rms2[:, :], 3)
            v.wait_ge(S("l1_zero"), 1)
            XS = X[:, :, :].rearrange("p (g t) d -> p g t d", g=B)
            MS = mean[:, :].rearrange("p (g t) -> p g t", g=B)
            RS = rstd[:, :].rearrange("p (g t) -> p g t", g=B)

            def wait(s, *names):
                for name in names:
                    v.wait_ge(S(name), count(name, s))

            def over(ap, shape, at):
                return ap.unsqueeze(at).to_broadcast(shape)

            def flat(t):
                return t.rearrange("p g j -> p (g j)")

            def heads_first(t):
                return t.rearrange("p (g h) j -> p h g j", g=B)

            G3 = [P, GH, SUB]

            def f_xn(s):
                for g in range(B):
                    ins = v.tensor_scalar(xn1[:, g, :], XS[:, g, ds(s, 1), :].rearrange("p a d -> p (a d)"),
                                          MS[:, g, ds(s, 1)], RS[:, g, ds(s, 1)], ALU.subtract, ALU.mult)
                ins.then_inc(S("xn1_ready"), 1)

            def f_control(s):
                wait(s, "ctrl_done")
                for i in range(2):
                    ins = v.tensor_tensor(ctl[:, 2 * i:2 * i + 2, :], bank(i)[:, 0:2 * CT].rearrange("p (g c) -> p g c", g=2),
                                          over(b_ctrl[:, :], [P, 2, CT], 1), ALU.add)
                ins.then_inc(S("ctl_raw"), 1)
                wait(s, "ctl_raw")
                v.tensor_scalar(ctl[:, :, :], ctl[:, :, :], Z_MIN, None, ALU.max).then_inc(S("ctl_ready"), 1)

            def f_alpha(s):
                wait(s, "sg_ready")
                v.tensor_scalar(al[:, :, :], sg[:, :, 0:H1], 0.98, 0.01, ALU.mult, ALU.add).then_inc(S("al_ready"), 1)

            def f_conv(s, k):
                for i in range(2):
                    wait(s, f"qkv{i}_ready" if k == 2 else f"conv{i}_{k + 1}")
                    v.scalar_tensor_tensor(cy[:, i, :, :], qkv_in[:, i, :, k:k + P], conv_w[:, i, k:k + 1],
                                           cy[:, i, :, :], ALU.mult, ALU.add).then_inc(S(f"conv{i}_{k}"), 1)

            def f_clamp(s):
                for i in range(3):
                    wait(s, f"conv{i}_0")
                    v.tensor_scalar(ce[:, i, :, :], cy[:, i, :, :], Z_MIN, None, ALU.max).then_inc(S(f"conv{i}_done"), 1)

            def f_tokens(s, those, done):
                for i in those:
                    wait(s, f"tok{i}_turned")
                    ins = v.tensor_copy(tok[:, i, :, :].rearrange("p g d -> p (g d)"), bank(i + i // 2))
                ins.then_inc(S(done), 1)

            def b_residual(s, p):
                wait(s, "ffn_out")
                v.tensor_tensor(acc[:, p, :, :].unsqueeze(2), XS[:, :, ds(s, 1), :], bank(0).rearrange("p (g a d) -> p g a d", g=B, a=1),
                                ALU.add).then_inc(S("acc_ready"), 1)

            def b_bias(s, p):
                wait(s, "acc_ready")
                v.tensor_tensor(acc[:, p, :, :], acc[:, p, :, :], over(b2row[:, :], [P, B, D], 1), ALU.add).then_inc(S("acc2_ready"), 1)

            def refine(y, x, t, names, s, last):
                wait(s, names[0])
                v.tensor_tensor(t, y, y, ALU.mult).then_inc(S(names[1]), 1)
                wait(s, names[1])
                v.scalar_tensor_tensor(t, t, -0.5, x, ALU.mult, ALU.mult).then_inc(S(names[2]), 1)
                wait(s, names[2])
                v.scalar_tensor_tensor(y, t, 1.5, y, ALU.add, ALU.mult).then_inc(S(last), 1)

            def f_sums(s):
                wait(s, "tok_ready")
                for i in range(2):
                    ins = v.tensor_tensor(sq[:, i, :, :], tok[:, i, :, :], tok[:, i, :, :], ALU.mult)
                ins.then_inc(S("sq_ready"), 1)
                wait(s, "sq_ready")
                v.tensor_reduce(ss[:, :, :], sq[:, :, :, :].rearrange("p i g (h e) -> p i (g h) e", e=E1), AX.X, ALU.add).then_inc(S("ss_raw"), 1)
                wait(s, "ss_raw")
                v.tensor_scalar(ss[:, :, :], ss[:, :, :], 1e-12, None, ALU.max).then_inc(S("ss_ready"), 1)

            def f_norm(s):
                refine(rn[:, :, :], ss[:, :, :], rt[:, :, :], ("rn_e", "rn_a", "rn_b"), s, "rn_ready")
                wait(s, "rn_ready")
                for i in range(2):
                    ins = v.tensor_tensor(qk_n[:, i, :, :].rearrange("p g (h e) -> p (g h) e", e=E1),
                                          tok[:, i, :, :].rearrange("p g (h e) -> p (g h) e", e=E1), over(rn[:, i, :], G3, 2), ALU.mult)
                ins.then_inc(S("kn_ready"), 1)

            def f_gam_t(s):
                wait(s, "gam_m_ready")
                v.transpose(flat(gam_t[:, :, :]), flat(gam_m[:, :, :])).then_inc(S("gam_t_ready"), 1)

            def f_kk(s, p):
                wait(s, "kk_done", "gam_b_ready")
                kkp = ps_all[:, 0:4, 0:256].rearrange("p h (g a j) -> p h g a j", g=B, a=2)
                v.tensor_tensor(heads_first(Lc[:, p, :, :]), kkp[:, :, :, 0, :], heads_first(gam_b[:, :, :]), ALU.mult).then_inc(S("Lc_ready"), 1)
                wait(s, "gam_t_ready")
                v.tensor_tensor(heads_first(Pc[:, p, :, :]), kkp[:, :, :, 1, :], heads_first(gam_t[:, :, :]), ALU.mult).then_inc(S("Pc_ready"), 1)

            def spread(src, name, half=slice(0, GH)):
                for q in range(NB):
                    r = slice(q * SUB, (q + 1) * SUB)
                    ins = v.tensor_copy(Tx[r, half, q * SUB:(q + 1) * SUB], src[r, half, :])
                ins.then_inc(S(name), 1)

            def b_pairs(s, p):
                wait(s, "Lc_ready")
                v.tensor_tensor(Tc[:, :, :], Lc[:, p, :, :], over(merge[:, 0, :], G3, 1), ALU.mult).then_inc(S("T2_raw"), 1)
                wait(s, "T2_raw")
                v.tensor_tensor(Tc[:, :, :], over(eye, G3, 1), Tc[:, :, :], ALU.subtract).then_inc(S("T0_ready"), 1)
                wait(s, "T0_ready")
                v.transpose(flat(Zc[:, 0, :, :]), flat(Tc[:, :, :])).then_inc(S("Z0_ready"), 1)

            def b_join(s, k):
                new = Zc[:, (k + 1) % 2, :, :]
                for x, c in enumerate("ab"):
                    half = slice(x * GH // 2, (x + 1) * GH // 2)
                    wait(s, f"ZY{k}{c}_done")
                    v.tensor_tensor(new[:, half, :], Zc[:, k % 2, half, :], bank(6 + x)[:, 0:256].rearrange("p (g j) -> p g j", g=GH // 2),
                                    ALU.subtract).then_inc(S(f"Z{k + 1}{c}_ready"), 1)
                    wait(s, f"Z{k + 1}{c}_ready")
                    if k < 3:
                        v.transpose(flat(Tc[:, half, :]), flat(new[:, half, :])).then_inc(S(f"T{k + 1}{c}_ready"), 1)
                        wait(s, f"T{k + 1}{c}_ready")
                        spread(Tc, f"Tx{k + 1}{c}_ready", half)
                    else:
                        spread(new, f"Tx4{c}_ready", half)

            def b_pw(s, p):
                wait(s, "Qd_ready")
                for x, c in enumerate("ab"):
                    half = slice(x * GH // 2, (x + 1) * GH // 2)
                    wait(s, f"PW{c}_done")
                    pw = bank(4 + x).rearrange("p (g j) -> p g j", g=GH // 2)
                    v.tensor_tensor(Mo[:, half, :], Qd[:, p, half, :], pw[:, :, SUB:], ALU.subtract).then_inc(S(f"Mo{c}_ready"), 1)
                v.tensor_copy(Ov[:, :, :], bank(4, 2).rearrange("p (g j) -> p g j", g=GH)[:, :, 0:SUB]).then_inc(S("Ov_ready"), 1)

            def b_maps(s, p):
                wait(s, "AB_done", "decI_ready")
                abp = ps_all[:, 4:8, 0:256].rearrange("p q (g a j) -> p q g a j", g=B, a=2)
                v.tensor_tensor(At, decI[:, :, :, :], abp[:, :, :, 1, :], ALU.subtract).then_inc(S("At_ready"), 1)
                wait(s, "At_ready")
                v.transpose(Ac[:, :, :, :].rearrange("p q g e -> p (q g e)"), At[:, :, :, :].rearrange("p q g e -> p (q g e)")).then_inc(S("Ac_ready"), 1)
                v.tensor_copy(Bc[:, :, :, :], abp[:, :, :, 0, :]).then_inc(S("Bc_ready"), 1)
                v.tensor_copy(St[:, 0, :, :], St[:, NB, :, :]).then_inc(S("St0_ready"), 1)

            def b_state(s):
                wait(s, "St0_ready", "Bc_ready")
                for q in range(NB):
                    wait(s, f"AS{q}_done")
                    v.tensor_tensor(St[:, q + 1, :, :], bank(4)[:, 0:P].rearrange("p (g j) -> p g j", g=B),
                                    Bc[:, q, :, :], ALU.add).then_inc(S(f"St{q + 1}_ready"), 1)

            def b_read(s):
                wait(s, "MS_done", "Ov_ready")
                v.tensor_tensor(heads_first(rd[:, :, :]), ps_all[:, 4:8, 0:P].rearrange("p h (g j) -> p h g j", g=B),
                                heads_first(Ov[:, :, :]), ALU.add).then_inc(S("rd_ready"), 1)

            def b_read_sums(s):
                wait(s, "rd_ready")
                v.tensor_tensor(rsq, rd[:, :, :], rd[:, :, :], ALU.mult).then_inc(S("rsq_ready"), 1)
                wait(s, "rsq_ready")
                v.tensor_reduce(rss[:, :], rsq, AX.X, ALU.add).then_inc(S("rss_raw"), 1)
                wait(s, "rss_raw")
                v.tensor_scalar(rss[:, :], rss[:, :], 1.0 / E1, 1e-6, ALU.mult, ALU.add).then_inc(S("rss_ready"), 1)

            def b_read_norm(s):
                refine(rrs[:, :], rss[:, :], rrt[:, :], ("rrs_e", "rrs_a", "rrs_b"), s, "rrs_ready")
                wait(s, "rrs_ready")
                v.tensor_tensor(rdn[:, :, :].rearrange("p g (h e) -> p (g h) e", e=E1), rd[:, :, :], over(rrs[:, :], G3, 2),
                                ALU.mult).then_inc(S("rdn_ready"), 1)

            def b_out(s, p):
                wait(s, "out_done")
                v.tensor_tensor(ao[:, :, :], bank(2).rearrange("p (g d) -> p g d", g=B), over(b_out_row, [P, B, D], 1),
                                ALU.add).then_inc(S("out_read"), 1)
                v.wait_ge(S("out_read"), s + 2)
                wait(s, "ogr_ready")
                v.tensor_tensor(ao[:, :, :], ao[:, :, :], ogr[:, p, :, :], ALU.mult).then_inc(S("ao2"), 1)
                v.wait_ge(S("stored"), s * 16 + 16)
                wait(s, "ao2", "acc2_ready")
                v.tensor_tensor(res[:, :, :], acc[:, p, :, :], ao[:, :, :], ALU.add).then_inc(S("res_ready"), 1)

            b_out_row = b_out_sb[:, :]

            def round_of(s, p, ahead, after=True):
                b_join(s, 1)
                if ahead:
                    f_conv(s + 1, 2)
                    f_control(s + 1)
                    f_conv(s + 1, 1)
                    f_conv(s + 1, 0)
                    f_clamp(s + 1)
                b_join(s, 2)
                b_residual(s, p)
                b_join(s, 3)
                b_bias(s, p)
                if ahead:
                    f_alpha(s + 1)
                    f_tokens(s + 1, (0, 1), "tok_ready")
                    f_sums(s + 1)
                b_pw(s, p)
                if ahead:
                    f_tokens(s + 1, (2,), "v_tok_ready")
                    f_norm(s + 1)
                b_maps(s, p)
                if after:
                    f_xn(s + 2)
                if ahead:
                    f_gam_t(s + 1)
                b_state(s)
                if ahead:
                    f_kk(s + 1, 1 - p)
                    b_pairs(s + 1, 1 - p)
                b_read(s)
                if ahead:
                    spread(Tc, "Tx0_ready")
                b_read_sums(s)
                b_read_norm(s)
                if ahead:
                    b_join(s + 1, 0)
                b_out(s, p)

            f_xn(0)
            f_conv(0, 2)
            f_control(0)
            f_conv(0, 1)
            f_conv(0, 0)
            f_clamp(0)
            f_alpha(0)
            f_tokens(0, (0, 1), "tok_ready")
            f_sums(0)
            f_tokens(0, (2,), "v_tok_ready")
            f_norm(0)
            f_gam_t(0)
            f_xn(1)
            v.wait_ge(S("l1_zero"), 2)
            f_kk(0, 0)
            b_pairs(0, 0)
            spread(Tc, "Tx0_ready")
            b_join(0, 0)
            with v.Fori(0, NT // 2 - 1) as i:
                round_of(i * 2, 0, True)
                round_of(i * 2 + 1, 1, True)
            round_of(NT - 2, 0, True, False)
            round_of(NT - 1, 1, False, False)


_INS = ['L0_attn_tokens', 'L0_attn_wq', 'L0_attn_wk', 'L0_attn_wv', 'L0_attn_wo', 'L0_attn_w_gates', 'L0_attn_rms_w',
        'L0_ffn_W_r', 'L0_ffn_W_k', 'L0_ffn_W_v', 'L0_ffn_mu_r', 'L0_ffn_mu_k', 'L1_attn_W_in', 'L1_attn_W_ctrl',
        'L1_attn_b_ctrl', 'L1_attn_w_q', 'L1_attn_w_k', 'L1_attn_w_v', 'L1_attn_W_out', 'L1_attn_b_out',
        'L1_attn_ramp_logit', 'L1_ffn_w1', 'L1_ffn_b1', 'L1_ffn_w2', 'L1_ffn_b2']
_OUTS = [((4, 1024, 128), 'float32')]


def _masks():
    import numpy as _np

    n, sub = 128, 32
    r, c = _np.arange(n)[:, None], _np.arange(n)[None, :]
    j = _np.arange(sub)[None, :]
    i = r % sub
    parts = [(r // sub == c // sub) & (r <= c), (r // sub == c // sub) & (r > c),
             r // sub == _np.arange(n // sub)[None, :], i == j, j < i, j <= i]
    for m in (1, 2, 4, 8, 16):
        parts.append((i // (2 * m) == j // (2 * m)) & (i % (2 * m) >= m) & (j % (2 * m) < m))
    return _np.concatenate(parts, axis=1).astype(_np.float32)


def kernel(**inputs):
    import numpy as _np
    import concourse.bacc as _bacc
    from concourse import mybir as _mybir
    from concourse.bass_utils import run_bass_kernel_spmd as _run

    nc = _bacc.Bacc("TRN2", target_bir_lowering=False, num_devices=1)
    arrays, aps = {}, {}
    for name in _INS:
        a = _np.ascontiguousarray(inputs[name])
        arrays[f"in_{name}_dram"] = a
        aps[name] = nc.dram_tensor(f"in_{name}_dram", a.shape, _mybir.dt.from_np(a.dtype), kind="ExternalInput").ap()
    arrays["masks_dram"] = _masks()
    aps["masks"] = nc.dram_tensor("masks_dram", arrays["masks_dram"].shape, _mybir.dt.float32, kind="ExternalInput").ap()
    outs = []
    for i, (shape, dtype) in enumerate(_OUTS):
        dt = _mybir.dt.from_np(_np.dtype(dtype))
        outs.append(nc.dram_tensor(f"out_{i}_dram", shape, dt, kind="ExternalOutput").ap())
    build(nc, aps, outs[0])
    r = _run(nc, [arrays], core_ids=[0])
    return r.results[0]["out_0_dram"]
```
